# Optimizing a Trainium2 kernel written in Bass

```python
import numpy as np
import jax
import jax.numpy as jnp

def _softmax(x, axis=-1):
    return jax.nn.softmax(x, axis=axis)

def _gelu(x):
    return jax.nn.gelu(x, approximate=True)

def _silu(x):
    return jax.nn.silu(x)

def _sigmoid(x):
    return jax.nn.sigmoid(x)

def _layernorm(x, axis=-1, eps=1e-05):
    m = jnp.mean(x, axis=axis, keepdims=True)
    v = jnp.var(x, axis=axis, keepdims=True)
    return (x - m) / jnp.sqrt(v + eps)

def _scatter_add(tgt, idx, src, axis=0):
    return tgt.at[idx].add(src)

def _segment_sum(src, seg, n):
    return jax.ops.segment_sum(src, seg, n)
kernel_name = 'mk_decoder_postln_d2_seqx_r4_5c2f0c'

def setup_inputs(seed: int=0):
    np.random.seed(seed)
    _w = jnp.asarray

    def _rec_inputs():
        import jax
        import jax.numpy as jnp
        _rk = jax.random.key(seed)
        x = 7.22e-05 + 1 * jax.random.normal(jax.random.fold_in(_rk, 1), (16, 256, 256), jnp.float32)
        _lenS = 256 - jax.random.randint(jax.random.fold_in(_rk, 7), (16,), 0, max(1, 256 // 4) + 1, jnp.int32)
        _lenS2 = 256 - jax.random.randint(jax.random.fold_in(_rk, 8), (16,), 0, max(1, 256 // 4) + 1, jnp.int32)
        _ctx_1024P = jax.random.normal(jax.random.fold_in(_rk, 11), (16, 16, 256), jnp.float32)
        _ctx_1024c = jax.random.dirichlet(jax.random.fold_in(_rk, 511), 0.3 * jnp.ones((16,), jnp.float32), (16, 256))
        _ctx_1024t = jnp.einsum('bsk,bkd->bsd', _ctx_1024c, _ctx_1024P)
        _ctx_1024t = _ctx_1024t * jax.lax.rsqrt(jnp.mean(jnp.square(_ctx_1024t)) + 1e-12) * 0.953939
        ctx_1024 = 4.13588e-05 + 0.999923 * (_ctx_1024t + 0.3 * jax.random.normal(jax.random.fold_in(_rk, 611), (16, 256, 256), jnp.float32))
        return (x, ctx_1024)
    x, ctx_1024 = _rec_inputs()

    def _L0_attn_setup():
        import jax, jax.numpy as jnp
        import numpy as np
        DIM = 256
        NUM_HEADS = 16
        HEAD_DIM = DIM // NUM_HEADS
        SCALE = 1.0 / float(np.sqrt(HEAD_DIM))
        key = jax.random.key(seed)
        kx, kw1, kb1, kw2, kb2 = jax.random.split(key, 5)
        b, l = (2, 512)
        s = 1.0 / np.sqrt(DIM)
        return {'x': jax.random.normal(kx, (b, l, DIM), dtype=jnp.float32), 'w_qkv': jax.random.uniform(kw1, (DIM, 3 * DIM), jnp.float32, -s, s), 'b_qkv': jax.random.uniform(kb1, (3 * DIM,), jnp.float32, -s, s), 'w_proj': jax.random.uniform(kw2, (DIM, DIM), jnp.float32, -s, s), 'b_proj': jax.random.uniform(kb2, (DIM,), jnp.float32, -s, s)}
    _L0_attn_all = _L0_attn_setup()
    _L0_attn_in = {k: v for k, v in _L0_attn_all.items() if k in ('w_qkv', 'b_qkv', 'w_proj', 'b_proj')}
    del _L0_attn_all

    def _L0_xattn_setup():
        import jax, jax.numpy as jnp
        import numpy as np
        D_K = 256
        HEADS = 16
        HK = 64
        HV = 64
        key = jax.random.key(seed)
        ks = jax.random.split(key, 12)
        B, S = (4, 512)
        sc_in = 1.0 / np.sqrt(D_K)
        sc_u = 1.0 / np.sqrt(HV * HEADS)
        return {'q': jax.random.normal(ks[0], (B, S, D_K), jnp.float32), 'k': jax.random.normal(ks[1], (B, S, D_K), jnp.float32), 'v': jax.random.normal(ks[2], (B, S, D_K), jnp.float32), 'Wq': jax.random.normal(ks[3], (D_K, HK * HEADS), jnp.float32) * sc_in, 'bq': jax.random.normal(ks[4], (HK * HEADS,), jnp.float32) * sc_in, 'Wk': jax.random.normal(ks[5], (D_K, HK * HEADS), jnp.float32) * sc_in, 'bk': jax.random.normal(ks[6], (HK * HEADS,), jnp.float32) * sc_in, 'Wv': jax.random.normal(ks[7], (D_K, HV * HEADS), jnp.float32) * sc_in, 'bv': jax.random.normal(ks[8], (HV * HEADS,), jnp.float32) * sc_in, 'Wu': jax.random.normal(ks[9], (HV * HEADS, D_K), jnp.float32) * sc_u, 'bu': jax.random.normal(ks[10], (D_K,), jnp.float32) * sc_u}
    _L0_xattn_all = _L0_xattn_setup()
    _L0_xattn_in = {k: v for k, v in _L0_xattn_all.items() if k in ('Wq', 'bq', 'Wk', 'bk', 'Wv', 'bv', 'Wu', 'bu')}
    del _L0_xattn_all

    def _L0_ffn_setup():
        import jax, jax.numpy as jnp
        import numpy as np
        HIDDEN = 256
        NUM_EXPERTS = 8
        TOP_K = 2
        FFN = 1024
        BATCH, SEQ = (4, 512)
        key = jax.random.key(seed)
        k_x, k_r, k_w1, k_w2 = jax.random.split(key, 4)
        x = jax.random.normal(k_x, (BATCH, SEQ, HIDDEN), dtype=jnp.float32)
        router_w = jax.random.normal(k_r, (NUM_EXPERTS, HIDDEN), dtype=jnp.float32) * (1.0 / np.sqrt(HIDDEN))
        lim = float(np.sqrt(6.0 / (FFN + HIDDEN)))
        expert_w1 = jax.random.uniform(k_w1, (NUM_EXPERTS, FFN, HIDDEN), dtype=jnp.float32, minval=-lim, maxval=lim)
        expert_w2 = jax.random.uniform(k_w2, (NUM_EXPERTS, HIDDEN, FFN), dtype=jnp.float32, minval=-lim, maxval=lim)
        return {'x': x, 'router_w': router_w, 'expert_w1': expert_w1, 'expert_w2': expert_w2}
    _L0_ffn_all = _L0_ffn_setup()
    _L0_ffn_in = {k: v for k, v in _L0_ffn_all.items() if k in ('router_w', 'expert_w1', 'expert_w2')}
    del _L0_ffn_all

    def _L1_attn_setup():
        import jax, jax.numpy as jnp
        import numpy as np
        N_EMBD = 256
        N_HEAD = 16
        N_LAYER = 24
        LAYER_ID = 12
        B, T = (4, 1024)
        Q = 64
        EPS = 1e-05 * 64

        def _static_params():
            C, H = (N_EMBD, N_HEAD)
            r01 = LAYER_ID / (N_LAYER - 1)
            r1a0 = 1.0 - LAYER_ID / N_LAYER
            ddd = np.arange(C, dtype=np.float64) / C
            maa_k = (1.0 - ddd ** r1a0).astype(np.float32).reshape(1, 1, C)
            maa_v = (1.0 - (ddd ** r1a0 + 0.3 * r01)).astype(np.float32).reshape(1, 1, C)
            maa_r = (1.0 - ddd ** (0.5 * r1a0)).astype(np.float32).reshape(1, 1, C)
            maa_g = maa_r.copy()
            h = np.arange(H, dtype=np.float64)
            decay = (-6.0 + 5.0 * (h / (H - 1)) ** (0.7 + 1.3 * r01)).astype(np.float32).reshape(H, 1)
            faaaa = (r01 * (1.0 - h / (H - 1))).astype(np.float32).reshape(H, 1)
            return (maa_k, maa_v, maa_r, maa_g, decay, faaaa)

        def _rwkv_forward(x, time_maa_k, time_maa_v, time_maa_r, time_maa_g, time_decay, time_faaaa, Wr, Wk, Wv, Wg, Wo, ln_w, ln_b):
            Bv, Tv, C = x.shape
            H = N_HEAD
            N = C // H
            nC = Tv // Q
            xx = jnp.pad(x, ((0, 0), (1, 0), (0, 0)))[:, :Tv] - x
            xk = x + xx * time_maa_k
            xv = x + xx * time_maa_v
            xr = x + xx * time_maa_r
            xg = x + xx * time_maa_g
            r = (xr @ Wr.T).reshape(Bv, Tv, H, N).transpose(0, 2, 1, 3)
            k = (xk @ Wk.T).reshape(Bv, Tv, H, N).transpose(0, 2, 3, 1)
            v = (xv @ Wv.T).reshape(Bv, Tv, H, N).transpose(0, 2, 1, 3)
            g = jax.nn.gelu(xg @ Wg.T, approximate=False)
            w = jnp.exp(-jnp.exp(time_decay))[:, 0]
            u = time_faaaa[:, 0]
            q = jnp.arange(Q)
            ws = (w ** Q).reshape(1, H, 1, 1)
            wk = (w[:, None] ** (Q - 1 - q)).reshape(1, H, 1, Q)
            wb = (w[:, None] ** q).reshape(1, H, Q, 1)
            i_idx = q[:, None]
            j_idx = q[None, :]
            e = jnp.maximum(i_idx - j_idx - 1, 0)
            Wmat = jnp.where(i_idx > j_idx, w[:, None, None] ** e, 0.0)
            Wmat = Wmat + jnp.eye(Q, dtype=x.dtype) * u[:, None, None]
            Wmat = Wmat.reshape(1, H, Q, Q)
            rr = r.reshape(Bv, H, nC, Q, N).transpose(2, 0, 1, 3, 4)
            kk = k.reshape(Bv, H, N, nC, Q).transpose(3, 0, 1, 2, 4)
            vv = v.reshape(Bv, H, nC, Q, N).transpose(2, 0, 1, 3, 4)

            def step(state, inp):
                rc, kc, vc = inp
                att = rc @ kc
                yc = att * Wmat @ vc + rc @ state * wb
                new_state = ws * state + kc * wk @ vc
                return (new_state, yc)
            state0 = jnp.zeros((Bv, H, N, N), dtype=x.dtype)
            _, ys = jax.lax.scan(step, state0, (rr, kk, vv))
            y = ys.transpose(1, 2, 0, 3, 4).reshape(Bv, H, Tv, N)
            y = y.transpose(0, 2, 1, 3)
            mean = y.mean(axis=-1, keepdims=True)
            var = y.var(axis=-1, keepdims=True)
            yn = (y - mean) / jnp.sqrt(var + EPS)
            yn = yn * ln_w.reshape(1, 1, H, N) + ln_b.reshape(1, 1, H, N)
            yn = yn.reshape(Bv, Tv, C)
            out = yn * g @ Wo.T
            return out
        key = jax.random.key(seed)
        ks = jax.random.split(key, 8)
        C = N_EMBD
        maa_k, maa_v, maa_r, maa_g, decay, faaaa = _static_params()
        std = 0.02
        return {'x': jax.random.normal(ks[0], (B, T, C), dtype=jnp.float32), 'time_maa_k': jnp.asarray(maa_k), 'time_maa_v': jnp.asarray(maa_v), 'time_maa_r': jnp.asarray(maa_r), 'time_maa_g': jnp.asarray(maa_g), 'time_decay': jnp.asarray(decay), 'time_faaaa': jnp.asarray(faaaa), 'Wr': jax.random.normal(ks[1], (C, C), dtype=jnp.float32) * std, 'Wk': jax.random.normal(ks[2], (C, C), dtype=jnp.float32) * std, 'Wv': jax.random.normal(ks[3], (C, C), dtype=jnp.float32) * std, 'Wg': jax.random.normal(ks[4], (C, C), dtype=jnp.float32) * std, 'Wo': jax.random.normal(ks[5], (C, C), dtype=jnp.float32) * std, 'ln_w': jnp.ones((C,), dtype=jnp.float32), 'ln_b': jnp.zeros((C,), dtype=jnp.float32)}
    _L1_attn_all = _L1_attn_setup()
    _L1_attn_in = {k: v for k, v in _L1_attn_all.items() if k in ('time_maa_k', 'time_maa_v', 'time_maa_r', 'time_maa_g', 'time_decay', 'time_faaaa', 'Wr', 'Wk', 'Wv', 'Wg', 'Wo', 'ln_w', 'ln_b')}
    del _L1_attn_all

    def _L1_xattn_setup():
        import jax, jax.numpy as jnp
        import numpy as np
        ATTN_WINDOW = 128
        HIDDEN = 256
        NUM_HEADS = 16

        def _sliding_window_attention(q, k, v, w):
            B, nh, S, D = q.shape
            nc = S // w
            k_pad = jnp.pad(k, ((0, 0), (0, 0), (w, w), (0, 0)))
            v_pad = jnp.pad(v, ((0, 0), (0, 0), (w, w), (0, 0)))
            idx = (jnp.arange(nc) * w)[:, None] + jnp.arange(3 * w)[None, :]
            k_c = k_pad[:, :, idx, :]
            v_c = v_pad[:, :, idx, :]
            q_c = q.reshape(B, nh, nc, w, D)
            scores = jnp.einsum('bhcid,bhcjd->bhcij', q_c, k_c)
            i = jnp.arange(w)[:, None]
            j = jnp.arange(3 * w)[None, :]
            band = jnp.abs(j - w - i) <= w
            key_pos = (jnp.arange(nc) * w)[:, None, None] + j[None, :, :] - w
            valid = band[None, :, :] & (key_pos >= 0) & (key_pos < S)
            big_neg = jnp.finfo(scores.dtype).min
            scores = jnp.where(valid[None, None], scores, big_neg)
            probs = jax.nn.softmax(scores, axis=-1)
            out = jnp.einsum('bhcij,bhcjd->bhcid', probs, v_c)
            return out.reshape(B, nh, S, D)
        key = jax.random.key(seed)
        k1, k2, k3 = jax.random.split(key, 3)
        B, S = (2, 2048)
        query = jax.random.normal(k1, (B, S, HIDDEN), dtype=jnp.float32)
        key_t = jax.random.normal(k2, (B, S, HIDDEN), dtype=jnp.float32)
        value = jax.random.normal(k3, (B, S, HIDDEN), dtype=jnp.float32)
        return {'query': query, 'key': key_t, 'value': value}
    _L1_xattn_all = _L1_xattn_setup()
    _L1_xattn_in = {k: v for k, v in _L1_xattn_all.items() if k in ()}
    del _L1_xattn_all

    def _L1_ffn_setup():
        import jax, jax.numpy as jnp
        import numpy as np
        THRESHOLD = 0.1
        key = jax.random.key(seed)
        k1, k2, k3 = jax.random.split(key, 3)
        B, S, D, E = (4, 1024, 256, 8)
        inputs = jax.random.normal(k1, (B, S, D), dtype=jnp.float32)
        gate_w = jax.random.normal(k2, (D, E), dtype=jnp.float32) * 0.02
        gate_b = jnp.zeros((E,), dtype=jnp.float32)
        expert_w = jax.random.normal(k3, (E, D, D), dtype=jnp.float32) * 0.02
        expert_b = jnp.zeros((E, D), dtype=jnp.float32)
        return {'inputs': inputs, 'gate_w': gate_w, 'gate_b': gate_b, 'expert_w': expert_w, 'expert_b': expert_b}
    _L1_ffn_all = _L1_ffn_setup()
    _L1_ffn_in = {k: v for k, v in _L1_ffn_all.items() if k in ('gate_w', 'gate_b', 'expert_w', 'expert_b')}
    del _L1_ffn_all
    return {'x': x, 'ctx_1024': ctx_1024, 'L0_attn_w_qkv': _L0_attn_in['w_qkv'], 'L0_attn_b_qkv': _L0_attn_in['b_qkv'], 'L0_attn_w_proj': _L0_attn_in['w_proj'], 'L0_attn_b_proj': _L0_attn_in['b_proj'], 'L0_xattn_Wq': _L0_xattn_in['Wq'], 'L0_xattn_bq': _L0_xattn_in['bq'], 'L0_xattn_Wk': _L0_xattn_in['Wk'], 'L0_xattn_bk': _L0_xattn_in['bk'], 'L0_xattn_Wv': _L0_xattn_in['Wv'], 'L0_xattn_bv': _L0_xattn_in['bv'], 'L0_xattn_Wu': _L0_xattn_in['Wu'], 'L0_xattn_bu': _L0_xattn_in['bu'], 'L0_ffn_router_w': _L0_ffn_in['router_w'], 'L0_ffn_expert_w1': _L0_ffn_in['expert_w1'], 'L0_ffn_expert_w2': _L0_ffn_in['expert_w2'], 'L1_attn_time_maa_k': _L1_attn_in['time_maa_k'], 'L1_attn_time_maa_v': _L1_attn_in['time_maa_v'], 'L1_attn_time_maa_r': _L1_attn_in['time_maa_r'], 'L1_attn_time_maa_g': _L1_attn_in['time_maa_g'], 'L1_attn_time_decay': _L1_attn_in['time_decay'], 'L1_attn_time_faaaa': _L1_attn_in['time_faaaa'], 'L1_attn_Wr': _L1_attn_in['Wr'], 'L1_attn_Wk': _L1_attn_in['Wk'], 'L1_attn_Wv': _L1_attn_in['Wv'], 'L1_attn_Wg': _L1_attn_in['Wg'], 'L1_attn_Wo': _L1_attn_in['Wo'], 'L1_attn_ln_w': _L1_attn_in['ln_w'], 'L1_attn_ln_b': _L1_attn_in['ln_b'], 'L1_ffn_gate_w': _L1_ffn_in['gate_w'], 'L1_ffn_gate_b': _L1_ffn_in['gate_b'], 'L1_ffn_expert_w': _L1_ffn_in['expert_w'], 'L1_ffn_expert_b': _L1_ffn_in['expert_b']}

def reference(x, ctx_1024, L0_attn_w_qkv, L0_attn_b_qkv, L0_attn_w_proj, L0_attn_b_proj, L0_xattn_Wq, L0_xattn_bq, L0_xattn_Wk, L0_xattn_bk, L0_xattn_Wv, L0_xattn_bv, L0_xattn_Wu, L0_xattn_bu, L0_ffn_router_w, L0_ffn_expert_w1, L0_ffn_expert_w2, L1_attn_time_maa_k, L1_attn_time_maa_v, L1_attn_time_maa_r, L1_attn_time_maa_g, L1_attn_time_decay, L1_attn_time_faaaa, L1_attn_Wr, L1_attn_Wk, L1_attn_Wv, L1_attn_Wg, L1_attn_Wo, L1_attn_ln_w, L1_attn_ln_b, L1_ffn_gate_w, L1_ffn_gate_b, L1_ffn_expert_w, L1_ffn_expert_b):
    import jax
    import jax.numpy as jnp

    def _L0_attn_ref(x, w_qkv, b_qkv, w_proj, b_proj):
        import jax, jax.numpy as jnp
        import numpy as np
        DIM = 256
        NUM_HEADS = 16
        HEAD_DIM = DIM // NUM_HEADS
        SCALE = 1.0 / float(np.sqrt(HEAD_DIM))
        b, l, c = x.shape
        n, d = (NUM_HEADS, HEAD_DIM)
        qkv = x @ w_qkv + b_qkv
        qkv = qkv.reshape(b, l, 3 * n, d)
        q, k, v = (qkv[:, :, :n], qkv[:, :, n:2 * n], qkv[:, :, 2 * n:])
        attn = SCALE * jnp.einsum('binc,bjnc->bnij', q, k)
        attn = jax.nn.softmax(attn.astype(jnp.float32), axis=-1).astype(q.dtype)
        out = jnp.einsum('bnij,bjnc->binc', attn, v)
        out = out.reshape(b, l, c)
        return out @ w_proj + b_proj

    def _L0_xattn_ref(q, k, v, Wq, bq, Wk, bk, Wv, bv, Wu, bu):
        import jax, jax.numpy as jnp
        import numpy as np
        D_K = 256
        HEADS = 16
        HK = 64
        HV = 64
        B, S, _ = q.shape
        qh = (q @ Wq + bq).reshape(B, S, HEADS, HK).transpose(0, 2, 1, 3)
        kh = (k @ Wk + bk).reshape(B, S, HEADS, HK).transpose(0, 2, 1, 3)
        vh = (v @ Wv + bv).reshape(B, S, HEADS, HV).transpose(0, 2, 1, 3)
        scores = jnp.einsum('bhqd,bhkd->bhqk', qh, kh) / jnp.sqrt(jnp.asarray(HK, qh.dtype))
        attn = jax.nn.softmax(scores, axis=-1)
        out = jnp.einsum('bhqk,bhkd->bhqd', attn, vh)
        merged = out.transpose(0, 2, 1, 3).reshape(B, S, HEADS * HV)
        return merged @ Wu + bu

    def _L0_ffn_ref(x, router_w, expert_w1, expert_w2):
        import jax, jax.numpy as jnp
        import numpy as np
        HIDDEN = 256
        NUM_EXPERTS = 8
        TOP_K = 2
        FFN = 1024
        BATCH, SEQ = (4, 512)
        B, S, D = x.shape
        xf = x.reshape(-1, D)
        scores = xf @ router_w.T
        top_v, top_i = jax.lax.top_k(scores, TOP_K)
        routing_w = jax.nn.softmax(top_v, axis=-1)
        out = jnp.zeros_like(xf)
        for e in range(NUM_EXPERTS):
            w_e = jnp.sum(jnp.where(top_i == e, routing_w, 0.0), axis=-1)
            h = jax.nn.gelu(xf @ expert_w1[e].T, approximate=False)
            out = out + h @ expert_w2[e].T * w_e[:, None]
        return out.reshape(B, S, D)

    def _L1_attn_ref(x, time_maa_k, time_maa_v, time_maa_r, time_maa_g, time_decay, time_faaaa, Wr, Wk, Wv, Wg, Wo, ln_w, ln_b):
        import jax, jax.numpy as jnp
        import numpy as np
        N_EMBD = 256
        N_HEAD = 16
        N_LAYER = 24
        LAYER_ID = 12
        B, T = (4, 1024)
        Q = 64
        EPS = 1e-05 * 64

        def _static_params():
            C, H = (N_EMBD, N_HEAD)
            r01 = LAYER_ID / (N_LAYER - 1)
            r1a0 = 1.0 - LAYER_ID / N_LAYER
            ddd = np.arange(C, dtype=np.float64) / C
            maa_k = (1.0 - ddd ** r1a0).astype(np.float32).reshape(1, 1, C)
            maa_v = (1.0 - (ddd ** r1a0 + 0.3 * r01)).astype(np.float32).reshape(1, 1, C)
            maa_r = (1.0 - ddd ** (0.5 * r1a0)).astype(np.float32).reshape(1, 1, C)
            maa_g = maa_r.copy()
            h = np.arange(H, dtype=np.float64)
            decay = (-6.0 + 5.0 * (h / (H - 1)) ** (0.7 + 1.3 * r01)).astype(np.float32).reshape(H, 1)
            faaaa = (r01 * (1.0 - h / (H - 1))).astype(np.float32).reshape(H, 1)
            return (maa_k, maa_v, maa_r, maa_g, decay, faaaa)

        def _rwkv_forward(x, time_maa_k, time_maa_v, time_maa_r, time_maa_g, time_decay, time_faaaa, Wr, Wk, Wv, Wg, Wo, ln_w, ln_b):
            Bv, Tv, C = x.shape
            H = N_HEAD
            N = C // H
            nC = Tv // Q
            xx = jnp.pad(x, ((0, 0), (1, 0), (0, 0)))[:, :Tv] - x
            xk = x + xx * time_maa_k
            xv = x + xx * time_maa_v
            xr = x + xx * time_maa_r
            xg = x + xx * time_maa_g
            r = (xr @ Wr.T).reshape(Bv, Tv, H, N).transpose(0, 2, 1, 3)
            k = (xk @ Wk.T).reshape(Bv, Tv, H, N).transpose(0, 2, 3, 1)
            v = (xv @ Wv.T).reshape(Bv, Tv, H, N).transpose(0, 2, 1, 3)
            g = jax.nn.gelu(xg @ Wg.T, approximate=False)
            w = jnp.exp(-jnp.exp(time_decay))[:, 0]
            u = time_faaaa[:, 0]
            q = jnp.arange(Q)
            ws = (w ** Q).reshape(1, H, 1, 1)
            wk = (w[:, None] ** (Q - 1 - q)).reshape(1, H, 1, Q)
            wb = (w[:, None] ** q).reshape(1, H, Q, 1)
            i_idx = q[:, None]
            j_idx = q[None, :]
            e = jnp.maximum(i_idx - j_idx - 1, 0)
            Wmat = jnp.where(i_idx > j_idx, w[:, None, None] ** e, 0.0)
            Wmat = Wmat + jnp.eye(Q, dtype=x.dtype) * u[:, None, None]
            Wmat = Wmat.reshape(1, H, Q, Q)
            rr = r.reshape(Bv, H, nC, Q, N).transpose(2, 0, 1, 3, 4)
            kk = k.reshape(Bv, H, N, nC, Q).transpose(3, 0, 1, 2, 4)
            vv = v.reshape(Bv, H, nC, Q, N).transpose(2, 0, 1, 3, 4)

            def step(state, inp):
                rc, kc, vc = inp
                att = rc @ kc
                yc = att * Wmat @ vc + rc @ state * wb
                new_state = ws * state + kc * wk @ vc
                return (new_state, yc)
            state0 = jnp.zeros((Bv, H, N, N), dtype=x.dtype)
            _, ys = jax.lax.scan(step, state0, (rr, kk, vv))
            y = ys.transpose(1, 2, 0, 3, 4).reshape(Bv, H, Tv, N)
            y = y.transpose(0, 2, 1, 3)
            mean = y.mean(axis=-1, keepdims=True)
            var = y.var(axis=-1, keepdims=True)
            yn = (y - mean) / jnp.sqrt(var + EPS)
            yn = yn * ln_w.reshape(1, 1, H, N) + ln_b.reshape(1, 1, H, N)
            yn = yn.reshape(Bv, Tv, C)
            out = yn * g @ Wo.T
            return out
        return _rwkv_forward(x, time_maa_k, time_maa_v, time_maa_r, time_maa_g, time_decay, time_faaaa, Wr, Wk, Wv, Wg, Wo, ln_w, ln_b)

    def _L1_xattn_ref(query, key, value):
        import jax, jax.numpy as jnp
        import numpy as np
        ATTN_WINDOW = 128
        HIDDEN = 256
        NUM_HEADS = 16

        def _sliding_window_attention(q, k, v, w):
            B, nh, S, D = q.shape
            nc = S // w
            k_pad = jnp.pad(k, ((0, 0), (0, 0), (w, w), (0, 0)))
            v_pad = jnp.pad(v, ((0, 0), (0, 0), (w, w), (0, 0)))
            idx = (jnp.arange(nc) * w)[:, None] + jnp.arange(3 * w)[None, :]
            k_c = k_pad[:, :, idx, :]
            v_c = v_pad[:, :, idx, :]
            q_c = q.reshape(B, nh, nc, w, D)
            scores = jnp.einsum('bhcid,bhcjd->bhcij', q_c, k_c)
            i = jnp.arange(w)[:, None]
            j = jnp.arange(3 * w)[None, :]
            band = jnp.abs(j - w - i) <= w
            key_pos = (jnp.arange(nc) * w)[:, None, None] + j[None, :, :] - w
            valid = band[None, :, :] & (key_pos >= 0) & (key_pos < S)
            big_neg = jnp.finfo(scores.dtype).min
            scores = jnp.where(valid[None, None], scores, big_neg)
            probs = jax.nn.softmax(scores, axis=-1)
            out = jnp.einsum('bhcij,bhcjd->bhcid', probs, v_c)
            return out.reshape(B, nh, S, D)
        B, S, _ = query.shape
        D = HIDDEN // NUM_HEADS
        q = query.reshape(B, S, NUM_HEADS, D).transpose(0, 2, 1, 3)
        k = key.reshape(B, S, NUM_HEADS, D).transpose(0, 2, 1, 3)
        v = value.reshape(B, S, NUM_HEADS, D).transpose(0, 2, 1, 3)
        out = _sliding_window_attention(q, k, v, ATTN_WINDOW)
        return out.transpose(0, 2, 1, 3).reshape(B, S, HIDDEN)

    def _L1_ffn_ref(inputs, gate_w, gate_b, expert_w, expert_b):
        import jax, jax.numpy as jnp
        import numpy as np
        THRESHOLD = 0.1
        d = inputs.shape[-1]
        x = inputs.reshape(-1, d)
        gate_logits = jax.nn.softmax(x @ gate_w + gate_b, axis=-1)
        selected = (gate_logits >= THRESHOLD).astype(x.dtype)
        weights = gate_logits * selected
        wsum = jnp.sum(weights, axis=-1, keepdims=True)
        weights = weights / jnp.where(wsum == 0, jnp.ones_like(wsum), wsum)
        E = expert_w.shape[0]
        out = jnp.zeros((x.shape[0], expert_w.shape[-1]), dtype=x.dtype)
        for e in range(E):
            out = out + weights[:, e:e + 1] * (x @ expert_w[e] + expert_b[e])
        return out.reshape(*inputs.shape[:-1], out.shape[-1])
    x = _layernorm(x + _L0_attn_ref(x, L0_attn_w_qkv, L0_attn_b_qkv, L0_attn_w_proj, L0_attn_b_proj), axis=-1)
    x = _layernorm(x + _L0_xattn_ref(x, ctx_1024, ctx_1024, L0_xattn_Wq, L0_xattn_bq, L0_xattn_Wk, L0_xattn_bk, L0_xattn_Wv, L0_xattn_bv, L0_xattn_Wu, L0_xattn_bu), axis=-1)
    x = _layernorm(x + _L0_ffn_ref(x, L0_ffn_router_w, L0_ffn_expert_w1, L0_ffn_expert_w2), axis=-1)
    x = _layernorm(x + _L1_attn_ref(x, L1_attn_time_maa_k, L1_attn_time_maa_v, L1_attn_time_maa_r, L1_attn_time_maa_g, L1_attn_time_decay, L1_attn_time_faaaa, L1_attn_Wr, L1_attn_Wk, L1_attn_Wv, L1_attn_Wg, L1_attn_Wo, L1_attn_ln_w, L1_attn_ln_b), axis=-1)
    x = _layernorm(x + _L1_xattn_ref(x, ctx_1024, ctx_1024), axis=-1)
    x = _layernorm(x + _L1_ffn_ref(x, L1_ffn_gate_w, L1_ffn_gate_b, L1_ffn_expert_w, L1_ffn_expert_b), axis=-1)
    return x

_drawn_inputs = setup_inputs


def setup_inputs(seed=0):
    import zlib

    import numpy as np

    out = dict(_drawn_inputs(seed))
    spreads = {'L1_attn_ln_w': (1.0, 0.6),
     'L1_attn_ln_b': (0.0, 0.8),
     'L1_ffn_gate_b': (0.0, 0.1),
     'L1_ffn_expert_b': (0.0, 0.1)}
    factors = {'L0_xattn_bk': 8.0,
     'L1_attn_time_maa_k': 3.194,
     'L1_attn_time_maa_v': 3.856,
     'L1_attn_time_maa_r': 2.71,
     'L1_attn_time_maa_g': 3.292,
     'L1_attn_time_faaaa': 8.0}
    for name, (base, spread) in spreads.items():
        noise = np.random.default_rng([zlib.crc32(name.encode()), seed]).standard_normal(out[name].shape)
        drawn = base * np.exp(spread * noise) if base else spread * noise
        out[name] = jnp.asarray(drawn.astype(out[name].dtype))
    for name, factor in factors.items():
        out[name] = (out[name] * factor).astype(out[name].dtype)
    return out
```

```python
import numpy as np
import concourse.bass as bass
from concourse import mybir
from contextlib import ExitStack

F32 = mybir.dt.float32
BF16 = mybir.dt.bfloat16
U32 = mybir.dt.uint32
ALU = mybir.AluOpType
ACT = mybir.ActivationFunctionType
AX = mybir.AxisListType
ds = bass.ds

P = 128
D = 256
KD = D // P
B = 16
S = 256
T = B * S
H = 16
DH = D // H
QUADS = H // 4
BLK = 512
NBLK = T // BLK
TPB = BLK // P
DX = 64
DM = H * DX
NE = 8
FFN = 1024
LN_EPS = 1e-5
GN_EPS = 1e-5 * 64

Q_PARTS = (0, 0, 0, 1, 1, 2)
K_PARTS = (0, 1, 2, 0, 1, 0)
ROWS = len(Q_PARTS) * DH
MAX_ROWS = 2


class Phase:

    def __init__(self, nc, name):
        self.nc, self.name, self.stack, self.sems = nc, name, ExitStack(), []

    def __enter__(self):
        self.stack.__enter__()
        return self

    def __exit__(self, *a):
        done = self.stack.__exit__(*a)
        self.nc.clear_and_free_semaphores(self.sems)
        self.nc.all_engine_barrier()
        return done

    def sb(self, name, shape, dt=F32):
        return self.stack.enter_context(self.nc.sbuf_tensor(f"{self.name}_{name}", shape, dt))

    def ps(self, name, shape, dt=F32):
        return self.stack.enter_context(self.nc.psum_tensor(f"{self.name}_{name}", shape, dt))

    def sem(self, name):
        self.sems.append(self.nc.alloc_semaphore(name=f"{self.name}_{name}"))
        return self.sems[-1]

    def block(self):
        return self.stack.enter_context(self.nc.Block())


def paired(eng, count, body):
    with eng.Fori(0, count // 2 - 1) as i:
        body(i, 0, False)
        body(i, 1, False)
    body(count // 2 - 1, 0, False)
    body(count // 2 - 1, 1, True)


def at(eng, start, size):
    return slice(start, start + size) if isinstance(start, int) else ds(eng.snap(start), size)


def wait_apart(eng, sem, value, met, met_value):
    value = value if isinstance(value, int) else eng.to_reg(value)
    eng.wait_ge(met, met_value)
    eng.wait_ge(sem, value)


def phase_qkv(nc, xT, w_qkv, b_qkv, qk_parts, v_pad):
    with Phase(nc, "qkv") as ph:
        w = ph.sb("w", [P, KD, 3 * D])
        bqk = ph.sb("bqk", [P, 4])
        bv = ph.sb("bv", [P, 2, D])
        x = ph.sb("x", [P, 2, KD, BLK])
        parts = ph.sb("parts", [P, 2, 4, 3, BLK], BF16)
        rest = ph.sb("rest", [P, 2, BLK])
        vp = ph.sb("vp", [P, 2, TPB, H, 32])
        qk_ps = ph.ps("qk_ps", [P, 4, BLK])
        v_ps = ph.ps("v_ps", [P, TPB, D])
        consts = ph.sem("consts")
        x_loaded = [ph.sem(f"x_loaded{s}") for s in range(2)]
        x_free = ph.sem("x_free")
        qk_done = ph.sem("qk_done")
        hi_done = ph.sem("hi_done")
        rest_done = ph.sem("rest_done")
        mid_done = ph.sem("mid_done")
        parts_done = ph.sem("parts_done")
        v_zeroed = ph.sem("v_zeroed")
        v_done = ph.sem("v_done")
        v_out = ph.sem("v_out")
        stored = [ph.sem(f"stored{s}") for s in range(2)]
        block = ph.block()

        @block.sync
        def _(sp):
            for s in range(2):
                sp.sem_inc(stored[s], 16)
            sp.dma_start(w[:], w_qkv.rearrange("(k p) n -> p k n", p=P)).then_inc(consts, 16)
            sp.dma_start(bqk[:], b_qkv[0:2 * D].rearrange("(m p) -> p m", p=P),
                         allow_slow_non_contiguous=True).then_inc(consts, 16)
            for t in range(2):
                sp.dma_start(bv[:, t], b_qkv[2 * D:3 * D].partition_broadcast(P)).then_inc(consts, 16)

            def load(i, s):
                tok = at(sp, i * (2 * BLK) + s * BLK, BLK)
                wait_apart(sp, x_free, i * 2 + (s + 1), consts, 64)
                sp.dma_start(x[:, s], xT[:, tok]
                             .rearrange("(k p) n -> p k n", p=P)).then_inc(x_loaded[s], 16)

            def body(i, s, last):
                if not last:
                    load(i + s, 1 - s)
                tok = at(sp, i * (2 * BLK) + s * BLK, BLK)
                half = at(sp, i * BLK + s * (BLK // 2), BLK // 2)
                for m in range(4):
                    wait_apart(sp, parts_done, i * 8 + (s * 4 + m + 3), consts, 64)
                    sp.dma_start(qk_parts[m // 2, :, (m % 2) * P:(m % 2 + 1) * P, half]
                                 .rearrange("a p n -> p a n"), parts[:, s, m].bitcast(F32)).then_inc(stored[s], 16)
                wait_apart(sp, v_out, i * 4 + (s * 2 + 4), consts, 64)
                sp.dma_start(v_pad[tok, :].rearrange("(t p) c -> p t c", p=P),
                             vp[:, s].rearrange("p t h c -> p t (h c)")).then_inc(stored[s], 16)

            load(0, 0)
            paired(sp, NBLK, body)
            for s in range(2):
                sp.wait_ge(stored[s], NBLK // 2 * 5 * 16 + 16)

        @block.tensor
        def _(pe):
            pe.sem_inc(x_free, 2)
            pe.wait_ge(consts, 64)

            def body(i, s, last):
                pe.wait_ge(x_loaded[s], i * 16 + 16)
                for m in range(4):
                    pe.wait_ge(rest_done, i * 8 + (s * 4 + m + 1))
                    for k in range(KD):
                        mm = nc.tensor.matmul(qk_ps[:, m], w[:, k, m * P:(m + 1) * P], x[:, s, k],
                                              start=(k == 0), stop=(k == KD - 1))
                    mm.then_inc(qk_done, 1)
                for t in range(TPB):
                    if t % 2 == 0:
                        pe.wait_ge(v_out, i * 4 + (s * 2 + t // 2 + 1))
                    for k in range(KD):
                        mm = nc.tensor.matmul(v_ps[:, t], x[:, s, k, t * P:(t + 1) * P],
                                              w[:, k, 2 * D:3 * D], start=(k == 0), stop=(k == KD - 1))
                    if t % 2:
                        mm.then_inc(v_done, 1)
                pe.drain().then_inc(x_free, 1)
            paired(pe, NBLK, body)

        @block.scalar
        def _(act):
            act.wait_ge(consts, 64)

            def body(i, s, last):
                act.wait_ge(stored[s], i * (5 * 16) + 16)
                for m in range(4):
                    act.wait_ge(qk_done, i * 8 + (s * 4 + m + 1))
                    nc.scalar.activation(parts[:, s, m, 0], qk_ps[:, m], ACT.Identity,
                                         bias=bqk[:, m:m + 1]).then_inc(hi_done, 1)
            paired(act, NBLK, body)

        @block.vector
        def _(dve):
            dve.sem_inc(rest_done, 4)
            dve.sem_inc(v_out, 2)
            dve.wait_ge(v_zeroed, 1)

            def body(i, s, last):
                for m in range(4):
                    dve.wait_ge(hi_done, i * 8 + (s * 4 + m + 1))
                    dve.wait_ge(parts_done, i * 8 + (s * 4 + m + 1))
                    nc.vector.scalar_tensor_tensor(rest[:, m % 2], qk_ps[:, m], bqk[:, m:m + 1],
                                                   parts[:, s, m, 0], ALU.add, ALU.subtract)\
                        .then_inc(rest_done, 1)
                dve.wait_ge(stored[s], i * (5 * 16) + 16)
                for t in (0, 2):
                    dve.wait_ge(v_done, i * 4 + (s * 2 + t // 2 + 1))
                    nc.vector.tensor_tensor(vp[:, s, t:t + 2, :, 0:DH],
                                            v_ps[:, t:t + 2].rearrange("p t (h c) -> p t h c", c=DH),
                                            bv[:].rearrange("p t (h c) -> p t h c", c=DH),
                                            ALU.add).then_inc(v_out, 1)
            paired(dve, NBLK, body)

        @block.gpsimd
        def _(pool):
            nc.gpsimd.memset(vp[:], 0.0).then_inc(v_zeroed, 1)
            pool.sem_inc(parts_done, 2)

            def body(i, s, last):
                for m in range(4):
                    wait_apart(pool, rest_done, i * 8 + (s * 4 + m + 5), v_zeroed, 1)
                    nc.gpsimd.tensor_copy(parts[:, s, m, 1], rest[:, m % 2]).then_inc(mid_done, 1)
                    pool.wait_ge(mid_done, i * 8 + (s * 4 + m + 1))
                    nc.gpsimd.tensor_tensor(parts[:, s, m, 2], rest[:, m % 2], parts[:, s, m, 1],
                                            ALU.subtract).then_inc(parts_done, 1)
            paired(pool, NBLK, body)


def phase_core(nc, name, qk_parts, v_pad, ident_in, out_T, scale, window_masks=None):
    with Phase(nc, name) as ph:
        q6 = ph.sb("q6", [P, 2, H, S], BF16)
        k6 = ph.sb("k6", [P, 2, H, S], BF16)
        v = ph.sb("v", [P, 2, 2, H * 32])
        consts_f32 = ph.sb("consts_f32", [P, 5, P])
        ident = ph.sb("ident", [P, P], BF16)
        ones = ph.sb("ones", [P, 32])
        masks = ph.sb("masks", [P, 4, P], BF16)
        nmax = ph.sb("nmax", [P, 2, 4])
        mparts = ph.sb("mparts", [P, 2, 4, MAX_ROWS], BF16)
        probs = ph.sb("probs", [P, 2, 4, 2, S])
        o_sb = ph.sb("o_sb", [P, 2, S])
        rsum = ph.sb("rsum", [P, 2, S])
        o_norm = ph.sb("o_norm", [P, 2, S])
        s_ps = ph.ps("s_ps", [P, 2, 2, 2, S])
        t_ps = ph.ps("t_ps", [P, 2, 2, S])
        m_ps = ph.ps("m_ps", [P, 4, P])
        o_ps = ph.ps("o_ps", [P, 2, S])
        consts = ph.sem("consts")
        filled = ph.sem("filled")
        ones_set = ph.sem("ones_set")
        loaded = [ph.sem(f"loaded{s}") for s in range(2)]
        batch_done = ph.sem("batch_done")
        s_done = ph.sem("s_done")
        max_done = ph.sem("max_done")
        hi_done = ph.sem("hi_done")
        mparts_done = ph.sem("mparts_done")
        mrow_done = ph.sem("mrow_done")
        mcopied = ph.sem("mcopied")
        t_done = ph.sem("t_done")
        t_free = ph.sem("t_free")
        pv_done = ph.sem("pv_done")
        o_copied = ph.sem("o_copied")
        o_free = ph.sem("o_free")
        o_ready = ph.sem("o_ready")
        stored = [ph.sem(f"stored{s}") for s in range(2)]
        block = ph.block()
        nload = 13
        n_masks = 0 if window_masks is None else 1
        NCONST = 16 * (1 + n_masks)
        PAIRS = H // 2

        @block.sync
        def _(sp):
            for s in range(2):
                sp.sem_inc(stored[s], 16)
            sp.dma_start(consts_f32[:, 4], ident_in).then_inc(consts, 16)
            if n_masks:
                sp.dma_start(consts_f32[:, 0:4], window_masks.rearrange("a p n -> p a n")).then_inc(consts, 16)

            def load(tok, half, s):
                for r in range(len(Q_PARTS)):
                    for tile, qk, part in ((q6, 0, Q_PARTS[r]), (k6, 1, K_PARTS[r])):
                        sp.dma_start(tile[r * DH:(r + 1) * DH, s].bitcast(F32),
                                     qk_parts[qk, part, :, half].rearrange("(h d) n -> d h n", d=DH))\
                            .then_inc(loaded[s], 16)
                sp.dma_start(v[:, s], v_pad[tok, :].rearrange("(k p) c -> p k c", p=P))\
                    .then_inc(loaded[s], 16)

            def body(i, s, last):
                if not last:
                    tok = at(sp, i * (2 * S) + (s + 1) * S, S)
                    half = at(sp, i * S + (s + 1) * (S // 2), S // 2)
                    wait_apart(sp, batch_done, i * 2 + (s + 1), consts, NCONST)
                    load(tok, half, 1 - s)
                tok = at(sp, i * (2 * S) + s * S, S)
                for j in range(QUADS):
                    wait_apart(sp, o_ready, i * (2 * QUADS) + (s * QUADS + j + 3), consts, NCONST)
                    sp.dma_start(out_T[j, :, tok], o_norm[:, j % 2])\
                        .then_inc(stored[j % 2], 16)

            load(slice(0, S), slice(0, S // 2), 0)
            paired(sp, B, body)
            for s in range(2):
                sp.wait_ge(stored[s], B * QUADS // 2 * 16 + 16)

        @block.tensor
        def _(pe):
            pe.sem_inc(pv_done, 2)
            pe.sem_inc(batch_done, 1)
            pe.wait_ge(consts, NCONST)
            pe.wait_ge(filled, 1)
            pe.wait_ge(ones_set, 1)

            def maximum_rows(n, buf):
                pe.wait_ge(mparts_done, n + 1)
                for c in range(4):
                    mm = nc.tensor.matmul(m_ps[ROWS:ROWS + MAX_ROWS, c], mparts[:, buf, c, :],
                                          ident[:], start=True, stop=True, tile_position=(0, ROWS))
                mm.then_inc(mrow_done, 1)

            def scores(s, p):
                buf = p % 2
                for h2 in range(2):
                    h = 2 * p + h2
                    for qt in range(2):
                        mm = nc.tensor.matmul(s_ps[:, buf, h2, qt], q6[0:ROWS, s, h, qt * P:(qt + 1) * P],
                                              k6[0:ROWS, s, h, :], start=True, stop=not n_masks)
                        if n_masks:
                            kt = 1 - qt
                            mm = nc.tensor.matmul(s_ps[:, buf, h2, qt, kt * P:(kt + 1) * P], ident[:],
                                                  masks[:, qt], start=False, stop=True)
                mm.then_inc(s_done, 1)

            def values(s, j):
                for half, wide in ((0, None), (1, ones)):
                    for kt in range(2):
                        for c in range(4):
                            h = 4 * j + c
                            st = v[:, s, kt, h * 32:(h + 1) * 32] if wide is None else wide[:]
                            mm = nc.tensor.matmul(o_ps[32 * c:32 * c + 32, half], st,
                                                  probs[:, j % 2, c, kt],
                                                  start=(kt == 0), stop=(kt == 1),
                                                  tile_position=(0, 32 * c))
                mm.then_inc(pv_done, 1)

            def wait_values(i, s, j):
                pe.wait_ge(t_free, i * (2 * H) + (s * H + 4 * j + 6))
                pe.wait_ge(o_free, i * (2 * QUADS) + (s * QUADS + j + 1))

            def body(i, s, last):
                for p in range(PAIRS):
                    n = i * (2 * PAIRS) + (s * PAIRS + p)
                    if p + 2 < PAIRS or not last:
                        pe.wait_ge(max_done, n + 1)
                        if p + 2 == PAIRS:
                            pe.wait_ge(loaded[1 - s], i * (16 * nload) + 16 * nload * (s + 1))
                        scores((s + (p + 2) // PAIRS) % 2, (p + 2) % PAIRS)
                    if p + 1 < PAIRS or not last:
                        pe.wait_ge(mcopied, n + 1)
                        maximum_rows(n + 1, (p + 1) % 2)
                    if p % 2 == 0 and p:
                        wait_values(i, s, p // 2 - 1)
                        values(s, p // 2 - 1)
                    if last and p == PAIRS - 1:
                        pe.wait_ge(mcopied, n + 1)
                    for h2 in range(2):
                        h = 2 * p + h2
                        pe.wait_ge(t_free, i * (2 * H) + (s * H + h + 1))
                        for kt in range(2):
                            mm = nc.tensor.matmul(t_ps[:, h2, kt],
                                                  k6[0:ROWS + MAX_ROWS, s, h, kt * P:(kt + 1) * P],
                                                  q6[0:ROWS + MAX_ROWS, s, h, :],
                                                  start=True, stop=not n_masks)
                            if n_masks:
                                qt = 1 - kt
                                mm = nc.tensor.matmul(t_ps[:, h2, kt, qt * P:(qt + 1) * P], ident[:],
                                                      masks[:, 2 + kt], start=False, stop=True)
                        mm.then_inc(t_done, 1)
                wait_values(i, s, QUADS - 1)
                values(s, QUADS - 1)
                pe.drain().then_inc(batch_done, 1)

            pe.wait_ge(loaded[0], 16 * nload)
            scores(0, 0)
            scores(0, 1)
            maximum_rows(0, 0)
            paired(pe, B, body)

        @block.vector
        def _(dve):
            dve.wait_ge(consts, NCONST)
            nc.vector.tensor_copy(ident[:], consts_f32[:, 4])
            if n_masks:
                nc.vector.tensor_copy(masks[:], consts_f32[:, 0:4])
            nc.vector.memset(ones[:], 1.0).then_inc(filled, 1)
            dve.sem_inc(o_free, 1)

            def maximum(n, p):
                dve.wait_ge(s_done, n)
                nc.vector.tensor_reduce(nmax[:, p % 2], s_ps[:, p % 2].rearrange("p a b n -> p (a b) n"),
                                        axis=AX.X, op=ALU.max, negate=True).then_inc(max_done, 1)

            def sums(i, s, j):
                dve.wait_ge(o_copied, i * (2 * QUADS) + (s * QUADS + j + 1))
                nc.vector.reciprocal(rsum[:, j % 2], o_ps[:, 1]).then_inc(o_free, 1)

            def body(i, s, last):
                for p in range(PAIRS):
                    if not (last and p >= PAIRS - 2):
                        maximum(i * (2 * PAIRS) + (s * PAIRS + p + 3), p)
                    if p % 2 == 0 and p:
                        sums(i, s, p // 2 - 1)
                sums(i, s, QUADS - 1)

            maximum(1, 0)
            maximum(2, 1)
            paired(dve, B, body)

        @block.gpsimd
        def _(pool):
            nc.gpsimd.memset(k6[ROWS:ROWS + MAX_ROWS], 1.0).then_inc(ones_set, 1)
            pool.sem_inc(o_ready, 2)

            def split_maximum(n, buf):
                wait_apart(pool, max_done, n, ones_set, 1)
                nc.gpsimd.tensor_copy(mparts[:, buf, :, 0], nmax[:, buf]).then_inc(hi_done, 1)
                pool.wait_ge(hi_done, n)
                nc.gpsimd.tensor_tensor(mparts[:, buf, :, 1], nmax[:, buf], mparts[:, buf, :, 0],
                                        ALU.subtract).then_inc(mparts_done, 1)

            def body(i, s, last):
                def norm(j):
                    n = i * (2 * QUADS) + (s * QUADS + j)
                    pool.wait_ge(o_free, n + 2)
                    pool.wait_ge(stored[j % 2], i * (QUADS * 16) + (s * QUADS // 2 + j // 2) * 16 + 16)
                    nc.gpsimd.tensor_tensor(o_norm[:, j % 2], o_sb[:, j % 2], rsum[:, j % 2], ALU.mult)\
                        .then_inc(o_ready, 1)
                for p in range(PAIRS):
                    if not (last and p >= PAIRS - 2):
                        split_maximum(i * (2 * PAIRS) + (s * PAIRS + p + 3), p % 2)
                    if p % 2 == 0 and p:
                        norm(p // 2 - 1)
                norm(QUADS - 1)

            split_maximum(1, 0)
            split_maximum(2, 1)
            paired(pool, B, body)

        @block.scalar
        def _(act):
            act.sem_inc(t_free, 2)

            def copy_rows(n, s, p):
                act.wait_ge(mrow_done, n)
                nc.scalar.activation(q6[ROWS:ROWS + MAX_ROWS, s, 2 * p:2 * p + 2, :],
                                     m_ps[ROWS:ROWS + MAX_ROWS].rearrange("p (a b) n -> p a (b n)", a=2),
                                     ACT.Copy).then_inc(mcopied, 1)

            def body(i, s, last):
                def copy_out(j):
                    n = i * (2 * QUADS) + (s * QUADS + j)
                    act.wait_ge(pv_done, n + 3)
                    act.wait_ge(o_ready, n + 1)
                    nc.scalar.activation(o_sb[:, j % 2], o_ps[:, 0], ACT.Copy).then_inc(o_copied, 1)
                for p in range(PAIRS):
                    if p + 1 < PAIRS or not last:
                        copy_rows(i * (2 * PAIRS) + (s * PAIRS + p + 2), (s + (p + 1) // PAIRS) % 2, (p + 1) % PAIRS)
                    for h2 in range(2):
                        h = 2 * p + h2
                        act.wait_ge(t_done, i * (2 * H) + (s * H + h + 1))
                        act.wait_ge(pv_done, i * (2 * QUADS) + (s * QUADS + h // 4 + 1))
                        nc.scalar.activation(probs[:, (h // 4) % 2, h % 4], t_ps[:, h2],
                                             ACT.Exp, scale=scale).then_inc(t_free, 1)
                    if p % 2 == 0 and p:
                        copy_out(p // 2 - 1)
                copy_out(QUADS - 1)

            copy_rows(1, 0, 0)
            paired(act, B, body)


def phase_post(nc, name, o_T, groups, w_out, padded, bias, x_in, ident, x_out, x_outT):
    with Phase(nc, name) as ph:
        w = ph.sb("w", [P, max(groups, 1), D])
        bias_sb = ph.sb("bias", [P, TPB, D])
        idt = ph.sb("idt", [P, P])
        power = ph.sb("power", [P, TPB])
        o = ph.sb("o", [P, 2, max(groups, 1), BLK])
        x = ph.sb("x", [P, 2, TPB, D])
        xb = ph.sb("xb", [P, 2, TPB, D])
        r = ph.sb("r", [P, 2, TPB, D])
        stats = ph.sb("stats", [P, 2, TPB, 6])
        mv = ph.sb("mv", [P, 2, TPB, 2])
        vare = ph.sb("vare", [P, 2, TPB])
        rstd = ph.sb("rstd", [P, 2, TPB])
        xo = ph.sb("xo", [P, 2, TPB, D])
        xoT = ph.sb("xoT", [P, 2, KD, BLK])
        y_ps = ph.ps("y_ps", [P, 2, TPB, D])
        xT_ps = ph.ps("xT_ps", [P, KD, BLK])
        consts = ph.sem("consts")
        zeroed = ph.sem("zeroed")
        power_set = ph.sem("power_set")
        loaded = [ph.sem(f"loaded{s}") for s in range(2)]
        in_free = ph.sem("in_free")
        y_done = ph.sem("y_done")
        biased = ph.sem("biased")
        summed = ph.sem("summed")
        stats_done = ph.sem("stats_done")
        mv_done = ph.sem("mv_done")
        vare_done = ph.sem("vare_done")
        rstd_done = ph.sem("rstd_done")
        normed = ph.sem("normed")
        xT_done = ph.sem("xT_done")
        xT_out = ph.sem("xT_out")
        stored = [ph.sem(f"stored{s}") for s in range(2)]
        block = ph.block()
        n_in = 2 if groups else 1
        n_out = 2 if x_outT is not None else 1
        NCONST = 16 * (1 + (groups and (4 if padded else 1)) + (TPB if bias is not None else 0))

        @block.sync
        def _(sp):
            for s in range(2):
                sp.sem_inc(stored[s], 16)
            sp.dma_start(idt[:], ident).then_inc(consts, 16)
            if groups and padded:
                sp.wait_ge(zeroed, 1)
                rows = w_out.rearrange("(g c d) n -> c d g n", c=4, d=DH)
                for c in range(4):
                    sp.dma_start(w[32 * c:32 * c + DH], rows[c]).then_inc(consts, 16)
            elif groups:
                sp.wait_ge(zeroed, 1)
                sp.dma_start(w[:], w_out.rearrange("(g p) n -> p g n", p=P)).then_inc(consts, 16)
            if bias is not None:
                for t in range(TPB):
                    sp.dma_start(bias_sb[:, t], bias.partition_broadcast(P)).then_inc(consts, 16)

            def load(i, s):
                tok = at(sp, i * (2 * BLK) + s * BLK, BLK)
                wait_apart(sp, in_free, i * 2 + (s + 1), consts, NCONST)
                if groups:
                    sp.dma_start(o[:, s], o_T[:, :, tok].rearrange("g p n -> p g n")).then_inc(loaded[s], 16)
                sp.dma_start(x[:, s], x_in[tok, :].rearrange("(t p) c -> p t c", p=P)).then_inc(loaded[s], 16)

            def body(i, s, last):
                if not last:
                    load(i + s, 1 - s)
                tok = at(sp, i * (2 * BLK) + s * BLK, BLK)
                wait_apart(sp, normed, i * 2 + (s + 1), consts, NCONST)
                sp.dma_start(x_out[tok, :].rearrange("(t p) c -> p t c", p=P), xo[:, s]).then_inc(stored[s], 16)
                if x_outT is not None:
                    wait_apart(sp, xT_out, i * 2 + (s + 2), consts, NCONST)
                    sp.dma_start(x_outT[:, tok].rearrange("(k p) n -> p k n", p=P), xoT[:, s])\
                        .then_inc(stored[s], 16)

            load(0, 0)
            paired(sp, NBLK, body)
            for s in range(2):
                sp.wait_ge(stored[s], NBLK // 2 * 16 * n_out + 16)

        @block.tensor
        def _(pe):
            pe.wait_ge(consts, NCONST)
            if groups:
                pe.wait_ge(zeroed, 1)

            def project(i, s):
                pe.wait_ge(loaded[s], i * (16 * n_in) + 16 * n_in)
                for t in range(TPB):
                    for g in range(groups):
                        mm = nc.tensor.matmul(y_ps[:, s, t], o[:, s, g, t * P:(t + 1) * P], w[:, g],
                                              start=(g == 0), stop=(g == groups - 1))
                mm.then_inc(y_done, 1)

            def body(i, s, last):
                if groups and not last:
                    project(i + s, 1 - s)
                if x_outT is not None:
                    pe.wait_ge(normed, i * 2 + (s + 1))
                    pe.wait_ge(xT_out, i * 2 + (s + 1))
                    for t in range(TPB):
                        for k in range(KD):
                            mm = nc.tensor.transpose(xT_ps[:, k, t * P:(t + 1) * P],
                                                     xo[:, s, t, k * P:(k + 1) * P], idt[:])
                    mm.then_inc(xT_done, 1)
            if groups:
                project(0, 0)
            paired(pe, NBLK, body)

        @block.gpsimd
        def _(pool):
            nc.gpsimd.memset(w[:], 0.0).then_inc(zeroed, 1)
            nc.gpsimd.memset(power[:], -0.5).then_inc(power_set, 1)
            if bias is not None:
                pool.wait_ge(consts, NCONST)

            def body(i, s, last):
                if bias is not None:
                    pool.wait_ge(loaded[s], i * (16 * n_in) + 16 * n_in)
                    nc.gpsimd.tensor_tensor(xb[:, s], x[:, s], bias_sb[:], ALU.add).then_inc(biased, 1)
                wait_apart(pool, mv_done, i * 2 + (s + 1), power_set, 1)
                nc.gpsimd.tensor_scalar(vare[:, s], mv[:, s, :, 1], LN_EPS, None, ALU.add).then_inc(vare_done, 1)
                pool.wait_ge(vare_done, i * 2 + (s + 1))
                nc.gpsimd.tensor_tensor(rstd[:, s], vare[:, s], power[:], ALU.pow).then_inc(rstd_done, 1)
            paired(pool, NBLK, body)

        @block.vector
        def _(dve):
            dve.sem_inc(in_free, 2)

            def body(i, s, last):
                n = i * 2 + (s + 1)
                res = xb if bias is not None else x
                if groups:
                    dve.wait_ge(y_done, n)
                    if bias is not None:
                        dve.wait_ge(biased, n)
                    dve.wait_ge(loaded[s], i * (16 * n_in) + 16 * n_in)
                    nc.vector.tensor_tensor(r[:, s], y_ps[:, s], res[:, s], ALU.add).then_inc(summed, 1)
                else:
                    dve.wait_ge(loaded[s], i * (16 * n_in) + 16 * n_in)
                    nc.vector.tensor_copy(r[:, s], x[:, s]).then_inc(summed, 1)
                dve.wait_ge(summed, n)
                dve.sem_inc(in_free, 1)
                for t in range(TPB):
                    last_op = nc.vector.bn_stats(stats[:, s, t], r[:, s, t])
                last_op.then_inc(stats_done, 1)
                wait_apart(dve, stats_done, n, consts, NCONST)
                for t in range(TPB):
                    last_op = nc.vector.bn_aggr(mv[:, s, t], stats[:, s, t])
                last_op.then_inc(mv_done, 1)
                dve.wait_ge(stored[s], i * (16 * n_out) + 16)
                dve.wait_ge(mv_done, n)
                dve.wait_ge(rstd_done, n)
                for t in range(TPB):
                    last_op = nc.vector.tensor_scalar(xo[:, s, t], r[:, s, t], mv[:, s, t, 0:1],
                                                      rstd[:, s, t:t + 1], ALU.subtract, ALU.mult)
                last_op.then_inc(normed, 1)
            paired(dve, NBLK, body)

        @block.scalar
        def _(act):
            act.sem_inc(xT_out, 1)

            def body(i, s, last):
                if x_outT is not None:
                    act.wait_ge(stored[s], i * (16 * n_out) + 16)
                    act.wait_ge(xT_done, i * 2 + (s + 1))
                    for k in range(KD):
                        op = nc.scalar.activation(xoT[:, s, k], xT_ps[:, k], ACT.Copy)
                    op.then_inc(xT_out, 1)
            paired(act, NBLK, body)


def phase_cross(nc, xT, ctxT, Wq, bq, Wk, bk, Wv, bv, ident, o_T):
    with Phase(nc, "cross") as ph:
        PAIRS = H // 2
        wq = ph.sb("wq", [P, KD, DM])
        wk = ph.sb("wk", [P, KD, DM])
        wv = ph.sb("wv", [P, KD, DM])
        bqs = ph.sb("bqs", [P, PAIRS])
        bks = ph.sb("bks", [P, PAIRS])
        bvs = ph.sb("bvs", [P, 2, DM])
        idt = ph.sb("idt", [P, P])
        x = ph.sb("x", [P, 2, KD, S])
        c = ph.sb("c", [P, 2, KD, S])
        q = ph.sb("q", [P, 2, 2, S])
        k = ph.sb("k", [P, 2, 2, S])
        v = ph.sb("v", [P, 2, 2, 4, DX])
        nmax = ph.sb("nmax", [P, 2, 2])
        probs = ph.sb("probs", [P, 2, 2, 2, S])
        rsum = ph.sb("rsum", [P, S])
        on = ph.sb("on", [P, 2, S])
        qk_ps = ph.ps("qk_ps", [P, 2, S])
        v_ps = ph.ps("v_ps", [P, 2, 2, DX])
        s_ps = ph.ps("s_ps", [P, 2, 2, S])
        t_ps = ph.ps("t_ps", [P, 2, 2, S])
        m_ps = ph.ps("m_ps", [P, 2 * S])
        o_ps = ph.ps("o_ps", [P, 2, S])
        consts = ph.sem("consts")
        NCONST = 16 * 8
        k_filled = ph.sem("k_filled")
        v_filled = ph.sem("v_filled")
        q_filled = ph.sem("q_filled")
        loaded = [ph.sem(f"loaded{s}") for s in range(2)]
        in_free = ph.sem("in_free")
        qk_done = ph.sem("qk_done")
        qk_out = ph.sem("qk_out")
        vp_done = ph.sem("vp_done")
        v_out = ph.sem("v_out")
        s_done = ph.sem("s_done")
        max_done = ph.sem("max_done")
        m_done = ph.sem("m_done")
        m_out = ph.sem("m_out")
        t_done = ph.sem("t_done")
        t_free = ph.sem("t_free")
        pv_done = ph.sem("pv_done")
        rsum_done = ph.sem("rsum_done")
        o_ready = ph.sem("o_ready")
        stored = [ph.sem(f"stored{s}") for s in range(2)]
        block = ph.block()

        @block.sync
        def _(sp):
            for s in range(2):
                sp.sem_inc(stored[s], 16)
            for dst, src in ((wq, Wq), (wk, Wk), (wv, Wv)):
                sp.dma_start(dst[:], src.rearrange("(k p) n -> p k n", p=P)).then_inc(consts, 16)
            for dst, src in ((bqs, bq), (bks, bk)):
                sp.dma_start(dst[:], src.rearrange("(m p) -> p m", p=P),
                             allow_slow_non_contiguous=True).then_inc(consts, 16)
            for t in range(2):
                sp.dma_start(bvs[:, t], bv.partition_broadcast(P)).then_inc(consts, 16)
            sp.dma_start(idt[:], ident).then_inc(consts, 16)

            def load(i, s):
                tok = at(sp, i * (2 * S) + s * S, S)
                wait_apart(sp, in_free, i * 2 + (s + 1), consts, NCONST)
                for dst, src in ((x, xT), (c, ctxT)):
                    sp.dma_start(dst[:, s], src[:, tok].rearrange("(k p) n -> p k n", p=P))\
                        .then_inc(loaded[s], 16)

            def body(i, s, last):
                if not last:
                    load(i + s, 1 - s)
                tok = at(sp, i * (2 * S) + s * S, S)
                for p in range(PAIRS):
                    wait_apart(sp, o_ready, i * (2 * PAIRS) + (s * PAIRS + p + 2), consts, NCONST)
                    sp.dma_start(o_T[p, :, tok], on[:, p % 2]).then_inc(stored[p % 2], 16)

            load(0, 0)
            paired(sp, B, body)
            for s in range(2):
                sp.wait_ge(stored[s], B * PAIRS // 2 * 16 + 16)

        @block.tensor
        def _(pe):
            pe.sem_inc(in_free, 2)
            pe.wait_ge(consts, NCONST)
            pe.wait_ge(k_filled, 1)
            pe.wait_ge(q_filled, 1)
            pe.wait_ge(v_filled, 1)

            def project_qk(s, p):
                for j, (wt, src) in enumerate(((wq, x), (wk, c))):
                    for kd in range(KD):
                        mm = nc.tensor.matmul(qk_ps[:, j], wt[:, kd, p * P:(p + 1) * P], src[:, s, kd],
                                              start=(kd == 0), stop=(kd == KD - 1))
                mm.then_inc(qk_done, 1)

            def project_v(s, p):
                for t in range(2):
                    for kd in range(KD):
                        mm = nc.tensor.matmul(v_ps[:, t].rearrange("p a b -> p (a b)"),
                                              c[:, s, kd, t * P:(t + 1) * P],
                                              wv[:, kd, p * P:(p + 1) * P],
                                              start=(kd == 0), stop=(kd == KD - 1))
                mm.then_inc(vp_done, 1)

            def scores(buf):
                for h2 in range(2):
                    for qt in range(2):
                        mm = nc.tensor.matmul(s_ps[:, h2, qt], q[:, buf, h2, qt * P:(qt + 1) * P],
                                              k[:, buf, h2], start=True, stop=True)
                    mm.then_inc(s_done, 1)

            def body(i, s, last):
                for p in range(PAIRS):
                    n = i * (2 * PAIRS) + (s * PAIRS + p)
                    more = p + 1 < PAIRS or not last
                    ns, np_ = ((s + 1) % 2, 0) if p + 1 == PAIRS else (s, p + 1)
                    if more:
                        if np_ == 0:
                            pe.wait_ge(loaded[ns], i * 32 + 32 * (s + 1))
                        pe.wait_ge(qk_out, n + 2)
                        project_qk(ns, np_)
                    pe.wait_ge(max_done, n * 2 + 2)
                    for h2 in range(2):
                        at_row = DX * (1 - h2)
                        for qt in range(2):
                            mm = nc.tensor.matmul(m_ps[at_row:at_row + 1, qt * P:(qt + 1) * P],
                                                  nmax[:, h2, qt:qt + 1], idt[:], start=True, stop=True,
                                                  tile_position=(0, at_row))
                    mm.then_inc(m_done, 1)
                    if p:
                        values(i, s, p - 1, n)
                    if more:
                        pe.wait_ge(v_out, n + 2)
                        project_v(ns, np_)
                        if np_ == PAIRS - 1:
                            pe.drain().then_inc(in_free, 1)
                    pe.wait_ge(m_out, n + 1)
                    for h2 in range(2):
                        pe.wait_ge(t_free, n * 2 + (h2 + 1))
                        for kt in range(2):
                            mm = nc.tensor.matmul(t_ps[:, h2, kt], k[:, p % 2, h2, kt * P:(kt + 1) * P],
                                                  q[:, p % 2, h2], start=True, stop=True)
                        mm.then_inc(t_done, 1)
                    if more:
                        pe.wait_ge(qk_out, n + 3)
                        pe.wait_ge(max_done, n * 2 + 2)
                        scores((p + 1) % 2)
                values(i, s, PAIRS - 1, i * (2 * PAIRS) + (s * PAIRS + PAIRS))

            def values(i, s, p, n):
                pe.wait_ge(t_free, n * 2 + 2)
                pe.wait_ge(v_out, n + 1)
                pe.wait_ge(o_ready, n)
                for h2 in range(2):
                    for kt in range(2):
                        mm = nc.tensor.matmul(o_ps[:, h2],
                                              v[:, p % 2, kt, 2 * h2:2 * h2 + 2].rearrange("p a b -> p (a b)"),
                                              probs[:, p % 2, h2, kt], start=(kt == 0), stop=(kt == 1))
                mm.then_inc(pv_done, 1)

            pe.wait_ge(loaded[0], 32)
            pe.wait_ge(qk_out, 1)
            project_qk(0, 0)
            pe.wait_ge(v_out, 1)
            project_v(0, 0)
            pe.wait_ge(qk_out, 2)
            scores(0)
            paired(pe, B, body)

        @block.scalar
        def _(act):
            act.sem_inc(qk_out, 1)
            act.sem_inc(t_free, 2)
            act.wait_ge(consts, NCONST)
            act.wait_ge(k_filled, 1)
            act.wait_ge(q_filled, 1)

            def copy_qk(n, p):
                act.wait_ge(qk_done, n)
                for dst, j, b in ((q, 0, bqs), (k, 1, bks)):
                    for h2 in range(2):
                        rows = slice(DX * h2, DX * h2 + DX)
                        op = nc.scalar.activation(dst[rows, p % 2, h2], qk_ps[rows, j], ACT.Identity,
                                                  bias=b[rows, p:p + 1])
                op.then_inc(qk_out, 1)

            def body(i, s, last):
                for p in range(PAIRS):
                    n = i * (2 * PAIRS) + (s * PAIRS + p)
                    if p + 1 < PAIRS or not last:
                        copy_qk(n + 2, (p + 1) % PAIRS)
                    act.wait_ge(m_done, n + 1)
                    for h2 in range(2):
                        row = DX * (1 - h2)
                        op = nc.scalar.activation(q[row:row + 1, p % 2, h2], m_ps[row:row + 1, 0:S], ACT.Copy)
                    op.then_inc(m_out, 1)
                    for h2 in range(2):
                        act.wait_ge(t_done, n * 2 + (h2 + 1))
                        nc.scalar.activation(probs[:, p % 2, h2], t_ps[:, h2], ACT.Exp,
                                             scale=1.0 / DX ** 0.5).then_inc(t_free, 1)
            copy_qk(1, 0)
            paired(act, B, body)

        @block.vector
        def _(dve):
            dve.sem_inc(v_out, 1)
            dve.sem_inc(o_ready, 1)
            dve.wait_ge(consts, NCONST)
            dve.wait_ge(v_filled, 1)

            def copy_v(n, p):
                dve.wait_ge(vp_done, n)
                nc.vector.tensor_tensor(v[:, p % 2, :, 0:4:3, :], v_ps[:],
                                        bvs[:, :, p * P:(p + 1) * P].rearrange("p t (a b) -> p t a b", a=2),
                                        ALU.add).then_inc(v_out, 1)

            def maxima(n):
                for h2 in range(2):
                    dve.wait_ge(s_done, n * 2 + (h2 + 1))
                    nc.vector.tensor_reduce(nmax[:, h2], s_ps[:, h2], axis=AX.X, op=ALU.max,
                                            negate=True).then_inc(max_done, 1)

            def normalise(i, s, p, n):
                dve.wait_ge(pv_done, n)
                dve.wait_ge(stored[p % 2], i * (PAIRS * 16) + (s * PAIRS // 2 + p // 2) * 16 + 16)
                for h2 in range(2):
                    own = slice(DX * h2, DX * h2 + DX)
                    other = slice(DX * (1 - h2), DX * (1 - h2) + DX)
                    op = nc.vector.reciprocal(rsum[own], o_ps[other, h2])
                op.then_inc(rsum_done, 1)
                dve.wait_ge(rsum_done, n)
                for h2 in range(2):
                    own = slice(DX * h2, DX * h2 + DX)
                    op = nc.vector.tensor_tensor(on[own, p % 2], o_ps[own, h2], rsum[own], ALU.mult)
                op.then_inc(o_ready, 1)

            def body(i, s, last):
                for p in range(PAIRS):
                    n = i * (2 * PAIRS) + (s * PAIRS + p)
                    if p:
                        normalise(i, s, p - 1, n)
                    if p + 1 < PAIRS or not last:
                        copy_v(n + 2, (p + 1) % PAIRS)
                        dve.wait_ge(m_done, n + 1)
                        maxima(n + 1)
                normalise(i, s, PAIRS - 1, i * (2 * PAIRS) + (s * PAIRS + PAIRS))
            copy_v(1, 0)
            maxima(0)
            paired(dve, B, body)

        @block.gpsimd
        def _(pool):
            nc.gpsimd.memset(q[:], 0.0).then_inc(q_filled, 1)
            nc.gpsimd.memset(v[:], 1.0).then_inc(v_filled, 1)
            nc.gpsimd.memset(k[:], 0.0)
            pool.drain()
            nc.gpsimd.memset(k[DX:DX + 1, :, 0], 1.0)
            nc.gpsimd.memset(k[0:1, :, 1], 1.0).then_inc(k_filled, 1)


def phase_rwkv_in(nc, xT, maas, WT, qk_parts, v_pad, gate):
    with Phase(nc, "rin") as ph:
        w = ph.sb("w", [P, 4, KD, D])
        maa = ph.sb("maa", [P, 4, KD])
        x = ph.sb("x", [P, 2, KD, 2, S + 1])
        dx = ph.sb("dx", [P, KD, 2, S])
        mix = ph.sb("mix", [P, 4, KD, BLK])
        parts = ph.sb("parts", [P, 2, 4, 3, BLK], BF16)
        rest = ph.sb("rest", [P, 2, BLK])
        vp = ph.sb("vp", [P, 2, TPB, H, 32])
        g = ph.sb("g", [P, 2, TPB, D])
        qk_ps = ph.ps("qk_ps", [P, 4, BLK])
        v_ps = ph.ps("v_ps", [P, TPB, D])
        g_ps = ph.ps("g_ps", [P, TPB, D])
        consts = ph.sem("consts")
        NCONST = 16 * 8
        x_loaded = [ph.sem(f"x_loaded{s}") for s in range(2)]
        x_free = ph.sem("x_free")
        x_zeroed = ph.sem("x_zeroed")
        dx_done = ph.sem("dx_done")
        mixed = ph.sem("mixed")
        mix_free = ph.sem("mix_free")
        qk_done = ph.sem("qk_done")
        hi_done = ph.sem("hi_done")
        rest_done = ph.sem("rest_done")
        mid_done = ph.sem("mid_done")
        parts_done = ph.sem("parts_done")
        v_zeroed = ph.sem("v_zeroed")
        v_done = ph.sem("v_done")
        v_out = ph.sem("v_out")
        g_done = ph.sem("g_done")
        g_out = ph.sem("g_out")
        stored = [ph.sem(f"stored{s}") for s in range(2)]
        block = ph.block()

        @block.sync
        def _(sp):
            for s in range(2):
                sp.sem_inc(stored[s], 16)
            for j in range(4):
                sp.dma_start(w[:, j], WT[j].rearrange("(k p) n -> p k n", p=P)).then_inc(consts, 16)
                sp.dma_start(maa[:, j], maas[j].rearrange("a b (k p) -> p (a b k)", p=P),
                             allow_slow_non_contiguous=True).then_inc(consts, 16)
            sp.wait_ge(x_zeroed, 1)

            def load(i, s):
                tok = at(sp, i * (2 * BLK) + s * BLK, BLK)
                wait_apart(sp, x_free, i * 2 + (s + 1), consts, NCONST)
                for k in range(KD):
                    sp.dma_start(x[:, s, k, :, 1:S + 1], xT[k * P:(k + 1) * P, tok]
                                 .rearrange("p (b n) -> p b n", b=2)).then_inc(x_loaded[s], 16)

            def body(i, s, last):
                if not last:
                    load(i + s, 1 - s)
                tok = at(sp, i * (2 * BLK) + s * BLK, BLK)
                half = at(sp, i * BLK + s * (BLK // 2), BLK // 2)
                for m in range(4):
                    wait_apart(sp, parts_done, i * 8 + (s * 4 + m + 3), consts, NCONST)
                    sp.dma_start(qk_parts[m // 2, :, (m % 2) * P:(m % 2 + 1) * P, half]
                                 .rearrange("a p n -> p a n"), parts[:, s, m].bitcast(F32)).then_inc(stored[s], 16)
                wait_apart(sp, v_out, i * 4 + (s * 2 + 4), consts, NCONST)
                sp.dma_start(v_pad[tok, :].rearrange("(t p) c -> p t c", p=P),
                             vp[:, s].rearrange("p t h c -> p t (h c)")).then_inc(stored[s], 16)
                wait_apart(sp, g_out, i * 4 + (s * 2 + 4), consts, NCONST)
                sp.dma_start(gate[tok, :].rearrange("(t p) c -> p t c", p=P), g[:, s]).then_inc(stored[s], 16)

            load(0, 0)
            paired(sp, NBLK, body)
            for s in range(2):
                sp.wait_ge(stored[s], NBLK // 2 * 6 * 16 + 16)

        @block.vector
        def _(dve):
            dve.sem_inc(x_free, 2)
            dve.sem_inc(rest_done, 4)
            dve.sem_inc(v_out, 2)
            nc.vector.memset(x[:, :, :, :, 0:1], 0.0).then_inc(x_zeroed, 1)
            dve.wait_ge(consts, NCONST)
            dve.wait_ge(x_zeroed, 1)
            dve.wait_ge(v_zeroed, 1)

            def shift(i, s):
                n = i * 2 + (s + 1)
                dve.wait_ge(x_loaded[s], i * 32 + 32)
                nc.vector.tensor_tensor(dx[:].rearrange("p k b n -> p (k b) n"),
                                        x[:, s, :, :, 0:S].rearrange("p k b n -> p (k b) n"),
                                        x[:, s, :, :, 1:S + 1].rearrange("p k b n -> p (k b) n"),
                                        ALU.subtract).then_inc(dx_done, 1)
                dve.wait_ge(mix_free, n)
                dve.wait_ge(dx_done, n)
                for j in range(4):
                    for k in range(KD):
                        op = nc.vector.scalar_tensor_tensor(
                            mix[:, j, k].rearrange("p (b n) -> p b n", b=2), dx[:, k], maa[:, j, k:k + 1],
                            x[:, s, k, :, 1:S + 1], ALU.mult, ALU.add)
                    op.then_inc(mixed, 1)
                dve.wait_ge(mixed, n * 4)
                dve.sem_inc(x_free, 1)

            def body(i, s, last):
                shift(i, s)
                for m in range(4):
                    dve.wait_ge(hi_done, i * 8 + (s * 4 + m + 1))
                    dve.wait_ge(parts_done, i * 8 + (s * 4 + m + 1))
                    nc.vector.tensor_tensor(rest[:, m % 2], qk_ps[:, m], parts[:, s, m, 0], ALU.subtract)\
                        .then_inc(rest_done, 1)
                dve.wait_ge(stored[s], i * (6 * 16) + 16)
                for t in (0, 2):
                    dve.wait_ge(v_done, i * 4 + (s * 2 + t // 2 + 1))
                    nc.vector.tensor_copy(vp[:, s, t:t + 2, :, 0:DH],
                                          v_ps[:, t:t + 2].rearrange("p t (h c) -> p t h c", c=DH))\
                        .then_inc(v_out, 1)
            paired(dve, NBLK, body)

        @block.tensor
        def _(pe):
            pe.sem_inc(mix_free, 1)
            pe.wait_ge(consts, NCONST)

            def body(i, s, last):
                for m in range(4):
                    pe.wait_ge(mixed, i * 8 + (s * 4 + m // 2 + 1))
                    pe.wait_ge(rest_done, i * 8 + (s * 4 + m + 1))
                    for k in range(KD):
                        mm = nc.tensor.matmul(qk_ps[:, m], w[:, m // 2, k, (m % 2) * P:(m % 2 + 1) * P],
                                              mix[:, m // 2, k], start=(k == 0), stop=(k == KD - 1))
                    mm.then_inc(qk_done, 1)
                for j, out, free, done in ((2, v_ps, v_out, v_done), (3, g_ps, g_out, g_done)):
                    pe.wait_ge(mixed, i * 8 + (s * 4 + j + 1))
                    for t in range(TPB):
                        if t % 2 == 0:
                            pe.wait_ge(free, i * 4 + (s * 2 + t // 2 + 1))
                        for k in range(KD):
                            mm = nc.tensor.matmul(out[:, t], mix[:, j, k, t * P:(t + 1) * P], w[:, j, k],
                                                  start=(k == 0), stop=(k == KD - 1))
                        if t % 2:
                            mm.then_inc(done, 1)
                pe.drain().then_inc(mix_free, 1)
            paired(pe, NBLK, body)

        @block.scalar
        def _(act):
            act.sem_inc(g_out, 2)

            def body(i, s, last):
                act.wait_ge(stored[s], i * (6 * 16) + 16)
                for m in range(4):
                    act.wait_ge(qk_done, i * 8 + (s * 4 + m + 1))
                    nc.scalar.activation(parts[:, s, m, 0], qk_ps[:, m], ACT.Copy).then_inc(hi_done, 1)
                for t in (0, 2):
                    act.wait_ge(g_done, i * 4 + (s * 2 + t // 2 + 1))
                    nc.scalar.activation(g[:, s, t:t + 2].rearrange("p t c -> p (t c)"),
                                         g_ps[:, t:t + 2].rearrange("p t c -> p (t c)"), ACT.Gelu)\
                        .then_inc(g_out, 1)
            paired(act, NBLK, body)

        @block.gpsimd
        def _(pool):
            nc.gpsimd.memset(vp[:], 0.0).then_inc(v_zeroed, 1)
            pool.sem_inc(parts_done, 2)

            def body(i, s, last):
                for m in range(4):
                    wait_apart(pool, rest_done, i * 8 + (s * 4 + m + 5), v_zeroed, 1)
                    nc.gpsimd.tensor_copy(parts[:, s, m, 1], rest[:, m % 2]).then_inc(mid_done, 1)
                    pool.wait_ge(mid_done, i * 8 + (s * 4 + m + 1))
                    nc.gpsimd.tensor_tensor(parts[:, s, m, 2], rest[:, m % 2], parts[:, s, m, 1],
                                            ALU.subtract).then_inc(parts_done, 1)
            paired(pool, NBLK, body)


def phase_rwkv_core(nc, qk_parts, v_pad, decay, faaaa, diag, out_T):
    with Phase(nc, "rwkv") as ph:
        WIDE = S + P
        q6 = ph.sb("q6", [P, 2, H, S], BF16)
        k6 = ph.sb("k6", [P, 2, H, S], BF16)
        v = ph.sb("v", [P, 2, 2, H * 32])
        dg = ph.sb("dg", [P, S])
        dec = ph.sb("dec", [P, H])
        u = ph.sb("u", [P, H])
        neg = ph.sb("neg", [P, H])
        dist = ph.sb("dist", [P, S])
        weight = ph.sb("weight", [P, H, S])
        att = ph.sb("att", [P, 2, 4, WIDE])
        o_sb = ph.sb("o_sb", [P, 2, S])
        t_ps = ph.ps("t_ps", [P, 4, 2 * S])
        o_ps = ph.ps("o_ps", [P, 2, 2 * S])
        consts = ph.sem("consts")
        dist_done = ph.sem("dist_done")
        expdec_done = ph.sem("expdec_done")
        neg_done = ph.sem("neg_done")
        powers_done = ph.sem("powers_done")
        masked = ph.sem("masked")
        weight_done = ph.sem("weight_done")
        loaded = [ph.sem(f"loaded{s}") for s in range(2)]
        batch_done = ph.sem("batch_done")
        t_done = ph.sem("t_done")
        att_done = ph.sem("att_done")
        pv_done = ph.sem("pv_done")
        o_out = ph.sem("o_out")
        stored = [ph.sem(f"stored{s}") for s in range(2)]
        block = ph.block()
        nload = 13
        NCONST = 48

        @block.sync
        def _(sp):
            for s in range(2):
                sp.sem_inc(stored[s], 16)
            sp.dma_start(dec[:], decay.rearrange("h a -> (h a)").partition_broadcast(P)).then_inc(consts, 16)
            sp.dma_start(u[:], faaaa.rearrange("h a -> (h a)").partition_broadcast(P)).then_inc(consts, 16)
            sp.dma_start(dg[:], diag).then_inc(consts, 16)

            def load(tok, half, s):
                for r in range(len(Q_PARTS)):
                    for tile, qk, part in ((q6, 0, Q_PARTS[r]), (k6, 1, K_PARTS[r])):
                        sp.dma_start(tile[r * DH:(r + 1) * DH, s].bitcast(F32),
                                     qk_parts[qk, part, :, half].rearrange("(h d) n -> d h n", d=DH))\
                            .then_inc(loaded[s], 16)
                sp.dma_start(v[:, s], v_pad[tok, :].rearrange("(k p) c -> p k c", p=P))\
                    .then_inc(loaded[s], 16)

            def body(i, s, last):
                if not last:
                    tok = at(sp, i * (2 * S) + (s + 1) * S, S)
                    half = at(sp, i * S + (s + 1) * (S // 2), S // 2)
                    wait_apart(sp, batch_done, i * 2 + (s + 1), consts, NCONST)
                    load(tok, half, 1 - s)
                tok = at(sp, i * (2 * S) + s * S, S)
                for j in range(QUADS):
                    wait_apart(sp, o_out, i * (2 * QUADS) + (s * QUADS + j + 3), consts, NCONST)
                    sp.dma_start(out_T[j, :, tok], o_sb[:, j % 2]).then_inc(stored[j % 2], 16)

            load(slice(0, S), slice(0, S // 2), 0)
            paired(sp, B, body)
            for s in range(2):
                sp.wait_ge(stored[s], B * QUADS // 2 * 16 + 16)

        @block.gpsimd
        def _(pool):
            nc.gpsimd.iota(dist[:], pattern=[[1, S]], base=-1, channel_multiplier=-1,
                           allow_small_or_imprecise_dtypes=True).then_inc(dist_done, 1)
            pool.wait_ge(dist_done, 1)
            nc.gpsimd.tensor_scalar(dist[:], dist[:], 0.0, None, ALU.max).then_inc(dist_done, 1)
            pool.wait_ge(powers_done, 1)
            nc.gpsimd.affine_select(out=weight[:], in_=weight[:], pattern=[[0, H], [1, S]],
                                    compare_op=ALU.is_ge, fill=0.0, base=-1, channel_multiplier=-1)\
                .then_inc(masked, 1)

        @block.tensor
        def _(pe):
            pe.sem_inc(pv_done, 2)
            pe.sem_inc(batch_done, 1)

            def scores(s, h):
                for kt in range(2):
                    mm = nc.tensor.matmul(t_ps[:, h % 4, (0, S)[kt]:(S, WIDE)[kt]],
                                          k6[0:ROWS, s, h, kt * P:(kt + 1) * P], q6[0:ROWS, s, h, kt * P:S],
                                          start=True, stop=True)
                mm.then_inc(t_done, 1)

            def values(s, j):
                for kt in range(2):
                    for c in range(4):
                        h = 4 * j + c
                        mm = nc.tensor.matmul(o_ps[32 * c:32 * c + 32, j % 2, kt * P:S],
                                              v[:, s, kt, h * 32:(h + 1) * 32],
                                              att[:, j % 2, c, (0, S)[kt]:(S, WIDE)[kt]],
                                              start=(kt == 0), stop=(kt == 1), tile_position=(0, 32 * c))
                mm.then_inc(pv_done, 1)

            def body(i, s, last):
                pe.wait_ge(loaded[s], i * (16 * nload) + 16 * nload)
                for j in range(QUADS + 1):
                    n = i * (2 * QUADS) + (s * QUADS + j)
                    if j < QUADS:
                        for c in range(4):
                            pe.wait_ge(att_done, n * 4 + (c + 1))
                            scores(s, 4 * j + c)
                    if j:
                        pe.wait_ge(att_done, n * 4 + 4)
                        pe.wait_ge(o_out, n)
                        values(s, j - 1)
                pe.drain().then_inc(batch_done, 1)
            paired(pe, B, body)

        @block.vector
        def _(dve):
            dve.sem_inc(att_done, 4)
            dve.wait_ge(expdec_done, 1)
            nc.vector.tensor_scalar(neg[:], neg[:], -1.0, None, ALU.mult).then_inc(neg_done, 1)
            dve.wait_ge(masked, 1)
            for h in range(H):
                op = nc.vector.scalar_tensor_tensor(weight[:, h], dg[:], u[:, h:h + 1], weight[:, h],
                                                    ALU.mult, ALU.add)
            op.then_inc(weight_done, 1)
            dve.wait_ge(weight_done, 1)

            def body(i, s, last):
                for h in range(H):
                    dve.wait_ge(t_done, i * (2 * H) + (s * H + h + 1))
                    dve.wait_ge(pv_done, i * (2 * QUADS) + (s * QUADS + h // 4 + 1))
                    nc.vector.tensor_tensor(att[:, (h // 4) % 2, h % 4, 0:S], t_ps[:, h % 4, 0:S],
                                            weight[:, h], ALU.mult)
                    nc.vector.tensor_tensor(att[:, (h // 4) % 2, h % 4, S:WIDE], t_ps[:, h % 4, S:WIDE],
                                            weight[:, h, 0:P], ALU.mult).then_inc(att_done, 1)
            paired(dve, B, body)

        @block.scalar
        def _(act):
            act.sem_inc(o_out, 2)
            act.wait_ge(consts, NCONST)
            nc.scalar.activation(neg[:], dec[:], ACT.Exp).then_inc(expdec_done, 1)
            act.wait_ge(neg_done, 1)
            act.wait_ge(dist_done, 2)
            for h in range(H):
                op = nc.scalar.activation(weight[:, h], dist[:], ACT.Exp, scale=neg[:, h:h + 1])
            op.then_inc(powers_done, 1)

            def body(i, s, last):
                for j in range(QUADS):
                    act.wait_ge(stored[j % 2], i * (QUADS * 16) + (s * QUADS // 2 + j // 2) * 16 + 16)
                    act.wait_ge(pv_done, i * (2 * QUADS) + (s * QUADS + j + 3))
                    nc.scalar.activation(o_sb[:, j % 2], o_ps[:, j % 2, 0:S], ACT.Copy).then_inc(o_out, 1)
            paired(act, B, body)


def phase_group_norm(nc, y_T, identity, ln_w, ln_b, gate, ident, z_T):
    with Phase(nc, "gn") as ph:
        w = ph.sb("w", [P, QUADS, D])
        idt = ph.sb("idt", [P, P])
        lw = ph.sb("lw", [P, D])
        lb = ph.sb("lb", [P, D])
        power = ph.sb("power", [P, TPB * H])
        yT = ph.sb("yT", [P, 2, QUADS, BLK])
        g = ph.sb("g", [P, 2, TPB, D])
        yc = ph.sb("yc", [P, TPB, D])
        sq = ph.sb("sq", [P, TPB, D])
        sums = ph.sb("sums", [P, TPB * H])
        mean = ph.sb("mean", [P, TPB * H])
        sqs = ph.sb("sqs", [P, TPB * H])
        var = ph.sb("var", [P, TPB * H])
        rstd = ph.sb("rstd", [P, TPB * H])
        z = ph.sb("z", [P, TPB, D])
        zT = ph.sb("zT", [P, 2, KD, BLK])
        y_ps = ph.ps("y_ps", [P, 2, TPB, D])
        zT_ps = ph.ps("zT_ps", [P, KD, BLK])
        consts = ph.sem("consts")
        NCONST = 16 * 7
        zeroed = ph.sem("zeroed")
        power_set = ph.sem("power_set")
        loaded = [ph.sem(f"loaded{s}") for s in range(2)]
        y_done = ph.sem("y_done")
        step = ph.sem("step")
        centred = ph.sem("centred")
        squared = ph.sem("squared")
        sqs_done = ph.sem("sqs_done")
        var_done = ph.sem("var_done")
        rstd_done = ph.sem("rstd_done")
        in_free = ph.sem("in_free")
        zT_done = ph.sem("zT_done")
        zT_out = ph.sem("zT_out")
        stored = [ph.sem(f"stored{s}") for s in range(2)]
        block = ph.block()

        @block.sync
        def _(sp):
            for s in range(2):
                sp.sem_inc(stored[s], 16)
            sp.dma_start(idt[:], ident).then_inc(consts, 16)
            sp.dma_start(lw[:], ln_w.partition_broadcast(P)).then_inc(consts, 16)
            sp.dma_start(lb[:], ln_b.partition_broadcast(P)).then_inc(consts, 16)
            sp.wait_ge(zeroed, 1)
            rows = identity.rearrange("(g c d) n -> c d g n", c=4, d=DH)
            for c in range(4):
                sp.dma_start(w[32 * c:32 * c + DH], rows[c]).then_inc(consts, 16)

            def load(i, s):
                tok = at(sp, i * (2 * BLK) + s * BLK, BLK)
                wait_apart(sp, in_free, i * 2 + (s + 1), consts, NCONST)
                sp.dma_start(yT[:, s], y_T[:, :, tok].rearrange("g p n -> p g n")).then_inc(loaded[s], 16)
                sp.dma_start(g[:, s], gate[tok, :].rearrange("(t p) c -> p t c", p=P)).then_inc(loaded[s], 16)

            def body(i, s, last):
                if not last:
                    load(i + s, 1 - s)
                tok = at(sp, i * (2 * BLK) + s * BLK, BLK)
                wait_apart(sp, zT_out, i * 2 + (s + 2), consts, NCONST)
                sp.dma_start(z_T[:, :, tok].rearrange("k p n -> p k n"), zT[:, s]).then_inc(stored[s], 16)
            load(0, 0)
            paired(sp, NBLK, body)
            for s in range(2):
                sp.wait_ge(stored[s], NBLK // 2 * 16 + 16)

        @block.tensor
        def _(pe):
            pe.wait_ge(consts, NCONST)
            pe.wait_ge(zeroed, 1)

            def turn(i, s):
                pe.wait_ge(loaded[s], i * 32 + 32)
                for t in range(TPB):
                    for c in range(QUADS):
                        mm = nc.tensor.matmul(y_ps[:, s, t], yT[:, s, c, t * P:(t + 1) * P], w[:, c],
                                              start=(c == 0), stop=(c == QUADS - 1))
                mm.then_inc(y_done, 1)

            def body(i, s, last):
                if not last:
                    turn(i + s, 1 - s)
                pe.wait_ge(in_free, i * 2 + (s + 3))
                pe.wait_ge(zT_out, i * 2 + (s + 1))
                for t in range(TPB):
                    for k in range(KD):
                        mm = nc.tensor.transpose(zT_ps[:, k, t * P:(t + 1) * P], z[:, t, k * P:(k + 1) * P],
                                                 idt[:])
                mm.then_inc(zT_done, 1)
            turn(0, 0)
            paired(pe, NBLK, body)

        def heads(ap):
            return ap.rearrange("p t (h c) -> p (t h) c", c=DH)

        def spread(ap):
            return ap.unsqueeze(2).broadcast_to([P, TPB * H, DH])

        @block.vector
        def _(dve):
            dve.sem_inc(in_free, 2)
            dve.wait_ge(consts, NCONST)
            STEPS = 5

            def body(i, s, last):
                n = i * 2 + (s + 1)
                done = 0

                def link(op):
                    nonlocal done
                    done += 1
                    op.then_inc(step, 1)
                    dve.wait_ge(step, (n - 1) * STEPS + done)
                dve.wait_ge(y_done, n)
                link(nc.vector.tensor_reduce(sums[:], heads(y_ps[:, s]), axis=AX.X, op=ALU.add))
                link(nc.vector.tensor_scalar(mean[:], sums[:], 1.0 / DH, None, ALU.mult))
                nc.vector.tensor_tensor(heads(yc[:]), heads(y_ps[:, s]), spread(mean[:]), ALU.subtract)\
                    .then_inc(centred, 1)
                dve.wait_ge(squared, n)
                nc.vector.tensor_reduce(sqs[:], heads(sq[:]), axis=AX.X, op=ALU.add).then_inc(sqs_done, 1)
                dve.wait_ge(centred, n)
                dve.wait_ge(rstd_done, n)
                link(nc.vector.tensor_tensor(heads(yc[:]), heads(yc[:]), spread(rstd[:]), ALU.mult))
                link(nc.vector.tensor_tensor(yc[:], yc[:], lw[:].unsqueeze(1).broadcast_to([P, TPB, D]), ALU.mult))
                link(nc.vector.tensor_tensor(yc[:], yc[:], lb[:].unsqueeze(1).broadcast_to([P, TPB, D]), ALU.add))
                dve.wait_ge(zT_out, n)
                dve.wait_ge(loaded[s], i * 32 + 32)
                nc.vector.tensor_tensor(z[:], yc[:], g[:, s], ALU.mult).then_inc(in_free, 1)
            paired(dve, NBLK, body)

        @block.gpsimd
        def _(pool):
            nc.gpsimd.memset(w[:], 0.0).then_inc(zeroed, 1)
            nc.gpsimd.memset(power[:], -0.5).then_inc(power_set, 1)

            def body(i, s, last):
                wait_apart(pool, sqs_done, i * 2 + (s + 1), power_set, 1)
                nc.gpsimd.tensor_scalar(var[:], sqs[:], 1.0 / DH, GN_EPS, ALU.mult, ALU.add).then_inc(var_done, 1)
                pool.wait_ge(var_done, i * 2 + (s + 1))
                nc.gpsimd.tensor_tensor(rstd[:], var[:], power[:], ALU.pow).then_inc(rstd_done, 1)
            paired(pool, NBLK, body)

        @block.scalar
        def _(act):
            act.sem_inc(zT_out, 1)

            def body(i, s, last):
                act.wait_ge(centred, i * 2 + (s + 1))
                nc.scalar.activation(sq[:], yc[:], ACT.Square).then_inc(squared, 1)
                act.wait_ge(stored[s], i * 16 + 16)
                act.wait_ge(zT_done, i * 2 + (s + 1))
                for k in range(KD):
                    op = nc.scalar.activation(zT[:, s, k], zT_ps[:, k], ACT.Copy)
                op.then_inc(zT_out, 1)
            paired(act, NBLK, body)


def phase_split(nc, qT, kT, v_in, qk_parts, v_pad):
    with Phase(nc, "split") as ph:
        x = ph.sb("x", [P, 2, 2 * KD, BLK])
        parts = ph.sb("parts", [P, 2, 3, 2 * KD, BLK], BF16)
        rest = ph.sb("rest", [P, 2 * KD, BLK])
        vin = ph.sb("vin", [P, 2, TPB, D])
        vp = ph.sb("vp", [P, 2, TPB, H, 32])
        zeroed = ph.sem("zeroed")
        x_loaded = [ph.sem(f"x_loaded{s}") for s in range(2)]
        hi_done = ph.sem("hi_done")
        rest_done = ph.sem("rest_done")
        mid_done = ph.sem("mid_done")
        parts_done = ph.sem("parts_done")
        v_out = ph.sem("v_out")
        stored = [ph.sem(f"stored{s}") for s in range(2)]
        block = ph.block()

        @block.sync
        def _(sp):
            for s in range(2):
                sp.sem_inc(stored[s], 16)
            def load(i, s):
                tok = at(sp, i * (2 * BLK) + s * BLK, BLK)
                wait_apart(sp, parts_done, i * 2 + (s + 1), zeroed, 1)
                wait_apart(sp, v_out, i * 2 + (s + 1), zeroed, 1)
                for j, src in ((0, qT), (KD, kT)):
                    sp.dma_start(x[:, s, j:j + KD], src[:, tok].rearrange("(k p) n -> p k n", p=P))\
                        .then_inc(x_loaded[s], 16)
                sp.dma_start(vin[:, s], v_in[tok, :].rearrange("(t p) c -> p t c", p=P))\
                    .then_inc(x_loaded[s], 16)

            def body(i, s, last):
                if not last:
                    load(i + s, 1 - s)
                tok = at(sp, i * (2 * BLK) + s * BLK, BLK)
                half = at(sp, i * BLK + s * (BLK // 2), BLK // 2)
                wait_apart(sp, parts_done, i * 2 + (s + 3), zeroed, 1)
                for j in range(2):
                    for a in range(3):
                        sp.dma_start(qk_parts[j, a, :, half].rearrange("(k p) n -> p k n", p=P),
                                     parts[:, s, a, j * KD:(j + 1) * KD].bitcast(F32)).then_inc(stored[s], 16)
                wait_apart(sp, v_out, i * 2 + (s + 3), zeroed, 1)
                sp.dma_start(v_pad[tok, :].rearrange("(t p) c -> p t c", p=P),
                             vp[:, s].rearrange("p t h c -> p t (h c)")).then_inc(stored[s], 16)
            load(0, 0)
            paired(sp, NBLK, body)
            for s in range(2):
                sp.wait_ge(stored[s], NBLK // 2 * 7 * 16 + 16)

        @block.scalar
        def _(act):
            def body(i, s, last):
                act.wait_ge(stored[s], i * (7 * 16) + 16)
                act.wait_ge(x_loaded[s], i * 48 + 48)
                nc.scalar.activation(parts[:, s, 0], x[:, s], ACT.Copy).then_inc(hi_done, 1)
            paired(act, NBLK, body)

        @block.vector
        def _(dve):
            dve.sem_inc(v_out, 2)
            dve.wait_ge(zeroed, 1)

            def body(i, s, last):
                dve.wait_ge(hi_done, i * 2 + (s + 1))
                dve.wait_ge(x_loaded[s], i * 48 + 48)
                dve.wait_ge(parts_done, i * 2 + (s + 2))
                nc.vector.tensor_tensor(rest[:], x[:, s], parts[:, s, 0], ALU.subtract)\
                    .then_inc(rest_done, 1)
                dve.wait_ge(stored[s], i * (7 * 16) + 16)
                nc.vector.tensor_copy(vp[:, s, :, :, 0:DH],
                                      vin[:, s].rearrange("p t (h c) -> p t h c", c=DH))\
                    .then_inc(v_out, 1)
            paired(dve, NBLK, body)

        @block.gpsimd
        def _(pool):
            nc.gpsimd.memset(vp[:], 0.0).then_inc(zeroed, 1)
            pool.sem_inc(parts_done, 2)

            def body(i, s, last):
                wait_apart(pool, rest_done, i * 2 + (s + 1), zeroed, 1)
                nc.gpsimd.tensor_copy(parts[:, s, 1], rest[:]).then_inc(mid_done, 1)
                pool.wait_ge(mid_done, i * 2 + (s + 1))
                nc.gpsimd.tensor_tensor(parts[:, s, 2], rest[:], parts[:, s, 1],
                                        ALU.subtract).then_inc(parts_done, 1)
            paired(pool, NBLK, body)


def phase_moe(nc, x_in, xT, router_T, w1_T, w2_T, r_out):
    with Phase(nc, "moe") as ph:
        NF = FFN // P
        w1 = ph.sb("w1", [P, NE, KD, FFN])
        w2 = ph.sb("w2", [P, NE, NF, D])
        rw = ph.sb("rw", [P, KD, NE])
        iota = ph.sb("iota", [P, NE])
        xt = ph.sb("xt", [P, KD, BLK])
        x = ph.sb("x", [P, TPB, D])
        h = ph.sb("h", [P, 2, BLK])
        acc = ph.sb("acc", [P, TPB, D])
        scores = ph.sb("scores", [P, TPB, NE])
        top = ph.sb("top", [P, TPB, 8])
        top_i = ph.sb("top_i", [P, TPB, 8], U32)
        best = ph.sb("best", [P, TPB, 8])
        gap = ph.sb("gap", [P, TPB])
        odds = ph.sb("odds", [P, TPB])
        one_more = ph.sb("one_more", [P, TPB])
        share = ph.sb("share", [P, 2, TPB])
        we = ph.sb("we", [P, 2, TPB, NE])
        h_ps = ph.ps("h_ps", [P, 2, BLK])
        y_ps = ph.ps("y_ps", [P, 2, TPB, D])
        sc_ps = ph.ps("sc_ps", [P, TPB, P])
        consts = ph.sem("consts")
        w1_loaded = [ph.sem(f"w1_loaded{e}") for e in range(NE)]
        w2_loaded = [ph.sem(f"w2_loaded{e}") for e in range(NE)]
        iota_set = ph.sem("iota_set")
        xt_loaded = ph.sem("xt_loaded")
        x_loaded = ph.sem("x_loaded")
        xt_free = ph.sem("xt_free")
        x_free = ph.sem("x_free")
        sc_done = ph.sem("sc_done")
        sc_out = ph.sem("sc_out")
        route = ph.sem("route")
        gap_done = ph.sem("gap_done")
        odds_done = ph.sem("odds_done")
        h_done = ph.sem("h_done")
        h_out = ph.sem("h_out")
        h_used = ph.sem("h_used")
        y_done = ph.sem("y_done")
        y_out = ph.sem("y_out")
        stored = ph.sem("stored")
        block = ph.block()
        NH = NE * NF

        @block.sync
        def _(sp):
            sp.sem_inc(stored, 16)
            sp.dma_start(rw[:], router_T.rearrange("(k p) e -> p k e", p=P)).then_inc(consts, 16)

            def load(i):
                tok = at(sp, i * BLK, BLK)
                wait_apart(sp, xt_free, i, consts, 16)
                sp.dma_start(xt[:], xT[:, tok].rearrange("(k p) n -> p k n", p=P)).then_inc(xt_loaded, 16)
                wait_apart(sp, x_free, i, consts, 16)
                sp.dma_start(x[:], x_in[tok, :].rearrange("(t p) c -> p t c", p=P)).then_inc(x_loaded, 16)

            load(0)
            for e in range(NE):
                sp.dma_start(w1[:, e], w1_T[e].rearrange("(k p) f -> p k f", p=P)).then_inc(w1_loaded[e], 16)
                sp.dma_start(w2[:, e], w2_T[e].rearrange("(f p) c -> p f c", p=P)).then_inc(w2_loaded[e], 16)

            def body(i, last):
                if not last:
                    load(i + 1)
                tok = at(sp, i * BLK, BLK)
                wait_apart(sp, y_out, i * NE + (NE + 2), consts, 16)
                sp.dma_start(r_out[tok, :].rearrange("(t p) c -> p t c", p=P), acc[:]).then_inc(stored, 16)
            with sp.Fori(0, NBLK - 1) as i:
                body(i, False)
            body(NBLK - 1, True)
            sp.wait_ge(stored, NBLK * 16 + 16)

        @block.tensor
        def _(pe):
            def first(i, e, f):
                pe.wait_ge(h_out, i * NH + (e * NF + f + 1))
                for k in range(KD):
                    mm = nc.tensor.matmul(h_ps[:, f % 2], w1[:, e, k, f * P:(f + 1) * P], xt[:, k],
                                          start=(k == 0), stop=(k == KD - 1))
                mm.then_inc(h_done, 1)

            def second(i, e, f):
                pe.wait_ge(h_out, i * NH + (e * NF + f + 3))
                if f == 0:
                    pe.wait_ge(y_out, i * NE + (e + 1))
                for t in range(TPB):
                    mm = nc.tensor.matmul(y_ps[:, e % 2, t], h[:, f % 2, t * P:(t + 1) * P], w2[:, e, f],
                                          start=(f == 0 and t % 2 == 0), stop=(f == NF - 1),
                                          skip_group_check=True)
                mm.then_inc(h_used, 1)
                if f == NF - 1:
                    pe.drain().then_inc(y_done, 1)

            with pe.Fori(0, NBLK) as i:
                pe.wait_ge(consts, 16)
                pe.wait_ge(xt_loaded, i * 16 + 16)
                pe.wait_ge(sc_out, i + 1)
                for t in range(TPB):
                    for k in range(KD):
                        mm = nc.tensor.matmul(sc_ps[:, t, 0:NE], xt[:, k, t * P:(t + 1) * P], rw[:, k],
                                              start=(k == 0), stop=(k == KD - 1))
                mm.then_inc(sc_done, 1)
                pe.wait_ge(w1_loaded[0], 16)
                first(i, 0, 0)
                for e in range(NE):
                    pe.wait_ge(w2_loaded[e], 16)
                    for f in range(NF):
                        if f + 1 < NF:
                            first(i, e, f + 1)
                        elif e + 1 < NE:
                            pe.wait_ge(w1_loaded[e + 1], 16)
                            first(i, e + 1, 0)
                        if e == NE - 1 and f == NF - 2:
                            pe.drain().then_inc(xt_free, 1)
                        second(i, e, f)

        @block.scalar
        def _(act):
            act.sem_inc(h_out, 2)

            with act.Fori(0, NBLK) as i:
                act.wait_ge(gap_done, i + 1)
                nc.scalar.activation(odds[:], gap[:], ACT.Exp).then_inc(odds_done, 1)
                for g in range(NH):
                    act.wait_ge(h_done, i * NH + (g + 1))
                    act.wait_ge(h_used, i * NH + (g + 1))
                    nc.scalar.activation(h[:, g % 2], h_ps[:, g % 2], ACT.Gelu).then_inc(h_out, 1)

        @block.gpsimd
        def _(pool):
            nc.gpsimd.iota(iota[:], pattern=[[1, NE]], base=0, channel_multiplier=0,
                           allow_small_or_imprecise_dtypes=True).then_inc(iota_set, 1)

        @block.vector
        def _(dve):
            dve.sem_inc(y_out, 2)
            dve.sem_inc(h_used, 2)
            dve.sem_inc(sc_out, 1)
            dve.wait_ge(iota_set, 1)
            STEPS = 8

            with dve.Fori(0, NBLK) as i:
                done = 0

                def link(op):
                    nonlocal done
                    done += 1
                    op.then_inc(route, 1)
                    wait_apart(dve, route, i * STEPS + done, iota_set, 1)
                dve.wait_ge(sc_done, i + 1)
                link(nc.vector.tensor_copy(scores[:], sc_ps[:, :, 0:NE]))
                dve.sem_inc(sc_out, 1)
                for t in range(TPB):
                    op = nc.vector.max(out=top[:, t], in_=scores[:, t])
                link(op)
                for t in range(TPB):
                    op = nc.vector.max_index(out=top_i[:, t], in_max=top[:, t], in_values=scores[:, t])
                nc.vector.tensor_tensor(gap[:], top[:, :, 1], top[:, :, 0], ALU.subtract)\
                    .then_inc(gap_done, 1)
                wait_apart(dve, gap_done, i + 1, iota_set, 1)
                link(nc.vector.tensor_copy(best[:], top_i[:]))
                dve.wait_ge(odds_done, i + 1)
                link(nc.vector.tensor_scalar(one_more[:], odds[:], 1.0, None, ALU.add))
                link(nc.vector.reciprocal(share[:, 0], one_more[:]))
                link(nc.vector.tensor_tensor(share[:, 1], share[:, 0], odds[:], ALU.mult))
                for r in range(2):
                    for t in range(TPB):
                        op = nc.vector.tensor_scalar(we[:, r, t], iota[:], best[:, t, r:r + 1],
                                                     share[:, r, t:t + 1], ALU.is_equal, ALU.mult)
                link(op)
                link(nc.vector.tensor_tensor(we[:, 0], we[:, 0], we[:, 1], ALU.add))
                for e in range(NE):
                    dve.wait_ge(y_done, i * NE + (e + 1))
                    if e == 0:
                        dve.wait_ge(x_loaded, i * 16 + 16)
                        dve.wait_ge(stored, i * 16 + 16)
                    dve.wait_ge(y_out, i * NE + (e + 2))
                    for t in range(TPB):
                        op = nc.vector.scalar_tensor_tensor(acc[:, t], y_ps[:, e % 2, t], we[:, 0, t, e:e + 1],
                                                            (x if e == 0 else acc)[:, t], ALU.mult, ALU.add)
                    op.then_inc(y_out, 1)
                    if e == 0:
                        dve.wait_ge(y_out, i * NE + 3)
                        dve.sem_inc(x_free, 1)


def phase_experts(nc, x_in, xT, gate_w, gate_b, expert_w, expert_b, ident, r_out):
    with Phase(nc, "ffn") as ph:
        EP = NE // 2
        w = ph.sb("w", [P, KD, EP, 2, D])
        eb = ph.sb("eb", [NE, D])
        gw = ph.sb("gw", [P, KD, NE])
        gb = ph.sb("gb", [P, NE])
        idt = ph.sb("idt", [P, P])
        xt = ph.sb("xt", [P, 2, KD, BLK])
        x = ph.sb("x", [P, 2, TPB, D])
        lg = ph.sb("lg", [P, TPB, NE])
        mx = ph.sb("mx", [P, TPB])
        ex = ph.sb("ex", [P, TPB, NE])
        sm = ph.sb("sm", [P, TPB])
        rs = ph.sb("rs", [P, TPB])
        gate = ph.sb("gate", [P, TPB, NE])
        sel = ph.sb("sel", [P, TPB, NE])
        nil = ph.sb("nil", [P, TPB])
        we = ph.sb("we", [P, 2, TPB, NE])
        weT = ph.sb("weT", [NE, TPB, P])
        acc = ph.sb("acc", [P, 2, TPB, D])
        y_ps = ph.ps("y_ps", [P, 4, 2, D])
        b_ps = ph.ps("b_ps", [P, TPB, D])
        lg_ps = ph.ps("lg_ps", [P, TPB, P])
        wT_ps = ph.ps("wT_ps", [P, TPB, P])
        consts = ph.sem("consts")
        NCONST = 16 * (4 + NE)
        loaded = [ph.sem(f"loaded{s}") for s in range(2)]
        in_free = ph.sem("in_free")
        lg_done = ph.sem("lg_done")
        step = ph.sem("step")
        shift_done = ph.sem("shift_done")
        exp_done = ph.sem("exp_done")
        we_done = ph.sem("we_done")
        wT_done = ph.sem("wT_done")
        wT_out = ph.sem("wT_out")
        b_done = ph.sem("b_done")
        b_out = ph.sem("b_out")
        y_done = ph.sem("y_done")
        half_done = ph.sem("half_done")
        y_out = ph.sem("y_out")
        stored = [ph.sem(f"stored{s}") for s in range(2)]
        block = ph.block()
        NY = TPB * EP

        @block.sync
        def _(sp):
            for s in range(2):
                sp.sem_inc(stored[s], 16)
            sp.dma_start(eb[:], expert_b).then_inc(consts, 16)
            sp.dma_start(gw[:], gate_w.rearrange("(k p) e -> p k e", p=P)).then_inc(consts, 16)
            sp.dma_start(gb[:], gate_b.partition_broadcast(P)).then_inc(consts, 16)
            sp.dma_start(idt[:], ident).then_inc(consts, 16)
            for e in range(NE):
                sp.dma_start(w[:, :, e // 2, e % 2], expert_w[e].rearrange("(k p) c -> p k c", p=P))\
                    .then_inc(consts, 16)

            def load(i, s):
                tok = at(sp, i * (2 * BLK) + s * BLK, BLK)
                wait_apart(sp, in_free, i * 2 + (s + 1), consts, NCONST)
                sp.dma_start(xt[:, s], xT[:, tok].rearrange("(k p) n -> p k n", p=P)).then_inc(loaded[s], 16)
                sp.dma_start(x[:, s], x_in[tok, :].rearrange("(t p) c -> p t c", p=P)).then_inc(loaded[s], 16)

            def body(i, s, last):
                if not last:
                    load(i + s, 1 - s)
                tok = at(sp, i * (2 * BLK) + s * BLK, BLK)
                wait_apart(sp, y_out, i * (2 * NY) + (s * NY + NY + 4), consts, NCONST)
                sp.dma_start(r_out[tok, :].rearrange("(t p) c -> p t c", p=P), acc[:, s]).then_inc(stored[s], 16)
            load(0, 0)
            paired(sp, NBLK, body)
            for s in range(2):
                sp.wait_ge(stored[s], NBLK // 2 * 16 + 16)

        @block.tensor
        def _(pe):
            pe.wait_ge(consts, NCONST)

            def logits(i, s):
                pe.wait_ge(loaded[s], i * 32 + 32)
                for t in range(TPB):
                    for k in range(KD):
                        mm = nc.tensor.matmul(lg_ps[:, t, 0:NE], xt[:, s, k, t * P:(t + 1) * P], gw[:, k],
                                              start=(k == 0), stop=(k == KD - 1))
                mm.then_inc(lg_done, 1)

            def product(i, s, m):
                pe.wait_ge(y_out, i * (2 * NY) + (s * NY + m + 1))
                g, t = divmod(m, TPB)
                for k in range(KD):
                    mm = nc.tensor.matmul(y_ps[:, m % 4], xt[:, s, k, t * P:(t + 1) * P], w[:, k, g],
                                          start=(k == 0), stop=(k == KD - 1))
                mm.then_inc(y_done, 1)

            def body(i, s, last):
                for m in range(NY):
                    product(i, s, m)
                    if m == 1:
                        pe.wait_ge(we_done, i * 2 + (s + 1))
                        for t in range(TPB):
                            mm = nc.tensor.transpose(wT_ps[0:NE, t], we[:, s, t], idt[:])
                        mm.then_inc(wT_done, 1)
                    if m == 3:
                        pe.wait_ge(wT_out, i * 2 + (s + 1))
                        pe.wait_ge(b_out, i * 2 + (s + 1))
                        for t in range(TPB):
                            mm = nc.tensor.matmul(b_ps[:, t], weT[:, t], eb[:], start=True, stop=True)
                        mm.then_inc(b_done, 1)
                    if m == NY // 2 and not last:
                        logits(i + s, 1 - s)
                pe.drain().then_inc(in_free, 1)
            logits(0, 0)
            paired(pe, NBLK, body)

        @block.scalar
        def _(act):
            def body(i, s, last):
                act.wait_ge(shift_done, i * 2 + (s + 1))
                nc.scalar.activation(ex[:], lg[:], ACT.Exp).then_inc(exp_done, 1)
                act.wait_ge(wT_done, i * 2 + (s + 1))
                act.wait_ge(b_done, i * 2 + (s + 1))
                nc.scalar.activation(weT[:], wT_ps[0:NE], ACT.Copy).then_inc(wT_out, 1)
            paired(act, NBLK, body)

        def each(ap):
            return ap.unsqueeze(2).broadcast_to([P, TPB, NE])

        @block.vector
        def _(dve):
            dve.sem_inc(in_free, 2)
            dve.sem_inc(y_out, 4)
            dve.sem_inc(b_out, 1)
            dve.sem_inc(b_done, 1)
            dve.wait_ge(consts, NCONST)
            STEPS = 11

            def gates(i, s):
                n = i * 2 + s
                done = 0

                def link(op):
                    nonlocal done
                    done += 1
                    op.then_inc(step, 1)
                    dve.wait_ge(step, n * STEPS + done)
                dve.wait_ge(lg_done, n + 1)
                link(nc.vector.tensor_tensor(lg[:], lg_ps[:, :, 0:NE],
                                             gb[:].unsqueeze(1).broadcast_to([P, TPB, NE]), ALU.add))
                link(nc.vector.tensor_reduce(mx[:], lg[:], axis=AX.X, op=ALU.max))
                nc.vector.tensor_tensor(lg[:], lg[:], each(mx[:]), ALU.subtract).then_inc(shift_done, 1)
                dve.wait_ge(exp_done, n + 1)
                link(nc.vector.tensor_reduce(sm[:], ex[:], axis=AX.X, op=ALU.add))
                link(nc.vector.reciprocal(rs[:], sm[:]))
                link(nc.vector.tensor_tensor(gate[:], ex[:], each(rs[:]), ALU.mult))
                link(nc.vector.tensor_scalar(sel[:], gate[:], 0.1, None, ALU.is_ge))
                link(nc.vector.tensor_tensor(gate[:], gate[:], sel[:], ALU.mult))
                link(nc.vector.tensor_reduce(sm[:], gate[:], axis=AX.X, op=ALU.add))
                link(nc.vector.tensor_scalar(nil[:], sm[:], 0.0, None, ALU.is_equal))
                link(nc.vector.tensor_tensor(sm[:], sm[:], nil[:], ALU.add))
                link(nc.vector.reciprocal(rs[:], sm[:]))
                nc.vector.tensor_tensor(we[:, s], gate[:], each(rs[:]), ALU.mult).then_inc(we_done, 1)

            def body(i, s, last):
                n = i * 2 + s
                dve.wait_ge(loaded[s], i * 32 + 32)
                dve.wait_ge(stored[s], i * 16 + 16)
                dve.wait_ge(b_done, n + 2)
                nc.vector.tensor_tensor(acc[:, s], b_ps[:], x[:, s], ALU.add).then_inc(b_out, 1)
                dve.wait_ge(b_out, n + 2)
                for m in range(0, NY, 2):
                    g, t = divmod(m, TPB)
                    if g:
                        dve.wait_ge(y_out, i * (2 * NY) + (s * NY + m + 2))
                    for e in range(2):
                        for d in range(2):
                            if e == 0:
                                dve.wait_ge(y_done, i * (2 * NY) + (s * NY + m + d + 1))
                            else:
                                dve.wait_ge(half_done, i * (2 * NY) + (s * NY + m + d + 1))
                            nc.vector.scalar_tensor_tensor(acc[:, s, t + d], y_ps[:, (m + d) % 4, e],
                                                           we[:, s, t + d, 2 * g + e:2 * g + e + 1],
                                                           acc[:, s, t + d], ALU.mult, ALU.add)\
                                .then_inc(y_out if e else half_done, 1)
                    if m == NY * 5 // 8 and not last:
                        gates(i + s, 1 - s)
            gates(0, 0)
            paired(dve, NBLK, body)


def window_masks():
    p, n = np.arange(P)[:, None], np.arange(P)[None, :]
    masked = np.stack([n > p, n < p, n > p, n < p])
    return np.where(masked, -1e30, 0.0).astype(np.float32)


def bass_decoder_layers(nc, a):
    def scratch(name, *shape):
        return nc.dram_tensor(f"scratch_{name}", list(shape), F32, kind="Internal").ap()

    qk_parts = scratch("qk_parts", 2, 3, D, T // 2)
    v_pad = scratch("v_pad", T, H * 32)
    o_T = scratch("o_T", QUADS, P, T)
    x1, x1T = scratch("x1", T, D), scratch("x1T", D, T)
    x2, x2T = scratch("x2", T, D), scratch("x2T", D, T)
    x3, x3T = scratch("x3", T, D), scratch("x3T", D, T)
    x4, x4T = scratch("x4", T, D), scratch("x4T", D, T)
    x5, x5T = scratch("x5", T, D), scratch("x5T", D, T)
    cross_T = scratch("cross_T", DM // P, P, T)
    sum2, sum5 = scratch("sum2", T, D), scratch("sum5", T, D)
    gate, z_T = scratch("gate", T, D), scratch("z_T", KD, P, T)

    phase_qkv(nc, a["xT"], a["w_qkv"], a["b_qkv"], qk_parts, v_pad)
    phase_core(nc, "self", qk_parts, v_pad, a["ident"], o_T, DH ** -0.5)
    phase_post(nc, "post0", o_T, QUADS, a["w_proj"], True, a["b_proj"], a["x"], a["ident"], x1, x1T)
    phase_cross(nc, x1T, a["ctxT"], a["Wq"], a["bq"], a["Wk"], a["bk"], a["Wv"], a["bv"], a["ident"], cross_T)
    phase_post(nc, "post1", cross_T, DM // P, a["Wu"], False, a["bu"], x1, a["ident"], x2, x2T)
    phase_moe(nc, x2, x2T, a["router_T"], a["w1_T"], a["w2_T"], sum2)
    phase_post(nc, "post2", None, 0, None, False, None, sum2, a["ident"], x3, x3T)
    phase_rwkv_in(nc, x3T, [a["maa_r"], a["maa_k"], a["maa_v"], a["maa_g"]],
                  [a["WrT"], a["WkT"], a["WvT"], a["WgT"]], qk_parts, v_pad, gate)
    phase_rwkv_core(nc, qk_parts, v_pad, a["decay"], a["faaaa"], a["diag"], o_T)
    phase_group_norm(nc, o_T, a["identity"], a["ln_w"], a["ln_b"], gate, a["ident"], z_T)
    phase_post(nc, "post3", z_T, KD, a["WoT"], False, None, x3, a["ident"], x4, x4T)
    phase_split(nc, x4T, a["ctxT"], a["ctx"], qk_parts, v_pad)
    phase_core(nc, "window", qk_parts, v_pad, a["ident"], o_T, 1.0, a["masks"])
    phase_post(nc, "post4", o_T, QUADS, a["identity"], True, None, x4, a["ident"], x5, x5T)
    phase_experts(nc, x5, x5T, a["gate_w"], a["gate_b"], a["expert_w"], a["expert_b"], a["ident"], sum5)
    phase_post(nc, "post5", None, 0, None, False, None, sum5, a["ident"], a["out"], None)


def kernel(**inputs):
    import concourse.bacc as _bacc
    from concourse.bass_utils import run_bass_kernel_spmd as _run

    i = {name: np.asarray(value) for name, value in inputs.items()}
    x, ctx = i["x"].reshape(T, D), i["ctx_1024"].reshape(T, D)
    layout = dict(
        x=x, xT=x.T, ctx=ctx, ctxT=ctx.T,
        w_qkv=i["L0_attn_w_qkv"], b_qkv=i["L0_attn_b_qkv"], w_proj=i["L0_attn_w_proj"], b_proj=i["L0_attn_b_proj"],
        Wq=i["L0_xattn_Wq"], bq=i["L0_xattn_bq"], Wk=i["L0_xattn_Wk"], bk=i["L0_xattn_bk"],
        Wv=i["L0_xattn_Wv"], bv=i["L0_xattn_bv"], Wu=i["L0_xattn_Wu"], bu=i["L0_xattn_bu"],
        router_T=i["L0_ffn_router_w"].T, w1_T=i["L0_ffn_expert_w1"].transpose(0, 2, 1),
        w2_T=i["L0_ffn_expert_w2"].transpose(0, 2, 1),
        maa_r=i["L1_attn_time_maa_r"], maa_k=i["L1_attn_time_maa_k"],
        maa_v=i["L1_attn_time_maa_v"], maa_g=i["L1_attn_time_maa_g"],
        decay=i["L1_attn_time_decay"], faaaa=i["L1_attn_time_faaaa"],
        WrT=i["L1_attn_Wr"].T, WkT=i["L1_attn_Wk"].T, WvT=i["L1_attn_Wv"].T, WgT=i["L1_attn_Wg"].T,
        WoT=i["L1_attn_Wo"].T, ln_w=i["L1_attn_ln_w"], ln_b=i["L1_attn_ln_b"],
        gate_w=i["L1_ffn_gate_w"], gate_b=i["L1_ffn_gate_b"],
        expert_w=i["L1_ffn_expert_w"], expert_b=i["L1_ffn_expert_b"],
        ident=np.eye(P, dtype=np.float32),
        identity=np.eye(D, dtype=np.float32), diag=np.eye(P, S, dtype=np.float32), masks=window_masks(),
    )
    nc = _bacc.Bacc("TRN2", target_bir_lowering=False, num_devices=1)
    arrays, args = {}, {}
    for name, value in layout.items():
        value = np.ascontiguousarray(value)
        arrays[f"in_{name}"] = value
        args[name] = nc.dram_tensor(f"in_{name}", value.shape, mybir.dt.from_np(value.dtype),
                                    kind="ExternalInput").ap()
    args["out"] = nc.dram_tensor("out", (T, D), F32, kind="ExternalOutput").ap()
    bass_decoder_layers(nc, args)
    r = _run(nc, [arrays], core_ids=[0])
    return r.results[0]["out"].reshape(B, S, D)
```

```python
import numpy as np
import concourse.bass as bass
from concourse import mybir
from contextlib import ExitStack

F32 = mybir.dt.float32
BF16 = mybir.dt.bfloat16
U32 = mybir.dt.uint32
I32 = mybir.dt.int32
ALU = mybir.AluOpType
ACT = mybir.ActivationFunctionType
AX = mybir.AxisListType
ds = bass.ds

P = 128
D = 256
KD = D // P
B = 16
S = 256
T = B * S
H = 16
DH = D // H
QUADS = H // 4
BLK = 512
NBLK = T // BLK
TPB = BLK // P
DX = 64
DM = H * DX
NE = 8
FFN = 1024
MOE_TILES = 2 * T // P + NE
ROUTE_STEPS = 33
LN_EPS = 1e-5
GN_EPS = 1e-5 * 64

Q_PARTS = (0, 0, 0, 1, 1, 2)
K_PARTS = (0, 1, 2, 0, 1, 0)
ROWS = len(Q_PARTS) * DH
MAX_ROWS = 2


class Phase:

    def __init__(self, nc, name):
        self.nc, self.name, self.stack, self.sems = nc, name, ExitStack(), []

    def __enter__(self):
        self.stack.__enter__()
        return self

    def __exit__(self, *a):
        done = self.stack.__exit__(*a)
        self.nc.clear_and_free_semaphores(self.sems)
        self.nc.all_engine_barrier()
        return done

    def sb(self, name, shape, dt=F32):
        return self.stack.enter_context(self.nc.sbuf_tensor(f"{self.name}_{name}", shape, dt))

    def ps(self, name, shape, dt=F32):
        return self.stack.enter_context(self.nc.psum_tensor(f"{self.name}_{name}", shape, dt))

    def sem(self, name):
        self.sems.append(self.nc.alloc_semaphore(name=f"{self.name}_{name}"))
        return self.sems[-1]

    def block(self):
        return self.stack.enter_context(self.nc.Block())


def paired(eng, count, body):
    with eng.Fori(0, count // 2 - 1) as i:
        body(i, 0, False)
        body(i, 1, False)
    body(count // 2 - 1, 0, False)
    body(count // 2 - 1, 1, True)


def paired_first(eng, count, body):
    body(0, 0, True, False)
    body(0, 1, False, False)
    with eng.Fori(1, count // 2 - 1) as i:
        body(i, 0, False, False)
        body(i, 1, False, False)
    body(count // 2 - 1, 0, False, False)
    body(count // 2 - 1, 1, False, True)


def load_all(sp, load):
    load(0, 1)
    with sp.Fori(1, NBLK // 2) as i:
        load(i, 0)
        load(i, 1)


def at(eng, start, size):
    return slice(start, start + size) if isinstance(start, int) else ds(eng.snap(start), size)


def wait_apart(eng, sem, value, met, met_value):
    if not isinstance(value, int):
        value = eng.to_reg(value)
        eng.wait_ge(met, met_value)
    eng.wait_ge(sem, value)


def phase_qkv(nc, xT, w_qkv, b_qkv, qk_parts, v_pad):
    with Phase(nc, "qkv") as ph:
        w = ph.sb("w", [P, KD, 3 * D])
        bqk = ph.sb("bqk", [P, 4])
        bv = ph.sb("bv", [P, 2, D])
        x = ph.sb("x", [P, 2, KD, BLK])
        parts = ph.sb("parts", [P, 2, 4, 3, BLK], BF16)
        rest = ph.sb("rest", [P, 2, BLK])
        vp = ph.sb("vp", [P, 2, TPB, H, 32])
        qk_ps = ph.ps("qk_ps", [P, 4, BLK])
        v_ps = ph.ps("v_ps", [P, TPB, D])
        consts = ph.sem("consts")
        x_loaded = [ph.sem(f"x_loaded{s}") for s in range(2)]
        x_free = ph.sem("x_free")
        qk_done = ph.sem("qk_done")
        hi_done = ph.sem("hi_done")
        rest_done = ph.sem("rest_done")
        mid_done = ph.sem("mid_done")
        parts_done = ph.sem("parts_done")
        v_filled = ph.sem("v_filled")
        v_done = ph.sem("v_done")
        v_out = ph.sem("v_out")
        stored = [ph.sem(f"stored{s}") for s in range(2)]
        block = ph.block()

        @block.sync
        def _(sp):
            for s in range(2):
                sp.sem_inc(stored[s], 16)
            def load(i, s):
                tok = at(sp, i * (2 * BLK) + s * BLK, BLK)
                wait_apart(sp, x_free, i * 2 + (s + 1), consts, 64)
                sp.dma_start(x[:, s], xT[:, tok]
                             .rearrange("(k p) n -> p k n", p=P)).then_inc(x_loaded[s], 16)
            load(0, 0)
            sp.dma_start(w[:], w_qkv.rearrange("(k p) n -> p k n", p=P)).then_inc(consts, 16)
            sp.dma_start(bqk[:], b_qkv[0:2 * D].rearrange("(m p) -> p m", p=P),
                         allow_slow_non_contiguous=True).then_inc(consts, 16)
            for t in range(2):
                sp.dma_start(bv[:, t], b_qkv[2 * D:3 * D].partition_broadcast(P)).then_inc(consts, 16)

            def body(i, s, last):
                if not last:
                    load(i + s, 1 - s)
                tok = at(sp, i * (2 * BLK) + s * BLK, BLK)
                half = at(sp, i * BLK + s * (BLK // 2), BLK // 2)
                for m in range(4):
                    wait_apart(sp, parts_done, i * 8 + (s * 4 + m + 3), consts, 64)
                    sp.dma_start(qk_parts[m // 2, :, (m % 2) * P:(m % 2 + 1) * P, half]
                                 .rearrange("a p n -> p a n"), parts[:, s, m].bitcast(F32)).then_inc(stored[s], 16)
                wait_apart(sp, v_out, i * 4 + (s * 2 + 4), consts, 64)
                sp.dma_start(v_pad[tok, :].rearrange("(t p) c -> p t c", p=P),
                             vp[:, s].rearrange("p t h c -> p t (h c)")).then_inc(stored[s], 16)

            paired(sp, NBLK, body)
            for s in range(2):
                sp.wait_ge(stored[s], NBLK // 2 * 5 * 16 + 16)

        @block.tensor
        def _(pe):
            pe.sem_inc(x_free, 2)
            pe.wait_ge(consts, 64)

            def body(i, s, last):
                pe.wait_ge(x_loaded[s], i * 16 + 16)
                for m in range(4):
                    pe.wait_ge(rest_done, i * 8 + (s * 4 + m + 1))
                    for k in range(KD):
                        mm = nc.tensor.matmul(qk_ps[:, m], w[:, k, m * P:(m + 1) * P], x[:, s, k],
                                              start=(k == 0), stop=(k == KD - 1))
                    mm.then_inc(qk_done, 1)
                for t in range(TPB):
                    if t % 2 == 0:
                        pe.wait_ge(v_out, i * 4 + (s * 2 + t // 2 + 1))
                    for k in range(KD):
                        mm = nc.tensor.matmul(v_ps[:, t], x[:, s, k, t * P:(t + 1) * P],
                                              w[:, k, 2 * D:3 * D], start=(k == 0), stop=(k == KD - 1))
                    if t % 2:
                        mm.then_inc(v_done, 1)
                pe.drain().then_inc(x_free, 1)
            paired(pe, NBLK, body)

        @block.scalar
        def _(act):
            act.wait_ge(consts, 64)

            def body(i, s, last):
                act.wait_ge(stored[s], i * (5 * 16) + 16)
                for m in range(4):
                    act.wait_ge(qk_done, i * 8 + (s * 4 + m + 1))
                    nc.scalar.activation(parts[:, s, m, 0], qk_ps[:, m], ACT.Identity,
                                         bias=bqk[:, m:m + 1]).then_inc(hi_done, 1)
            paired(act, NBLK, body)

        @block.vector
        def _(dve):
            dve.sem_inc(rest_done, 4)
            dve.sem_inc(v_out, 2)
            dve.wait_ge(v_filled, 1)

            def body(i, s, last):
                for m in range(4):
                    dve.wait_ge(hi_done, i * 8 + (s * 4 + m + 1))
                    dve.wait_ge(parts_done, i * 8 + (s * 4 + m + 1))
                    nc.vector.scalar_tensor_tensor(rest[:, m % 2], qk_ps[:, m], bqk[:, m:m + 1],
                                                   parts[:, s, m, 0], ALU.add, ALU.subtract)\
                        .then_inc(rest_done, 1)
                dve.wait_ge(stored[s], i * (5 * 16) + 16)
                for t in (0, 2):
                    dve.wait_ge(v_done, i * 4 + (s * 2 + t // 2 + 1))
                    nc.vector.tensor_tensor(vp[:, s, t:t + 2, :, 0:DH],
                                            v_ps[:, t:t + 2].rearrange("p t (h c) -> p t h c", c=DH),
                                            bv[:].rearrange("p t (h c) -> p t h c", c=DH),
                                            ALU.add).then_inc(v_out, 1)
            paired(dve, NBLK, body)

        @block.gpsimd
        def _(pool):
            nc.gpsimd.memset(vp[:], 1.0).then_inc(v_filled, 1)
            pool.sem_inc(parts_done, 2)

            def body(i, s, last):
                for m in range(4):
                    wait_apart(pool, rest_done, i * 8 + (s * 4 + m + 5), v_filled, 1)
                    nc.gpsimd.tensor_copy(parts[:, s, m, 1], rest[:, m % 2]).then_inc(mid_done, 1)
                    pool.wait_ge(mid_done, i * 8 + (s * 4 + m + 1))
                    nc.gpsimd.tensor_tensor(parts[:, s, m, 2], rest[:, m % 2], parts[:, s, m, 1],
                                            ALU.subtract).then_inc(parts_done, 1)
            paired(pool, NBLK, body)


def phase_core(nc, name, qk_parts, v_pad, ident_in, out_T, scale, window_masks=None):
    with Phase(nc, name) as ph:
        q6 = ph.sb("q6", [P, 2, H, S], BF16)
        k6 = ph.sb("k6", [P, 2, H, S], BF16)
        v = ph.sb("v", [P, 2, 2, H * 32])
        consts_f32 = ph.sb("consts_f32", [P, 5, P])
        ident = ph.sb("ident", [P, P], BF16)
        masks = ph.sb("masks", [P, 4, P], BF16)
        nmax = ph.sb("nmax", [P, 2, 4])
        mparts = ph.sb("mparts", [P, 2, 4, MAX_ROWS], BF16)
        probs = ph.sb("probs", [P, 2, 4, 2, S])
        o_sb = ph.sb("o_sb", [P, 2, S])
        o_turned = ph.sb("o_turned", [P, 2, S])
        rsum = ph.sb("rsum", [P, 2, S // 32])
        o_scaled = ph.sb("o_scaled", [P, 2, S])
        o_norm = ph.sb("o_norm", [P, 2, S])
        s_ps = ph.ps("s_ps", [P, 2, 2, 2, S])
        t_ps = ph.ps("t_ps", [P, 2, 2, S])
        m_ps = ph.ps("m_ps", [P, 4, P])
        o_ps = ph.ps("o_ps", [P, S])
        consts = ph.sem("consts")
        filled = ph.sem("filled")
        ones_set = ph.sem("ones_set")
        loaded = [ph.sem(f"loaded{s}") for s in range(2)]
        batch_done = ph.sem("batch_done")
        s_done = ph.sem("s_done")
        max_done = ph.sem("max_done")
        hi_done = ph.sem("hi_done")
        mparts_done = ph.sem("mparts_done")
        mrow_done = ph.sem("mrow_done")
        mcopied = ph.sem("mcopied")
        t_done = ph.sem("t_done")
        t_free = ph.sem("t_free")
        pv_done = ph.sem("pv_done")
        o_copied = ph.sem("o_copied")
        turned = ph.sem("turned")
        rsum_done = ph.sem("rsum_done")
        scaled = ph.sem("scaled")
        o_ready = ph.sem("o_ready")
        stored = [ph.sem(f"stored{s}") for s in range(2)]
        block = ph.block()
        nload = 13
        n_masks = 0 if window_masks is None else 1
        NCONST = 16 * (1 + n_masks)
        PAIRS = H // 2

        def blocks(ap):
            return ap.rearrange("p (b r) -> p b r", r=32)

        @block.sync
        def _(sp):
            for s in range(2):
                sp.sem_inc(stored[s], 16)
            def load(tok, half, s):
                for r in range(len(Q_PARTS)):
                    for tile, qk, part in ((q6, 0, Q_PARTS[r]), (k6, 1, K_PARTS[r])):
                        sp.dma_start(tile[r * DH:(r + 1) * DH, s].bitcast(F32),
                                     qk_parts[qk, part, :, half].rearrange("(h d) n -> d h n", d=DH))\
                            .then_inc(loaded[s], 16)
                sp.dma_start(v[:, s], v_pad[tok, :].rearrange("(k p) c -> p k c", p=P))\
                    .then_inc(loaded[s], 16)
            load(slice(0, S), slice(0, S // 2), 0)
            sp.dma_start(consts_f32[:, 4], ident_in).then_inc(consts, 16)
            if n_masks:
                sp.dma_start(consts_f32[:, 0:4], window_masks.rearrange("a p n -> p a n")).then_inc(consts, 16)

            def body(i, s, last):
                if not last:
                    tok = at(sp, i * (2 * S) + (s + 1) * S, S)
                    half = at(sp, i * S + (s + 1) * (S // 2), S // 2)
                    wait_apart(sp, batch_done, i * 2 + (s + 1), consts, NCONST)
                    load(tok, half, 1 - s)
                tok = at(sp, i * (2 * S) + s * S, S)
                for j in range(QUADS):
                    wait_apart(sp, o_ready, i * (2 * QUADS) + (s * QUADS + j + 3), consts, NCONST)
                    sp.dma_start(out_T[j, :, tok], o_norm[:, j % 2])\
                        .then_inc(stored[j % 2], 16)

            paired(sp, B, body)
            for s in range(2):
                sp.wait_ge(stored[s], B * QUADS // 2 * 16 + 16)

        @block.tensor
        def _(pe):
            pe.sem_inc(pv_done, 2)
            pe.sem_inc(batch_done, 1)
            pe.wait_ge(consts, NCONST)
            pe.wait_ge(filled, 1)
            pe.wait_ge(ones_set, 1)

            def maximum_rows(n, buf):
                pe.wait_ge(mparts_done, n + 1)
                for c in range(4):
                    mm = nc.tensor.matmul(m_ps[ROWS:ROWS + MAX_ROWS, c], mparts[:, buf, c, :],
                                          ident[:], start=True, stop=True, tile_position=(0, ROWS))
                mm.then_inc(mrow_done, 1)

            def scores(s, p):
                buf = p % 2
                for h2 in range(2):
                    h = 2 * p + h2
                    for qt in range(2):
                        mm = nc.tensor.matmul(s_ps[:, buf, h2, qt], q6[0:ROWS, s, h, qt * P:(qt + 1) * P],
                                              k6[0:ROWS, s, h, :], start=True, stop=not n_masks)
                        if n_masks:
                            kt = 1 - qt
                            mm = nc.tensor.matmul(s_ps[:, buf, h2, qt, kt * P:(kt + 1) * P], ident[:],
                                                  masks[:, qt], start=False, stop=True)
                mm.then_inc(s_done, 1)

            def values(s, j):
                if j < 0:
                    s, j = 1 - s, QUADS - 1
                for kt in range(2):
                    for c in range(4):
                        h = 4 * j + c
                        mm = nc.tensor.matmul(o_ps[32 * c:32 * c + 32], v[:, s, kt, h * 32:(h + 1) * 32],
                                              probs[:, j % 2, c, kt], start=(kt == 0), stop=(kt == 1),
                                              tile_position=(0, 32 * c))
                mm.then_inc(pv_done, 1)

            def wait_values(i, s, j):
                pe.wait_ge(t_free, i * (2 * H) + (s * H + 4 * j + 6))
                pe.wait_ge(o_copied, i * (2 * QUADS) + (s * QUADS + j + 1))

            def body(i, s, first, last):
                for p in range(PAIRS):
                    n = i * (2 * PAIRS) + (s * PAIRS + p)
                    if p + 2 < PAIRS or not last:
                        pe.wait_ge(max_done, n + 1)
                        if p + 2 == PAIRS:
                            pe.wait_ge(loaded[1 - s], i * (16 * nload) + 16 * nload * (s + 1))
                        scores((s + (p + 2) // PAIRS) % 2, (p + 2) % PAIRS)
                    if p + 1 < PAIRS or not last:
                        pe.wait_ge(mcopied, n + 1)
                        maximum_rows(n + 1, (p + 1) % 2)
                    if p % 2 == 0 and (p or not first):
                        wait_values(i, s, p // 2 - 1)
                        values(s, p // 2 - 1)
                        if p == 0:
                            pe.drain().then_inc(batch_done, 1)
                    if last and p == PAIRS - 1:
                        pe.wait_ge(mcopied, n + 1)
                    for h2 in range(2):
                        h = 2 * p + h2
                        pe.wait_ge(t_free, i * (2 * H) + (s * H + h + 1))
                        for kt in range(2):
                            mm = nc.tensor.matmul(t_ps[:, h2, kt],
                                                  k6[0:ROWS + MAX_ROWS, s, h, kt * P:(kt + 1) * P],
                                                  q6[0:ROWS + MAX_ROWS, s, h, :],
                                                  start=True, stop=not n_masks)
                            if n_masks:
                                qt = 1 - kt
                                mm = nc.tensor.matmul(t_ps[:, h2, kt, qt * P:(qt + 1) * P], ident[:],
                                                      masks[:, 2 + kt], start=False, stop=True)
                        mm.then_inc(t_done, 1)
                if last:
                    wait_values(i, s, QUADS - 1)
                    values(s, QUADS - 1)

            pe.wait_ge(loaded[0], 16 * nload)
            scores(0, 0)
            scores(0, 1)
            maximum_rows(0, 0)
            paired_first(pe, B, body)

        @block.vector
        def _(dve):
            dve.wait_ge(consts, NCONST)
            filling = nc.vector.tensor_copy(ident[:], consts_f32[:, 4])
            if n_masks:
                filling = nc.vector.tensor_copy(masks[:], consts_f32[:, 0:4])
            filling.then_inc(filled, 1)
            dve.sem_inc(o_copied, 1)

            def maximum(n, p):
                dve.wait_ge(s_done, n)
                nc.vector.tensor_reduce(nmax[:, p % 2], s_ps[:, p % 2].rearrange("p a b n -> p (a b) n"),
                                        axis=AX.X, op=ALU.max, negate=True).then_inc(max_done, 1)

            def turn_out(i, s, j):
                n = i * (2 * QUADS) + (s * QUADS + j)
                dve.wait_ge(o_copied, n + 2)
                nc.vector.transpose(o_turned[:, j % 2], o_sb[:, j % 2]).then_inc(turned, 1)
                dve.wait_ge(turned, n + 1)
                nc.vector.reciprocal(rsum[:, j % 2], blocks(o_turned[:, j % 2])[:, :, DH]).then_inc(rsum_done, 1)

            def turn_back(i, s, j):
                n = i * (2 * QUADS) + (s * QUADS + j)
                dve.wait_ge(stored[j % 2], i * (QUADS * 16) + (s * QUADS // 2 + j // 2) * 16 + 16)
                dve.wait_ge(scaled, n + 1)
                nc.vector.transpose(o_norm[:, j % 2], o_scaled[:, j % 2]).then_inc(o_ready, 1)

            def body(i, s, first, last):
                for p in range(PAIRS):
                    if not (last and p >= PAIRS - 2):
                        maximum(i * (2 * PAIRS) + (s * PAIRS + p + 3), p)
                    if p >= 2 or not first:
                        (turn_back if p % 2 else turn_out)(i, s, p // 2 - 1)
                if last:
                    turn_out(i, s, QUADS - 1)
                    turn_back(i, s, QUADS - 1)

            maximum(1, 0)
            maximum(2, 1)
            paired_first(dve, B, body)

        @block.gpsimd
        def _(pool):
            nc.gpsimd.memset(k6[ROWS:ROWS + MAX_ROWS], 1.0).then_inc(ones_set, 1)
            pool.sem_inc(o_ready, 2)

            def split_maximum(n, buf):
                wait_apart(pool, max_done, n, ones_set, 1)
                nc.gpsimd.tensor_copy(mparts[:, buf, :, 0], nmax[:, buf]).then_inc(hi_done, 1)
                pool.wait_ge(hi_done, n)
                nc.gpsimd.tensor_tensor(mparts[:, buf, :, 1], nmax[:, buf], mparts[:, buf, :, 0],
                                        ALU.subtract).then_inc(mparts_done, 1)

            def body(i, s, first, last):
                def norm(j):
                    n = i * (2 * QUADS) + (s * QUADS + j)
                    pool.wait_ge(rsum_done, n + 1)
                    pool.wait_ge(o_ready, n + 1)
                    nc.gpsimd.tensor_tensor(blocks(o_scaled[:, j % 2]), blocks(o_turned[:, j % 2]),
                                            rsum[:, j % 2].unsqueeze(2).broadcast_to([P, S // 32, 32]), ALU.mult)\
                        .then_inc(scaled, 1)
                for p in range(PAIRS):
                    if not (last and p >= PAIRS - 2):
                        split_maximum(i * (2 * PAIRS) + (s * PAIRS + p + 3), p % 2)
                    if p % 2 == 0 and (p or not first):
                        norm(p // 2 - 1)
                if last:
                    norm(QUADS - 1)

            split_maximum(1, 0)
            split_maximum(2, 1)
            paired_first(pool, B, body)

        @block.scalar
        def _(act):
            act.sem_inc(t_free, 2)

            def copy_rows(n, s, p):
                act.wait_ge(mrow_done, n)
                nc.scalar.activation(q6[ROWS:ROWS + MAX_ROWS, s, 2 * p:2 * p + 2, :],
                                     m_ps[ROWS:ROWS + MAX_ROWS].rearrange("p (a b) n -> p a (b n)", a=2),
                                     ACT.Copy).then_inc(mcopied, 1)

            def body(i, s, first, last):
                def copy_out(j):
                    n = i * (2 * QUADS) + (s * QUADS + j)
                    act.wait_ge(pv_done, n + 3)
                    act.wait_ge(o_ready, n + 1)
                    nc.scalar.activation(o_sb[:, j % 2], o_ps[:], ACT.Copy).then_inc(o_copied, 1)
                for p in range(PAIRS):
                    if p + 1 < PAIRS or not last:
                        copy_rows(i * (2 * PAIRS) + (s * PAIRS + p + 2), (s + (p + 1) // PAIRS) % 2, (p + 1) % PAIRS)
                    if p % 2 == 0 and (p or not first):
                        copy_out(p // 2 - 1)
                    for h2 in range(2):
                        h = 2 * p + h2
                        act.wait_ge(t_done, i * (2 * H) + (s * H + h + 1))
                        act.wait_ge(pv_done, i * (2 * QUADS) + (s * QUADS + h // 4 + 1))
                        nc.scalar.activation(probs[:, (h // 4) % 2, h % 4], t_ps[:, h2],
                                             ACT.Exp, scale=scale).then_inc(t_free, 1)
                if last:
                    copy_out(QUADS - 1)

            copy_rows(1, 0, 0)
            paired_first(act, B, body)


def phase_post(nc, name, o_T, groups, w_out, padded, bias, x_in, ident, x_out, x_outT, routes=None):
    with Phase(nc, name) as ph:
        w = ph.sb("w", [P, max(groups, 1), D])
        bias_sb = ph.sb("bias", [P, TPB, D])
        idt = ph.sb("idt", [P, P])
        power = ph.sb("power", [P, TPB])
        o = ph.sb("o", [P, 2, max(groups, 1), BLK])
        x = ph.sb("x", [P, 2, TPB, D])
        xb = ph.sb("xb", [P, 2, TPB, D])
        r = ph.sb("r", [P, 2, TPB, D])
        stats = ph.sb("stats", [P, 2, TPB, 6])
        mv = ph.sb("mv", [P, 2, TPB, 2])
        vare = ph.sb("vare", [P, 2, TPB])
        rstd = ph.sb("rstd", [P, 2, TPB])
        xo = ph.sb("xo", [P, 2, TPB, D])
        xoT = ph.sb("xoT", [P, 2, KD, BLK])
        NT = T // P
        if routes:
            y_sorted, positions, shares = routes
            pos = ph.sb("pos", [P, 2, NT], I32)
            share = ph.sb("share", [P, 2, NT])
            pos_c = ph.sb("pos_c", [P, 2, 2, TPB], I32)
            share_c = ph.sb("share_c", [P, 2, 2, TPB])
            yg = ph.sb("yg", [P, 2, 2, TPB, D])
            picked = ph.sem("picked")
            gathered = [ph.sem(f"gathered{s}") for s in range(2)]
            half_sum = ph.sem("half_sum")
        y_ps = ph.ps("y_ps", [P, 2, TPB, D])
        xT_ps = ph.ps("xT_ps", [P, KD, BLK])
        consts = ph.sem("consts")
        zeroed = ph.sem("zeroed")
        power_set = ph.sem("power_set")
        loaded = [ph.sem(f"loaded{s}") for s in range(2)]
        in_free = ph.sem("in_free")
        y_done = ph.sem("y_done")
        biased = ph.sem("biased")
        summed = ph.sem("summed")
        stats_done = ph.sem("stats_done")
        mv_done = ph.sem("mv_done")
        vare_done = ph.sem("vare_done")
        rstd_done = ph.sem("rstd_done")
        normed = ph.sem("normed")
        xT_done = ph.sem("xT_done")
        xT_out = ph.sem("xT_out")
        stored = [ph.sem(f"stored{s}") for s in range(2)]
        block = ph.block()
        n_in = 2 if groups else 1
        n_out = 2 if x_outT is not None else 1
        NCONST = 16 * (1 + (groups and (4 if padded else 1)) + (TPB if bias is not None else 0)
                       + (2 if routes else 0))

        @block.sync
        def _(sp):
            for s in range(2):
                sp.sem_inc(stored[s], 16)
            def load(i, s):
                tok = at(sp, i * (2 * BLK) + s * BLK, BLK)
                wait_apart(sp, in_free, i * 2 + (s + 1), consts, NCONST)
                if groups:
                    sp.dma_start(o[:, s], o_T[:, :, tok].rearrange("g p n -> p g n")).then_inc(loaded[s], 16)
                sp.dma_start(x[:, s], x_in[tok, :].rearrange("(t p) c -> p t c", p=P)).then_inc(loaded[s], 16)
            load(0, 0)
            sp.dma_start(idt[:], ident).then_inc(consts, 16)
            if groups and padded:
                sp.wait_ge(zeroed, 1)
                rows = w_out.rearrange("(g c d) n -> c d g n", c=4, d=DH)
                for c in range(4):
                    sp.dma_start(w[32 * c:32 * c + DH], rows[c]).then_inc(consts, 16)
            elif groups:
                sp.wait_ge(zeroed, 1)
                sp.dma_start(w[:], w_out.rearrange("(g p) n -> p g n", p=P)).then_inc(consts, 16)
            if bias is not None:
                for t in range(TPB):
                    sp.dma_start(bias_sb[:, t], bias.partition_broadcast(P)).then_inc(consts, 16)
            if routes:
                sp.dma_start(pos[:].rearrange("p r t -> p (r t)"), positions).then_inc(consts, 16)
                sp.dma_start(share[:].rearrange("p r t -> p (r t)"), shares).then_inc(consts, 16)

            load_all(sp, load)
            for s in range(2):
                sp.wait_ge(stored[s], NBLK // 2 * 16 * n_out + 16)

        @block.tensor
        def _(pe):
            pe.wait_ge(consts, NCONST)
            if groups:
                pe.wait_ge(zeroed, 1)

            def project(i, s):
                pe.wait_ge(loaded[s], i * (16 * n_in) + 16 * n_in)
                for t in range(TPB):
                    for g in range(groups):
                        mm = nc.tensor.matmul(y_ps[:, s, t], o[:, s, g, t * P:(t + 1) * P], w[:, g],
                                              start=(g == 0), stop=(g == groups - 1))
                mm.then_inc(y_done, 1)

            def body(i, s, last):
                if groups and not last:
                    project(i + s, 1 - s)
                if x_outT is not None:
                    pe.wait_ge(normed, i * 2 + (s + 1))
                    pe.wait_ge(xT_out, i * 2 + (s + 1))
                    for t in range(TPB):
                        for k in range(KD):
                            mm = nc.tensor.transpose(xT_ps[:, k, t * P:(t + 1) * P],
                                                     xo[:, s, t, k * P:(k + 1) * P], idt[:])
                    mm.then_inc(xT_done, 1)
            if groups:
                project(0, 0)
            paired(pe, NBLK, body)

        @block.gpsimd
        def _(pool):
            nc.gpsimd.memset(w[:], 0.0).then_inc(zeroed, 1)
            nc.gpsimd.memset(power[:], -0.5).then_inc(power_set, 1)
            if bias is not None or routes:
                pool.wait_ge(consts, NCONST)

            def gather(i, s):
                tiles = at(pool, i * (2 * TPB) + s * TPB, TPB)
                wait_apart(pool, in_free, i * 2 + (s + 1), consts, NCONST)
                nc.gpsimd.tensor_copy(pos_c[:, s], pos[:, :, tiles])
                nc.gpsimd.tensor_copy(share_c[:, s], share[:, :, tiles]).then_inc(picked, 1)
                wait_apart(pool, picked, i * 2 + (s + 1), consts, NCONST)
                for r in range(2):
                    for t in range(TPB):
                        nc.gpsimd.indirect_dma_start(
                            yg[:, s, r, t], None, y_sorted,
                            bass.IndirectOffsetOnAxis(ap=pos_c[:, s, r, t:t + 1], axis=0)).then_inc(gathered[s], 16)
            if routes:
                gather(0, 0)

            def body(i, s, last):
                if routes and not last:
                    gather(i + s, 1 - s)
                if bias is not None:
                    pool.wait_ge(loaded[s], i * (16 * n_in) + 16 * n_in)
                    nc.gpsimd.tensor_tensor(xb[:, s], x[:, s], bias_sb[:], ALU.add).then_inc(biased, 1)
                wait_apart(pool, mv_done, i * 2 + (s + 1), power_set, 1)
                nc.gpsimd.tensor_scalar(vare[:, s], mv[:, s, :, 1], LN_EPS, None, ALU.add).then_inc(vare_done, 1)
                pool.wait_ge(vare_done, i * 2 + (s + 1))
                nc.gpsimd.tensor_tensor(rstd[:, s], vare[:, s], power[:], ALU.pow).then_inc(rstd_done, 1)
            paired(pool, NBLK, body)

        @block.vector
        def _(dve):
            dve.sem_inc(in_free, 2)

            def body(i, s, last):
                n = i * 2 + (s + 1)
                res = xb if bias is not None else x
                if groups:
                    dve.wait_ge(y_done, n)
                    if bias is not None:
                        dve.wait_ge(biased, n)
                    dve.wait_ge(loaded[s], i * (16 * n_in) + 16 * n_in)
                    nc.vector.tensor_tensor(r[:, s], y_ps[:, s], res[:, s], ALU.add).then_inc(summed, 1)
                elif routes:
                    dve.wait_ge(loaded[s], i * (16 * n_in) + 16 * n_in)
                    dve.wait_ge(gathered[s], i * (32 * TPB) + 32 * TPB)
                    dve.wait_ge(picked, n)
                    for t in range(TPB):
                        op = nc.vector.scalar_tensor_tensor(r[:, s, t], yg[:, s, 0, t], share_c[:, s, 0, t:t + 1],
                                                            x[:, s, t], ALU.mult, ALU.add)
                    op.then_inc(half_sum, 1)
                    dve.wait_ge(half_sum, n)
                    for t in range(TPB):
                        op = nc.vector.scalar_tensor_tensor(r[:, s, t], yg[:, s, 1, t], share_c[:, s, 1, t:t + 1],
                                                            r[:, s, t], ALU.mult, ALU.add)
                    op.then_inc(summed, 1)
                else:
                    dve.wait_ge(loaded[s], i * (16 * n_in) + 16 * n_in)
                    nc.vector.tensor_copy(r[:, s], x[:, s]).then_inc(summed, 1)
                dve.wait_ge(summed, n)
                dve.sem_inc(in_free, 1)
                for t in range(TPB):
                    last_op = nc.vector.bn_stats(stats[:, s, t], r[:, s, t])
                last_op.then_inc(stats_done, 1)
                wait_apart(dve, stats_done, n, consts, NCONST)
                for t in range(TPB):
                    last_op = nc.vector.bn_aggr(mv[:, s, t], stats[:, s, t])
                last_op.then_inc(mv_done, 1)
                dve.wait_ge(stored[s], i * (16 * n_out) + 16)
                dve.wait_ge(mv_done, n)
                dve.wait_ge(rstd_done, n)
                for t in range(TPB):
                    last_op = nc.vector.tensor_scalar(xo[:, s, t], r[:, s, t], mv[:, s, t, 0:1],
                                                      rstd[:, s, t:t + 1], ALU.subtract, ALU.mult)
                last_op.then_inc(normed, 1)
            paired(dve, NBLK, body)

        @block.scalar
        def _(act):
            act.sem_inc(xT_out, 1)

            def body(i, s, last):
                tok = at(act, i * (2 * BLK) + s * BLK, BLK)
                wait_apart(act, normed, i * 2 + (s + 1), consts, NCONST)
                act.dma_start(x_out[tok, :].rearrange("(t p) c -> p t c", p=P), xo[:, s]).then_inc(stored[s], 16)
                if x_outT is not None:
                    act.wait_ge(xT_done, i * 2 + (s + 1))
                    for k in range(KD):
                        op = nc.scalar.activation(xoT[:, s, k], xT_ps[:, k], ACT.Copy)
                    op.then_inc(xT_out, 1)
                    wait_apart(act, xT_out, i * 2 + (s + 2), consts, NCONST)
                    act.dma_start(x_outT[:, tok].rearrange("(k p) n -> p k n", p=P), xoT[:, s])\
                        .then_inc(stored[s], 16)
            paired(act, NBLK, body)


def phase_cross(nc, xT, ctxT, Wq, bq, Wk, bk, Wv, bv, ident, o_T):
    with Phase(nc, "cross") as ph:
        PAIRS = H // 2
        LAST = B * PAIRS - 1
        wq = ph.sb("wq", [P, KD, DM])
        wk = ph.sb("wk", [P, KD, DM])
        wv = ph.sb("wv", [P, KD, DM])
        bqs = ph.sb("bqs", [P, PAIRS])
        bq_scaled = ph.sb("bq_scaled", [P, PAIRS])
        bks = ph.sb("bks", [P, PAIRS])
        bvs = ph.sb("bvs", [P, 2, DM])
        idt = ph.sb("idt", [P, P])
        x = ph.sb("x", [P, 2, KD, S])
        c = ph.sb("c", [P, 2, KD, S])
        q = ph.sb("q", [P, 2, 2, S])
        k = ph.sb("k", [P, 2, S])
        v = ph.sb("v", [P, 2, 2, P])
        nmax = ph.sb("nmax", [P, 4])
        probs = ph.sb("probs", [P, 2, 4, S])
        sums = ph.sb("sums", [P, 2, 4])
        rsum = ph.sb("rsum", [P, 2, 4])
        probs_T = ph.sb("probs_T", [P, 2, 2, S])
        o_sb = ph.sb("o_sb", [P, 2, S])
        qk_ps = ph.ps("qk_ps", [P, 2, S])
        v_ps = ph.ps("v_ps", [P, 2, 2 * P])
        s_ps = ph.ps("s_ps", [P, 4, S])
        pT_ps = ph.ps("pT_ps", [P, 2, 2, S])
        o_ps = ph.ps("o_ps", [P, 2 * S])
        consts = ph.sem("consts")
        NCONST = 16 * 8
        bias_scaled = ph.sem("bias_scaled")
        q_filled = ph.sem("q_filled")
        loaded = [ph.sem(f"loaded{s}") for s in range(2)]
        in_free = ph.sem("in_free")
        qk_done = ph.sem("qk_done")
        qk_out = ph.sem("qk_out")
        vp_done = ph.sem("vp_done")
        v_out = ph.sem("v_out")
        s_done = ph.sem("s_done")
        max_done = ph.sem("max_done")
        exp_done = ph.sem("exp_done")
        rsum_done = ph.sem("rsum_done")
        scaled = ph.sem("scaled")
        pT_done = ph.sem("pT_done")
        pT_out = ph.sem("pT_out")
        pv_done = ph.sem("pv_done")
        o_out = ph.sem("o_out")
        stored = [ph.sem(f"stored{s}") for s in range(2)]
        block = ph.block()

        @block.sync
        def _(sp):
            for s in range(2):
                sp.sem_inc(stored[s], 16)
            def load(i, s):
                tok = at(sp, i * (2 * S) + s * S, S)
                wait_apart(sp, in_free, i * 2 + (s + 1), consts, NCONST)
                for dst, src in ((x, xT), (c, ctxT)):
                    sp.dma_start(dst[:, s], src[:, tok].rearrange("(k p) n -> p k n", p=P))\
                        .then_inc(loaded[s], 16)
            load(0, 0)
            for dst, src in ((wq, Wq), (wk, Wk), (wv, Wv)):
                sp.dma_start(dst[:], src.rearrange("(k p) n -> p k n", p=P)).then_inc(consts, 16)
            for dst, src in ((bqs, bq), (bks, bk)):
                sp.dma_start(dst[:], src.rearrange("(m p) -> p m", p=P),
                             allow_slow_non_contiguous=True).then_inc(consts, 16)
            for t in range(2):
                sp.dma_start(bvs[:, t], bv.partition_broadcast(P)).then_inc(consts, 16)
            sp.dma_start(idt[:], ident).then_inc(consts, 16)

            def body(i, s, last):
                if not last:
                    load(i + s, 1 - s)
                tok = at(sp, i * (2 * S) + s * S, S)
                for p in range(PAIRS):
                    wait_apart(sp, o_out, i * (2 * PAIRS) + (s * PAIRS + p + 2), consts, NCONST)
                    sp.dma_start(o_T[p, :, tok], o_sb[:, p % 2]).then_inc(stored[p % 2], 16)

            paired(sp, B, body)
            for s in range(2):
                sp.wait_ge(stored[s], B * PAIRS // 2 * 16 + 16)

        @block.tensor
        def _(pe):
            pe.sem_inc(in_free, 2)
            pe.wait_ge(consts, NCONST)
            pe.wait_ge(q_filled, 1)

            def project_qk(m, s, p):
                pe.wait_ge(qk_out, m + 1)
                for j, (wt, src) in enumerate(((wq, x), (wk, c))):
                    for kd in range(KD):
                        mm = nc.tensor.matmul(qk_ps[:, j], wt[:, kd, p * P:(p + 1) * P], src[:, s, kd],
                                              start=(kd == 0), stop=(kd == KD - 1))
                mm.then_inc(qk_done, 1)

            def project_v(m, s, p):
                pe.wait_ge(v_out, m + 1)
                for t in range(2):
                    for kd in range(KD):
                        mm = nc.tensor.matmul(v_ps[:, t, 0:P], c[:, s, kd, t * P:(t + 1) * P],
                                              wv[:, kd, p * P:(p + 1) * P],
                                              start=(kd == 0), stop=(kd == KD - 1))
                mm.then_inc(vp_done, 1)

            def scores(m, buf):
                pe.wait_ge(qk_out, m + 2)
                pe.wait_ge(exp_done, m + 1)
                for h2 in range(2):
                    for qt in range(2):
                        mm = nc.tensor.matmul(s_ps[:, 2 * h2 + qt], q[:, buf, h2, qt * P:(qt + 1) * P],
                                              k[:, buf], start=True, stop=True)
                    mm.then_inc(s_done, 1)

            def turn(m, buf):
                pe.wait_ge(scaled, m + 1)
                for h2 in range(2):
                    for kt in range(2):
                        for qt in range(2):
                            mm = nc.tensor.transpose(pT_ps[:, h2, kt, qt * P:(qt + 1) * P],
                                                     probs[:, buf, 2 * h2 + qt, kt * P:(kt + 1) * P], idt[:])
                mm.then_inc(pT_done, 1)

            def values(m, buf):
                pe.wait_ge(pT_out, m + 1)
                pe.wait_ge(v_out, m + 2)
                pe.wait_ge(o_out, m + 1)
                for kt in range(2):
                    for h2 in range(2):
                        mm = nc.tensor.matmul(o_ps[DX * h2:DX * h2 + DX, 0:S],
                                              v[:, buf, kt, h2 * DX:(h2 + 1) * DX],
                                              probs_T[:, h2, kt], start=(kt == 0), stop=(kt == 1),
                                              tile_position=(0, DX * h2))
                mm.then_inc(pv_done, 1)

            def body(i, s, first, last):
                for p in range(PAIRS):
                    m = i * (2 * PAIRS) + (s * PAIRS + p)
                    if not (last and p >= PAIRS - 2):
                        if p == PAIRS - 2:
                            pe.wait_ge(loaded[1 - s], i * 32 + 32 * (s + 1))
                        project_qk(m + 2, (s + (p + 2) // PAIRS) % 2, (p + 2) % PAIRS)
                    if not (first and p == 0):
                        turn(m - 1, (p + 1) % 2)
                    project_v(m, s, p)
                    if p == PAIRS - 1:
                        pe.drain().then_inc(in_free, 1)
                    if not (last and p == PAIRS - 1):
                        scores(m + 1, (p + 1) % 2)
                    if not (first and p == 0):
                        values(m - 1, (p + 1) % 2)

            pe.wait_ge(loaded[0], 32)
            project_qk(0, 0, 0)
            project_qk(1, 0, 1)
            scores(0, 0)
            paired_first(pe, B, body)
            turn(LAST, 1)
            values(LAST, 1)

        @block.scalar
        def _(act):
            act.sem_inc(qk_out, 1)
            act.sem_inc(exp_done, 1)
            act.wait_ge(consts, NCONST)
            act.wait_ge(q_filled, 1)
            act.wait_ge(bias_scaled, 1)

            def copy_qk(m, p):
                act.wait_ge(qk_done, m + 1)
                for h2 in range(2):
                    rows = slice(DX * h2, DX * h2 + DX)
                    nc.scalar.activation(q[rows, p % 2, h2], qk_ps[rows, 0], ACT.Identity,
                                         bias=bq_scaled[rows, p:p + 1], scale=DX ** -0.5)
                nc.scalar.activation(k[:, p % 2], qk_ps[:, 1], ACT.Identity, bias=bks[:, p:p + 1])\
                    .then_inc(qk_out, 1)

            def exps(m, buf):
                act.wait_ge(max_done, m + 1)
                act.wait_ge(pT_done, m + 1)
                for r in range(4):
                    op = nc.scalar.activation(probs[:, buf, r], s_ps[:, r], ACT.Exp, bias=nmax[:, r:r + 1],
                                              accum_out=sums[:, buf, r:r + 1])
                op.then_inc(exp_done, 1)

            def copy_out(i, s, p):
                act.wait_ge(pv_done, i * (2 * PAIRS) + (s * PAIRS + p + 1))
                act.wait_ge(stored[p % 2], i * (PAIRS * 16) + (s * PAIRS // 2 + p // 2) * 16 + 16)
                nc.scalar.activation(o_sb[:, p % 2], o_ps[:, 0:S], ACT.Copy).then_inc(o_out, 1)

            def body(i, s, first, last):
                for p in range(PAIRS):
                    m = i * (2 * PAIRS) + (s * PAIRS + p)
                    if not (last and p >= PAIRS - 2):
                        copy_qk(m + 2, (p + 2) % PAIRS)
                    if not (first and p == 0):
                        copy_out(i, s, p - 1)
                    if not (last and p == PAIRS - 1):
                        exps(m + 1, (p + 1) % 2)
            copy_qk(0, 0)
            copy_qk(1, 1)
            exps(0, 0)
            paired_first(act, B, body)
            copy_out(B // 2 - 1, 1, PAIRS - 1)

        @block.vector
        def _(dve):
            dve.sem_inc(v_out, 1)
            dve.sem_inc(o_out, 1)
            dve.sem_inc(pT_done, 2)
            dve.wait_ge(consts, NCONST)
            nc.vector.tensor_scalar(bq_scaled[:], bqs[:], DX ** -0.5, None, ALU.mult).then_inc(bias_scaled, 1)

            def copy_turned(m):
                dve.wait_ge(pT_done, m + 3)
                for h2 in range(2):
                    op = nc.vector.tensor_copy(probs_T[:, h2], pT_ps[:, h2])
                op.then_inc(pT_out, 1)

            def copy_v(m, p):
                dve.wait_ge(vp_done, m + 1)
                nc.vector.tensor_tensor(v[:, p % 2], v_ps[:, :, 0:P], bvs[:, :, p * P:(p + 1) * P], ALU.add)\
                    .then_inc(v_out, 1)

            def maxima(m, buf):
                dve.wait_ge(exp_done, m + 1)
                for h2 in range(2):
                    dve.wait_ge(s_done, m * 2 + (h2 + 1))
                    op = nc.vector.tensor_reduce(nmax[:, 2 * h2:2 * h2 + 2], s_ps[:, 2 * h2:2 * h2 + 2],
                                                 axis=AX.X, op=ALU.max, negate=True)
                op.then_inc(max_done, 1)

            def reciprocals(m, buf):
                dve.wait_ge(exp_done, m + 2)
                nc.vector.reciprocal(rsum[:, buf], sums[:, buf]).then_inc(rsum_done, 1)

            def body(i, s, first, last):
                for p in range(PAIRS):
                    m = i * (2 * PAIRS) + (s * PAIRS + p)
                    if not (first and p == 0):
                        copy_turned(m - 1)
                    copy_v(m, p)
                    if not (last and p == PAIRS - 1):
                        maxima(m + 1, (p + 1) % 2)
                        reciprocals(m + 1, (p + 1) % 2)
            maxima(0, 0)
            reciprocals(0, 0)
            paired_first(dve, B, body)
            copy_turned(LAST)

        @block.gpsimd
        def _(pool):
            nc.gpsimd.memset(q[:], 0.0).then_inc(q_filled, 1)

            def body(i, s, last):
                pool.wait_ge(rsum_done, i * 2 + (s + 1))
                nc.gpsimd.tensor_tensor(probs[:, s], probs[:, s],
                                        rsum[:, s].unsqueeze(2).broadcast_to([P, 4, S]), ALU.mult)\
                    .then_inc(scaled, 1)
            paired(pool, LAST + 1, body)


def phase_rwkv_in(nc, xT, maas, WT, qk_parts, v_pad, gate):
    with Phase(nc, "rin") as ph:
        w = ph.sb("w", [P, 4, KD, D])
        maa = ph.sb("maa", [P, 4, KD])
        x = ph.sb("x", [P, 2, KD, 2, S + 1])
        dx = ph.sb("dx", [P, KD, 2, S])
        mix = ph.sb("mix", [P, 4, KD, BLK])
        parts = ph.sb("parts", [P, 2, 4, 3, BLK], BF16)
        rest = ph.sb("rest", [P, 2, BLK])
        vp = ph.sb("vp", [P, 2, TPB, H, 32])
        g = ph.sb("g", [P, 2, TPB, D])
        qk_ps = ph.ps("qk_ps", [P, 4, BLK])
        v_ps = ph.ps("v_ps", [P, TPB, D])
        g_ps = ph.ps("g_ps", [P, TPB, D])
        consts = ph.sem("consts")
        NCONST = 16 * 8
        x_loaded = [ph.sem(f"x_loaded{s}") for s in range(2)]
        x_free = ph.sem("x_free")
        x_zeroed = ph.sem("x_zeroed")
        dx_done = ph.sem("dx_done")
        mixed = ph.sem("mixed")
        mix_free = ph.sem("mix_free")
        qk_done = ph.sem("qk_done")
        hi_done = ph.sem("hi_done")
        rest_done = ph.sem("rest_done")
        mid_done = ph.sem("mid_done")
        parts_done = ph.sem("parts_done")
        v_zeroed = ph.sem("v_zeroed")
        v_done = ph.sem("v_done")
        v_out = ph.sem("v_out")
        g_done = ph.sem("g_done")
        g_out = ph.sem("g_out")
        stored = [ph.sem(f"stored{s}") for s in range(2)]
        block = ph.block()

        @block.sync
        def _(sp):
            for s in range(2):
                sp.sem_inc(stored[s], 16)
            def load(i, s):
                tok = at(sp, i * (2 * BLK) + s * BLK, BLK)
                wait_apart(sp, x_free, i * 2 + (s + 1), consts, NCONST)
                for k in range(KD):
                    sp.dma_start(x[:, s, k, :, 1:S + 1], xT[k * P:(k + 1) * P, tok]
                                 .rearrange("p (b n) -> p b n", b=2)).then_inc(x_loaded[s], 16)
            load(0, 0)
            for j in range(4):
                sp.dma_start(w[:, j], WT[j].rearrange("(k p) n -> p k n", p=P)).then_inc(consts, 16)
                sp.dma_start(maa[:, j], maas[j].rearrange("a b (k p) -> p (a b k)", p=P),
                             allow_slow_non_contiguous=True).then_inc(consts, 16)
            sp.wait_ge(x_zeroed, 1)

            def body(i, s, last):
                if not last:
                    load(i + s, 1 - s)
                tok = at(sp, i * (2 * BLK) + s * BLK, BLK)
                half = at(sp, i * BLK + s * (BLK // 2), BLK // 2)
                for m in range(4):
                    wait_apart(sp, parts_done, i * 8 + (s * 4 + m + 3), consts, NCONST)
                    sp.dma_start(qk_parts[m // 2, :, (m % 2) * P:(m % 2 + 1) * P, half]
                                 .rearrange("a p n -> p a n"), parts[:, s, m].bitcast(F32)).then_inc(stored[s], 16)
                wait_apart(sp, v_out, i * 4 + (s * 2 + 4), consts, NCONST)
                sp.dma_start(v_pad[tok, :].rearrange("(t p) c -> p t c", p=P),
                             vp[:, s].rearrange("p t h c -> p t (h c)")).then_inc(stored[s], 16)
                wait_apart(sp, g_out, i * 4 + (s * 2 + 4), consts, NCONST)
                sp.dma_start(gate[tok, :].rearrange("(t p) c -> p t c", p=P), g[:, s]).then_inc(stored[s], 16)

            paired(sp, NBLK, body)
            for s in range(2):
                sp.wait_ge(stored[s], NBLK // 2 * 6 * 16 + 16)

        @block.vector
        def _(dve):
            dve.sem_inc(x_free, 2)
            dve.sem_inc(rest_done, 4)
            dve.sem_inc(v_out, 2)
            nc.vector.memset(x[:, :, :, :, 0:1], 0.0).then_inc(x_zeroed, 1)
            dve.wait_ge(consts, NCONST)
            dve.wait_ge(x_zeroed, 1)
            dve.wait_ge(v_zeroed, 1)

            def shift(i, s):
                n = i * 2 + (s + 1)
                dve.wait_ge(x_loaded[s], i * 32 + 32)
                nc.vector.tensor_tensor(dx[:].rearrange("p k b n -> p (k b) n"),
                                        x[:, s, :, :, 0:S].rearrange("p k b n -> p (k b) n"),
                                        x[:, s, :, :, 1:S + 1].rearrange("p k b n -> p (k b) n"),
                                        ALU.subtract).then_inc(dx_done, 1)
                dve.wait_ge(mix_free, n)
                dve.wait_ge(dx_done, n)
                for j in range(4):
                    for k in range(KD):
                        op = nc.vector.scalar_tensor_tensor(
                            mix[:, j, k].rearrange("p (b n) -> p b n", b=2), dx[:, k], maa[:, j, k:k + 1],
                            x[:, s, k, :, 1:S + 1], ALU.mult, ALU.add)
                    op.then_inc(mixed, 1)
                dve.wait_ge(mixed, n * 4)
                dve.sem_inc(x_free, 1)

            def body(i, s, last):
                shift(i, s)
                for m in range(4):
                    dve.wait_ge(hi_done, i * 8 + (s * 4 + m + 1))
                    dve.wait_ge(parts_done, i * 8 + (s * 4 + m + 1))
                    nc.vector.tensor_tensor(rest[:, m % 2], qk_ps[:, m], parts[:, s, m, 0], ALU.subtract)\
                        .then_inc(rest_done, 1)
                dve.wait_ge(stored[s], i * (6 * 16) + 16)
                for t in (0, 2):
                    dve.wait_ge(v_done, i * 4 + (s * 2 + t // 2 + 1))
                    nc.vector.tensor_copy(vp[:, s, t:t + 2, :, 0:DH],
                                          v_ps[:, t:t + 2].rearrange("p t (h c) -> p t h c", c=DH))\
                        .then_inc(v_out, 1)
            paired(dve, NBLK, body)

        @block.tensor
        def _(pe):
            pe.sem_inc(mix_free, 1)
            pe.wait_ge(consts, NCONST)

            def body(i, s, last):
                for m in range(4):
                    pe.wait_ge(mixed, i * 8 + (s * 4 + m // 2 + 1))
                    pe.wait_ge(rest_done, i * 8 + (s * 4 + m + 1))
                    for k in range(KD):
                        mm = nc.tensor.matmul(qk_ps[:, m], w[:, m // 2, k, (m % 2) * P:(m % 2 + 1) * P],
                                              mix[:, m // 2, k], start=(k == 0), stop=(k == KD - 1))
                    mm.then_inc(qk_done, 1)
                for j, out, free, done in ((2, v_ps, v_out, v_done), (3, g_ps, g_out, g_done)):
                    pe.wait_ge(mixed, i * 8 + (s * 4 + j + 1))
                    for t in range(TPB):
                        if t % 2 == 0:
                            pe.wait_ge(free, i * 4 + (s * 2 + t // 2 + 1))
                        for k in range(KD):
                            mm = nc.tensor.matmul(out[:, t], mix[:, j, k, t * P:(t + 1) * P], w[:, j, k],
                                                  start=(k == 0), stop=(k == KD - 1))
                        if t % 2:
                            mm.then_inc(done, 1)
                pe.drain().then_inc(mix_free, 1)
            paired(pe, NBLK, body)

        @block.scalar
        def _(act):
            act.sem_inc(g_out, 2)

            def body(i, s, last):
                act.wait_ge(stored[s], i * (6 * 16) + 16)
                for m in range(4):
                    act.wait_ge(qk_done, i * 8 + (s * 4 + m + 1))
                    nc.scalar.activation(parts[:, s, m, 0], qk_ps[:, m], ACT.Copy).then_inc(hi_done, 1)
                for t in (0, 2):
                    act.wait_ge(g_done, i * 4 + (s * 2 + t // 2 + 1))
                    nc.scalar.activation(g[:, s, t:t + 2].rearrange("p t c -> p (t c)"),
                                         g_ps[:, t:t + 2].rearrange("p t c -> p (t c)"), ACT.Gelu)\
                        .then_inc(g_out, 1)
            paired(act, NBLK, body)

        @block.gpsimd
        def _(pool):
            nc.gpsimd.memset(vp[:], 0.0).then_inc(v_zeroed, 1)
            pool.sem_inc(parts_done, 2)

            def body(i, s, last):
                for m in range(4):
                    wait_apart(pool, rest_done, i * 8 + (s * 4 + m + 5), v_zeroed, 1)
                    nc.gpsimd.tensor_copy(parts[:, s, m, 1], rest[:, m % 2]).then_inc(mid_done, 1)
                    pool.wait_ge(mid_done, i * 8 + (s * 4 + m + 1))
                    nc.gpsimd.tensor_tensor(parts[:, s, m, 2], rest[:, m % 2], parts[:, s, m, 1],
                                            ALU.subtract).then_inc(parts_done, 1)
            paired(pool, NBLK, body)


def phase_rwkv_core(nc, qk_parts, v_pad, decay, faaaa, diag, out_T):
    with Phase(nc, "rwkv") as ph:
        WIDE = S + P
        q6 = ph.sb("q6", [P, 2, H, S], BF16)
        k6 = ph.sb("k6", [P, 2, H, S], BF16)
        v = ph.sb("v", [P, 2, 2, H * 32])
        dg = ph.sb("dg", [P, S])
        dec = ph.sb("dec", [P, H])
        u = ph.sb("u", [P, H])
        neg = ph.sb("neg", [P, H])
        dist = ph.sb("dist", [P, S])
        weight = ph.sb("weight", [P, H, S])
        att = ph.sb("att", [P, 2, 4, WIDE])
        o_sb = ph.sb("o_sb", [P, 2, S])
        t_ps = ph.ps("t_ps", [P, 4, 2 * S])
        o_ps = ph.ps("o_ps", [P, 2, 2 * S])
        consts = ph.sem("consts")
        dist_done = ph.sem("dist_done")
        expdec_done = ph.sem("expdec_done")
        neg_done = ph.sem("neg_done")
        powers_done = ph.sem("powers_done")
        masked = ph.sem("masked")
        weight_done = ph.sem("weight_done")
        loaded = [ph.sem(f"loaded{s}") for s in range(2)]
        batch_done = ph.sem("batch_done")
        t_done = ph.sem("t_done")
        att_done = ph.sem("att_done")
        pv_done = ph.sem("pv_done")
        o_out = ph.sem("o_out")
        stored = [ph.sem(f"stored{s}") for s in range(2)]
        block = ph.block()
        nload = 13
        NCONST = 48

        @block.sync
        def _(sp):
            for s in range(2):
                sp.sem_inc(stored[s], 16)
            def load(tok, half, s):
                for r in range(len(Q_PARTS)):
                    for tile, qk, part in ((q6, 0, Q_PARTS[r]), (k6, 1, K_PARTS[r])):
                        sp.dma_start(tile[r * DH:(r + 1) * DH, s].bitcast(F32),
                                     qk_parts[qk, part, :, half].rearrange("(h d) n -> d h n", d=DH))\
                            .then_inc(loaded[s], 16)
                sp.dma_start(v[:, s], v_pad[tok, :].rearrange("(k p) c -> p k c", p=P))\
                    .then_inc(loaded[s], 16)
            sp.dma_start(dec[:], decay.rearrange("h a -> (h a)").partition_broadcast(P)).then_inc(consts, 16)
            sp.dma_start(u[:], faaaa.rearrange("h a -> (h a)").partition_broadcast(P)).then_inc(consts, 16)
            sp.dma_start(dg[:], diag).then_inc(consts, 16)
            load(slice(0, S), slice(0, S // 2), 0)

            def body(i, s, last):
                if not last:
                    tok = at(sp, i * (2 * S) + (s + 1) * S, S)
                    half = at(sp, i * S + (s + 1) * (S // 2), S // 2)
                    wait_apart(sp, batch_done, i * 2 + (s + 1), consts, NCONST)
                    load(tok, half, 1 - s)
                tok = at(sp, i * (2 * S) + s * S, S)
                for j in range(QUADS):
                    wait_apart(sp, o_out, i * (2 * QUADS) + (s * QUADS + j + 3), consts, NCONST)
                    sp.dma_start(out_T[j, :, tok], o_sb[:, j % 2]).then_inc(stored[j % 2], 16)

            paired(sp, B, body)
            for s in range(2):
                sp.wait_ge(stored[s], B * QUADS // 2 * 16 + 16)

        @block.gpsimd
        def _(pool):
            nc.gpsimd.iota(dist[:], pattern=[[1, S]], base=-1, channel_multiplier=-1,
                           allow_small_or_imprecise_dtypes=True).then_inc(dist_done, 1)
            pool.wait_ge(dist_done, 1)
            nc.gpsimd.tensor_scalar(dist[:], dist[:], 0.0, None, ALU.max).then_inc(dist_done, 1)
            pool.wait_ge(powers_done, 1)
            nc.gpsimd.affine_select(out=weight[:], in_=weight[:], pattern=[[0, H], [1, S]],
                                    compare_op=ALU.is_ge, fill=0.0, base=-1, channel_multiplier=-1)\
                .then_inc(masked, 1)

        @block.tensor
        def _(pe):
            pe.sem_inc(pv_done, 2)
            pe.sem_inc(batch_done, 1)

            def scores(s, h):
                for kt in range(2):
                    mm = nc.tensor.matmul(t_ps[:, h % 4, (0, S)[kt]:(S, WIDE)[kt]],
                                          k6[0:ROWS, s, h, kt * P:(kt + 1) * P], q6[0:ROWS, s, h, kt * P:S],
                                          start=True, stop=True)
                mm.then_inc(t_done, 1)

            def values(s, j):
                for kt in range(2):
                    for c in range(4):
                        h = 4 * j + c
                        mm = nc.tensor.matmul(o_ps[32 * c:32 * c + 32, j % 2, kt * P:S],
                                              v[:, s, kt, h * 32:(h + 1) * 32],
                                              att[:, j % 2, c, (0, S)[kt]:(S, WIDE)[kt]],
                                              start=(kt == 0), stop=(kt == 1), tile_position=(0, 32 * c))
                mm.then_inc(pv_done, 1)

            def body(i, s, last):
                pe.wait_ge(loaded[s], i * (16 * nload) + 16 * nload)
                for j in range(QUADS + 1):
                    n = i * (2 * QUADS) + (s * QUADS + j)
                    if j < QUADS:
                        for c in range(4):
                            pe.wait_ge(att_done, n * 4 + (c + 1))
                            scores(s, 4 * j + c)
                    if j:
                        pe.wait_ge(att_done, n * 4 + 4)
                        pe.wait_ge(o_out, n)
                        values(s, j - 1)
                pe.drain().then_inc(batch_done, 1)
            paired(pe, B, body)

        @block.vector
        def _(dve):
            dve.sem_inc(att_done, 4)
            dve.wait_ge(expdec_done, 1)
            nc.vector.tensor_scalar(neg[:], neg[:], -1.0, None, ALU.mult).then_inc(neg_done, 1)
            dve.wait_ge(masked, 1)
            for h in range(H):
                op = nc.vector.scalar_tensor_tensor(weight[:, h], dg[:], u[:, h:h + 1], weight[:, h],
                                                    ALU.mult, ALU.add)
            op.then_inc(weight_done, 1)
            dve.wait_ge(weight_done, 1)

            def body(i, s, last):
                for h in range(H):
                    dve.wait_ge(t_done, i * (2 * H) + (s * H + h + 1))
                    dve.wait_ge(pv_done, i * (2 * QUADS) + (s * QUADS + h // 4 + 1))
                    nc.vector.tensor_tensor(att[:, (h // 4) % 2, h % 4, 0:S], t_ps[:, h % 4, 0:S],
                                            weight[:, h], ALU.mult)
                    nc.vector.tensor_tensor(att[:, (h // 4) % 2, h % 4, S:WIDE], t_ps[:, h % 4, S:WIDE],
                                            weight[:, h, 0:P], ALU.mult).then_inc(att_done, 1)
            paired(dve, B, body)

        @block.scalar
        def _(act):
            act.sem_inc(o_out, 2)
            act.wait_ge(consts, NCONST)
            nc.scalar.activation(neg[:], dec[:], ACT.Exp).then_inc(expdec_done, 1)
            act.wait_ge(neg_done, 1)
            act.wait_ge(dist_done, 2)
            for h in range(H):
                op = nc.scalar.activation(weight[:, h], dist[:], ACT.Exp, scale=neg[:, h:h + 1])
            op.then_inc(powers_done, 1)

            def body(i, s, last):
                for j in range(QUADS):
                    act.wait_ge(stored[j % 2], i * (QUADS * 16) + (s * QUADS // 2 + j // 2) * 16 + 16)
                    act.wait_ge(pv_done, i * (2 * QUADS) + (s * QUADS + j + 3))
                    nc.scalar.activation(o_sb[:, j % 2], o_ps[:, j % 2, 0:S], ACT.Copy).then_inc(o_out, 1)
            paired(act, B, body)


def phase_group_norm(nc, y_T, identity, ln_w, ln_b, gate, ident, z_T):
    with Phase(nc, "gn") as ph:
        w = ph.sb("w", [P, QUADS, D])
        idt = ph.sb("idt", [P, P])
        lw = ph.sb("lw", [P, D])
        lb = ph.sb("lb", [P, D])
        yT = ph.sb("yT", [P, 2, QUADS, BLK])
        g = ph.sb("g", [P, 2, TPB, D])
        yc = ph.sb("yc", [P, TPB, D])
        sq = ph.sb("sq", [P, TPB, D])
        sums = ph.sb("sums", [P, TPB * H])
        mean = ph.sb("mean", [P, TPB * H])
        sqs = ph.sb("sqs", [P, TPB * H])
        var = ph.sb("var", [P, TPB * H])
        std = ph.sb("std", [P, TPB * H])
        rstd = ph.sb("rstd", [P, TPB * H])
        z = ph.sb("z", [P, TPB, D])
        zT = ph.sb("zT", [P, 2, KD, BLK])
        y_ps = ph.ps("y_ps", [P, 2, TPB, D])
        zT_ps = ph.ps("zT_ps", [P, KD, BLK])
        consts = ph.sem("consts")
        NCONST = 16 * 7
        zeroed = ph.sem("zeroed")
        loaded = [ph.sem(f"loaded{s}") for s in range(2)]
        y_done = ph.sem("y_done")
        step = ph.sem("step")
        centred = ph.sem("centred")
        squared = ph.sem("squared")
        var_done = ph.sem("var_done")
        std_done = ph.sem("std_done")
        in_free = ph.sem("in_free")
        zT_done = ph.sem("zT_done")
        zT_out = ph.sem("zT_out")
        stored = [ph.sem(f"stored{s}") for s in range(2)]
        block = ph.block()

        @block.sync
        def _(sp):
            for s in range(2):
                sp.sem_inc(stored[s], 16)
            def load(i, s):
                tok = at(sp, i * (2 * BLK) + s * BLK, BLK)
                wait_apart(sp, in_free, i * 2 + (s + 1), consts, NCONST)
                sp.dma_start(yT[:, s], y_T[:, :, tok].rearrange("g p n -> p g n")).then_inc(loaded[s], 16)
                sp.dma_start(g[:, s], gate[tok, :].rearrange("(t p) c -> p t c", p=P)).then_inc(loaded[s], 16)
            load(0, 0)
            sp.dma_start(idt[:], ident).then_inc(consts, 16)
            sp.dma_start(lw[:], ln_w.partition_broadcast(P)).then_inc(consts, 16)
            sp.dma_start(lb[:], ln_b.partition_broadcast(P)).then_inc(consts, 16)
            sp.wait_ge(zeroed, 1)
            rows = identity.rearrange("(g c d) n -> c d g n", c=4, d=DH)
            for c in range(4):
                sp.dma_start(w[32 * c:32 * c + DH], rows[c]).then_inc(consts, 16)

            load_all(sp, load)
            for s in range(2):
                sp.wait_ge(stored[s], NBLK // 2 * 16 + 16)

        @block.tensor
        def _(pe):
            pe.wait_ge(consts, NCONST)
            pe.wait_ge(zeroed, 1)

            def turn(i, s):
                pe.wait_ge(loaded[s], i * 32 + 32)
                for t in range(TPB):
                    for c in range(QUADS):
                        mm = nc.tensor.matmul(y_ps[:, s, t], yT[:, s, c, t * P:(t + 1) * P], w[:, c],
                                              start=(c == 0), stop=(c == QUADS - 1))
                mm.then_inc(y_done, 1)

            def body(i, s, last):
                if not last:
                    turn(i + s, 1 - s)
                pe.wait_ge(in_free, i * 2 + (s + 3))
                pe.wait_ge(zT_out, i * 2 + (s + 1))
                for t in range(TPB):
                    for k in range(KD):
                        mm = nc.tensor.transpose(zT_ps[:, k, t * P:(t + 1) * P], z[:, t, k * P:(k + 1) * P],
                                                 idt[:])
                mm.then_inc(zT_done, 1)
            turn(0, 0)
            paired(pe, NBLK, body)

        def heads(ap):
            return ap.rearrange("p t (h c) -> p (t h) c", c=DH)

        def spread(ap):
            return ap.unsqueeze(2).broadcast_to([P, TPB * H, DH])

        @block.vector
        def _(dve):
            dve.sem_inc(in_free, 2)
            dve.wait_ge(consts, NCONST)
            STEPS = 11

            def body(i, s, last):
                n = i * 2 + (s + 1)
                done = 0

                def link(op):
                    nonlocal done
                    done += 1
                    op.then_inc(step, 1)
                    dve.wait_ge(step, (n - 1) * STEPS + done)
                dve.wait_ge(y_done, n)
                link(nc.vector.tensor_reduce(sums[:], heads(y_ps[:, s]), axis=AX.X, op=ALU.add))
                link(nc.vector.tensor_scalar(mean[:], sums[:], 1.0 / DH, None, ALU.mult))
                nc.vector.tensor_tensor(heads(yc[:]), heads(y_ps[:, s]), spread(mean[:]), ALU.subtract)\
                    .then_inc(centred, 1)
                dve.wait_ge(squared, n)
                link(nc.vector.tensor_reduce(sqs[:], heads(sq[:]), axis=AX.X, op=ALU.add))
                nc.vector.tensor_scalar(var[:], sqs[:], 1.0 / DH, GN_EPS, ALU.mult, ALU.add).then_inc(var_done, 1)
                dve.wait_ge(std_done, n)
                link(nc.vector.reciprocal(rstd[:], std[:]))
                link(nc.vector.tensor_tensor(std[:], rstd[:], rstd[:], ALU.mult))
                link(nc.vector.tensor_tensor(std[:], std[:], var[:], ALU.mult))
                link(nc.vector.tensor_scalar(std[:], std[:], -0.5, 1.5, ALU.mult, ALU.add))
                link(nc.vector.tensor_tensor(rstd[:], rstd[:], std[:], ALU.mult))
                dve.wait_ge(centred, n)
                link(nc.vector.tensor_tensor(heads(yc[:]), heads(yc[:]), spread(rstd[:]), ALU.mult))
                link(nc.vector.tensor_tensor(yc[:], yc[:], lw[:].unsqueeze(1).broadcast_to([P, TPB, D]), ALU.mult))
                link(nc.vector.tensor_tensor(yc[:], yc[:], lb[:].unsqueeze(1).broadcast_to([P, TPB, D]), ALU.add))
                dve.wait_ge(zT_out, n)
                dve.wait_ge(loaded[s], i * 32 + 32)
                nc.vector.tensor_tensor(z[:], yc[:], g[:, s], ALU.mult).then_inc(in_free, 1)
            paired(dve, NBLK, body)

        @block.gpsimd
        def _(pool):
            nc.gpsimd.memset(w[:], 0.0).then_inc(zeroed, 1)

        @block.scalar
        def _(act):
            act.sem_inc(zT_out, 1)

            def body(i, s, last):
                act.wait_ge(centred, i * 2 + (s + 1))
                nc.scalar.activation(sq[:], yc[:], ACT.Square).then_inc(squared, 1)
                act.wait_ge(var_done, i * 2 + (s + 1))
                nc.scalar.activation(std[:], var[:], ACT.Sqrt).then_inc(std_done, 1)
                act.wait_ge(stored[s], i * 16 + 16)
                act.wait_ge(zT_done, i * 2 + (s + 1))
                for k in range(KD):
                    op = nc.scalar.activation(zT[:, s, k], zT_ps[:, k], ACT.Copy)
                op.then_inc(zT_out, 1)
                tok = at(act, i * (2 * BLK) + s * BLK, BLK)
                wait_apart(act, zT_out, i * 2 + (s + 2), consts, NCONST)
                act.dma_start(z_T[:, :, tok].rearrange("k p n -> p k n"), zT[:, s]).then_inc(stored[s], 16)
            paired(act, NBLK, body)


def phase_split(nc, qT, kT, v_in, qk_parts, v_pad):
    with Phase(nc, "split") as ph:
        x = ph.sb("x", [P, 2, 2 * KD, BLK])
        parts = ph.sb("parts", [P, 2, 3, 2 * KD, BLK], BF16)
        rest = ph.sb("rest", [P, 2 * KD, BLK])
        vin = ph.sb("vin", [P, 2, TPB, D])
        vp = ph.sb("vp", [P, 2, TPB, H, 32])
        filled = ph.sem("filled")
        x_loaded = [ph.sem(f"x_loaded{s}") for s in range(2)]
        hi_done = ph.sem("hi_done")
        rest_done = ph.sem("rest_done")
        mid_done = ph.sem("mid_done")
        parts_done = ph.sem("parts_done")
        v_out = ph.sem("v_out")
        stored = [ph.sem(f"stored{s}") for s in range(2)]
        block = ph.block()

        @block.sync
        def _(sp):
            for s in range(2):
                sp.sem_inc(stored[s], 16)
            def load(i, s):
                tok = at(sp, i * (2 * BLK) + s * BLK, BLK)
                wait_apart(sp, parts_done, i * 2 + (s + 1), filled, 1)
                wait_apart(sp, v_out, i * 2 + (s + 1), filled, 1)
                for j, src in ((0, qT), (KD, kT)):
                    sp.dma_start(x[:, s, j:j + KD], src[:, tok].rearrange("(k p) n -> p k n", p=P))\
                        .then_inc(x_loaded[s], 16)
                sp.dma_start(vin[:, s], v_in[tok, :].rearrange("(t p) c -> p t c", p=P))\
                    .then_inc(x_loaded[s], 16)
            load(0, 0)
            load_all(sp, load)
            for s in range(2):
                sp.wait_ge(stored[s], NBLK // 2 * 7 * 16 + 16)

        @block.scalar
        def _(act):
            def high(i, s):
                act.wait_ge(stored[s], i * (7 * 16) + 16)
                act.wait_ge(x_loaded[s], i * 48 + 48)
                nc.scalar.activation(parts[:, s, 0], x[:, s], ACT.Copy).then_inc(hi_done, 1)

            def body(i, s, last):
                if not last:
                    high(i + s, 1 - s)
                tok = at(act, i * (2 * BLK) + s * BLK, BLK)
                half = at(act, i * BLK + s * (BLK // 2), BLK // 2)
                wait_apart(act, parts_done, i * 2 + (s + 3), filled, 1)
                for j in range(2):
                    for a in range(3):
                        act.dma_start(qk_parts[j, a, :, half].rearrange("(k p) n -> p k n", p=P),
                                      parts[:, s, a, j * KD:(j + 1) * KD].bitcast(F32)).then_inc(stored[s], 16)
                wait_apart(act, v_out, i * 2 + (s + 3), filled, 1)
                act.dma_start(v_pad[tok, :].rearrange("(t p) c -> p t c", p=P),
                              vp[:, s].rearrange("p t h c -> p t (h c)")).then_inc(stored[s], 16)
            high(0, 0)
            paired(act, NBLK, body)

        @block.vector
        def _(dve):
            dve.sem_inc(v_out, 2)
            dve.wait_ge(filled, 1)

            def body(i, s, last):
                dve.wait_ge(hi_done, i * 2 + (s + 1))
                dve.wait_ge(x_loaded[s], i * 48 + 48)
                dve.wait_ge(parts_done, i * 2 + (s + 2))
                nc.vector.tensor_tensor(rest[:], x[:, s], parts[:, s, 0], ALU.subtract)\
                    .then_inc(rest_done, 1)
                dve.wait_ge(stored[s], i * (7 * 16) + 16)
                nc.vector.tensor_copy(vp[:, s, :, :, 0:DH],
                                      vin[:, s].rearrange("p t (h c) -> p t h c", c=DH))\
                    .then_inc(v_out, 1)
            paired(dve, NBLK, body)

        @block.gpsimd
        def _(pool):
            nc.gpsimd.memset(vp[:], 1.0).then_inc(filled, 1)
            pool.sem_inc(parts_done, 2)

            def body(i, s, last):
                wait_apart(pool, rest_done, i * 2 + (s + 1), filled, 1)
                nc.gpsimd.tensor_copy(parts[:, s, 1], rest[:]).then_inc(mid_done, 1)
                pool.wait_ge(mid_done, i * 2 + (s + 1))
                nc.gpsimd.tensor_tensor(parts[:, s, 2], rest[:], parts[:, s, 1],
                                        ALU.subtract).then_inc(parts_done, 1)
            paired(pool, NBLK, body)


def phase_moe(nc, x_in, xT, router_T, w1_T, w2_T, before, ident, y_sorted, positions, shares):
    with Phase(nc, "moe") as ph:
        NF = FFN // P
        NT = T // P
        NS = MOE_TILES
        BATCH = 8
        NB = 2 * NT // BATCH
        w1 = ph.sb("w1", [P, NE, KD, FFN])
        w2 = ph.sb("w2", [P, NE, NF, D])
        rw = ph.sb("rw", [P, KD, NE])
        idt = ph.sb("idt", [P, P])
        bef = ph.sb("bef", [P, P])
        ones = ph.sb("ones", [P, P])
        iota_e = ph.sb("iota_e", [P, NE])
        iota_t = ph.sb("iota_t", [P, NT])
        iota_s = ph.sb("iota_s", [P, NS])
        iota_p = ph.sb("iota_p", [P, P])
        token = ph.sb("token", [P, NT])
        xt = ph.sb("xt", [P, 2, KD, BLK])
        scores = ph.sb("scores", [P, NT, NE])
        top = ph.sb("top", [P, NT, NE])
        top_i = ph.sb("top_i", [P, NT, NE], U32)
        best = ph.sb("best", [P, NT, NE])
        gap = ph.sb("gap", [P, NT])
        odds = ph.sb("odds", [P, NT])
        one_more = ph.sb("one_more", [P, NT])
        share = ph.sb("share", [P, 2, NT])
        chosen = ph.sb("chosen", [P, 2, NT, NE])
        either = ph.sb("either", [P, NT, NE])
        scan = ph.sb("scan", [P, 2, NT, NE])
        counts_gt = ph.sb("counts_gt", [P, NE, NT])
        tiles = ph.sb("tiles", [P, NE])
        ends = ph.sb("ends", [P, 2, NE])
        starts = ph.sb("starts", [P, NE])
        past = ph.sb("past", [P, NS, NE])
        owner = ph.sb("owner", [P, NS])
        owner_i = ph.sb("owner_i", [P, NS], I32)
        pos_e = ph.sb("pos_e", [P, NT, NE])
        pos = ph.sb("pos", [P, 2, NT])
        pos_i = ph.sb("pos_i", [P, 2, NT], I32)
        low_i = ph.sb("low_i", [P, 2, NT], I32)
        high_i = ph.sb("high_i", [P, 2, NT], I32)
        low = ph.sb("low", [P, 2 * NT])
        high = ph.sb("high", [P, 2 * NT])
        hot_low = ph.sb("hot_low", [P, 2, BATCH, P])
        hot_high = ph.sb("hot_high", [P, 2, BATCH, NS])
        source = ph.sb("source", [P, NS], I32)
        cur = ph.sb("cur", [P, 2], I32)
        xg = ph.sb("xg", [P, 2, D])
        xgT = ph.sb("xgT", [P, 2, KD, P])
        h = ph.sb("h", [P, 2, FFN])
        hT = ph.sb("hT", [P, 2, NF, P])
        y = ph.sb("y", [P, 2, D])
        sc_ps = ph.ps("sc_ps", [P, 2, 256])
        rank_ps = ph.ps("rank_ps", [P, 2, NT, NE])
        xT_ps = ph.ps("xT_ps", [P, KD, 256])
        h_ps = ph.ps("h_ps", [P, 2, BLK])
        hT_ps = ph.ps("hT_ps", [P, NF, P])
        y_ps = ph.ps("y_ps", [P, BLK])
        consts = ph.sem("consts")
        NCONST = 16 * 3
        weights = ph.sem("weights")
        iotas = ph.sem("iotas")
        ones_set = ph.sem("ones_set")
        xt_loaded = [ph.sem(f"xt_loaded{s}") for s in range(2)]
        xt_free = ph.sem("xt_free")
        sc_done = ph.sem("sc_done")
        route = ph.sem("route")
        gap_done = ph.sem("gap_done")
        odds_done = ph.sem("odds_done")
        either_done = ph.sem("either_done")
        rank_done = ph.sem("rank_done")
        owner_done = ph.sem("owner_done")
        low_hot = ph.sem("low_hot")
        high_eq = ph.sem("high_eq")
        high_hot = ph.sem("high_hot")
        batch_used = ph.sem("batch_used")
        source_done = ph.sem("source_done")
        cur_set = ph.sem("cur_set")
        gathered = [ph.sem(f"gathered{s}") for s in range(2)]
        turned = ph.sem("turned")
        xT_out = ph.sem("xT_out")
        h_done = ph.sem("h_done")
        gelu_done = ph.sem("gelu_done")
        hT_done = ph.sem("hT_done")
        hT_out = ph.sem("hT_out")
        y_done = ph.sem("y_done")
        y_out = ph.sem("y_out")
        routes_stored = ph.sem("routes_stored")
        stored = [ph.sem(f"stored{s}") for s in range(2)]
        block = ph.block()

        @block.sync
        def _(sp):
            for s in range(2):
                sp.sem_inc(stored[s], 16)
            sp.dma_start(rw[:], router_T.rearrange("(k p) e -> p k e", p=P)).then_inc(consts, 16)
            sp.dma_start(bef[:], before).then_inc(consts, 16)
            sp.dma_start(idt[:], ident).then_inc(consts, 16)

            def load(i, s):
                tok = at(sp, i * (2 * BLK) + s * BLK, BLK)
                wait_apart(sp, xt_free, i * 2 + (s + 1), consts, NCONST)
                sp.dma_start(xt[:, s], xT[:, tok].rearrange("(k p) n -> p k n", p=P))\
                    .then_inc(xt_loaded[s], 16)
            with sp.Fori(0, NBLK // 2) as i:
                load(i, 0)
                load(i, 1)
            for e in range(NE):
                sp.dma_start(w1[:, e], w1_T[e].rearrange("(k p) f -> p k f", p=P)).then_inc(weights, 16)
                sp.dma_start(w2[:, e], w2_T[e].rearrange("(f p) c -> p f c", p=P)).then_inc(weights, 16)
            sp.wait_ge(route, ROUTE_STEPS)
            sp.dma_start(positions, pos_i[:].rearrange("p r t -> p (r t)")).then_inc(routes_stored, 16)
            sp.dma_start(shares, share[:].rearrange("p r t -> p (r t)")).then_inc(routes_stored, 16)

            def body(i, s, last):
                rows = at(sp, i * (2 * P) + s * P, P)
                wait_apart(sp, y_out, i * 2 + (s + 2), consts, NCONST)
                sp.dma_start(y_sorted[rows, :], y[:, s]).then_inc(stored[s], 16)
            paired(sp, NS, body)
            sp.wait_ge(routes_stored, 32)
            for s in range(2):
                sp.wait_ge(stored[s], NS // 2 * 16 + 16)

        @block.tensor
        def _(pe):
            pe.sem_inc(xt_free, 2)
            pe.wait_ge(consts, NCONST)
            for b in range(NBLK):
                pe.wait_ge(xt_loaded[b % 2], 16 * (b // 2 + 1))
                for t in range(TPB):
                    for k in range(KD):
                        tile = b * TPB + t
                        mm = nc.tensor.matmul(sc_ps[:, 0, tile * NE:(tile + 1) * NE],
                                              xt[:, b % 2, k, t * P:(t + 1) * P],
                                              rw[:, k], start=(k == 0), stop=(k == KD - 1))
                mm.then_inc(xt_free, 1)
            pe.drain().then_inc(sc_done, 1)
            pe.wait_ge(either_done, 1)
            pe.wait_ge(ones_set, 1)
            nc.tensor.matmul(rank_ps[:, 0], bef[:], either[:].rearrange("p t e -> p (t e)"), start=True, stop=True)
            nc.tensor.matmul(rank_ps[:, 1], ones[:], either[:].rearrange("p t e -> p (t e)"), start=True, stop=True)\
                .then_inc(rank_done, 1)
            for b in range(NB):
                pe.wait_ge(low_hot, b + 1)
                pe.wait_ge(high_hot, b + 1)
                for t in range(BATCH):
                    mm = nc.tensor.matmul(sc_ps[:, 1, 0:NS], hot_low[:, b % 2, t], hot_high[:, b % 2, t],
                                          start=(b == 0 and t == 0), stop=(b == NB - 1 and t == BATCH - 1))
                mm.then_inc(batch_used, 1)
            pe.wait_ge(weights, 16 * 2 * NE)
            pe.wait_ge(owner_done, 1)

            def expert(j):
                return pe.value_load(owner_i[0:1, j:j + 1] if isinstance(j, int) else owner_i[0:1, ds(pe.snap(j), 1)],
                                     min_val=0, max_val=NE - 1)

            def turn_x(i, s):
                pe.wait_ge(gathered[s], i * 16 + 16)
                pe.wait_ge(xT_out, i * 2 + (s + 1))
                for k in range(KD):
                    mm = nc.tensor.transpose(xT_ps[:, k, 0:P], xg[:, s, k * P:(k + 1) * P], idt[:])
                mm.then_inc(turned, 1)

            def first(i, s):
                e = expert(i * 2 + s)
                pe.wait_ge(xT_out, i * 2 + (s + 2))
                for c in range(2):
                    pe.wait_ge(gelu_done, i * 4 + (s * 2 + c + 1))
                    for k in range(KD):
                        mm = nc.tensor.matmul(h_ps[:, c], xgT[:, s, k],
                                              w1[:, ds(e, 1), k, c * BLK:(c + 1) * BLK].rearrange("p a n -> p (a n)"),
                                              start=(k == 0), stop=(k == KD - 1))
                    mm.then_inc(h_done, 1)

            def turn_h(i, s):
                pe.wait_ge(gelu_done, i * 4 + (s * 2 + 4))
                for c in range(2):
                    pe.wait_ge(hT_out, i * 4 + (s * 2 + c + 1))
                    for f in range(4 * c, 4 * c + 4):
                        mm = nc.tensor.transpose(hT_ps[:, f], h[:, s, f * P:(f + 1) * P], idt[:])
                    mm.then_inc(hT_done, 1)

            def second(i, s):
                e = expert(i * 2 + s)
                pe.wait_ge(hT_out, i * 4 + (s * 2 + 4))
                pe.wait_ge(y_out, i * 2 + (s + 1))
                for f in range(NF):
                    mm = nc.tensor.matmul(y_ps[:, 0:D], hT[:, s, f],
                                          w2[:, ds(e, 1), f].rearrange("p a n -> p (a n)"),
                                          start=(f == 0), stop=(f == NF - 1))
                mm.then_inc(y_done, 1)

            def step(i, s, left):
                if left >= 1:
                    first(i + s, 1 - s)
                if left >= 2:
                    turn_x(i + 1, s)
                second(i, s)
                if left >= 1:
                    turn_h(i + s, 1 - s)
            turn_x(0, 0)
            first(0, 0)
            turn_x(0, 1)
            turn_h(0, 0)
            with pe.Fori(0, NS // 2 - 1) as i:
                step(i, 0, 2)
                step(i, 1, 2)
            step(NS // 2 - 1, 0, 1)
            step(NS // 2 - 1, 1, 0)

        @block.scalar
        def _(act):
            act.sem_inc(xT_out, 1)
            act.sem_inc(gelu_done, 2)
            act.wait_ge(gap_done, 1)
            nc.scalar.activation(odds[:], gap[:], ACT.Exp).then_inc(odds_done, 1)

            def copy_x(i, s):
                act.wait_ge(turned, i * 2 + (s + 3))
                nc.scalar.activation(xgT[:, s], xT_ps[:, :, 0:P], ACT.Copy).then_inc(xT_out, 1)

            def body(i, s, last):
                for c in range(2):
                    act.wait_ge(h_done, i * 4 + (s * 2 + c + 1))
                    nc.scalar.activation(h[:, s, c * BLK:(c + 1) * BLK], h_ps[:, c], ACT.Gelu).then_inc(gelu_done, 1)
                if not last:
                    copy_x(i + s, 1 - s)
            copy_x(0, 0)
            paired(act, NS, body)

        @block.gpsimd
        def _(pool):
            pool.sem_inc(turned, 2)
            nc.gpsimd.memset(ones[:], 1.0).then_inc(ones_set, 1)
            for tile, n, base, step, lanes in ((iota_e, NE, 0, 1, 0), (iota_t, NT, 0, P, 0), (iota_s, NS, 0, 1, 0),
                                               (iota_p, P, 0, 1, 0), (token, NT, 0, P, 1)):
                op = nc.gpsimd.iota(tile[:], pattern=[[step, n]], base=base, channel_multiplier=lanes,
                                    allow_small_or_imprecise_dtypes=True)
            op.then_inc(iotas, 1)
            pool.wait_ge(iotas, 1)
            for b in range(NB):
                pool.wait_ge(high_eq, b + 1)
                t = b * BATCH % NT
                nc.gpsimd.tensor_tensor(hot_high[:, b % 2], hot_high[:, b % 2],
                                        token[:, t:t + BATCH].unsqueeze(2).broadcast_to([P, BATCH, NS]),
                                        ALU.mult).then_inc(high_hot, 1)
            pool.wait_ge(source_done, 1)

            def body(i, s, last):
                wait_apart(pool, turned, i * 2 + (s + 1), source_done, 1)
                nc.gpsimd.tensor_copy(cur[:, s:s + 1], source[:, i * 2 + s:i * 2 + s + 1] if isinstance(i, int)
                                      else source[:, ds(pool.snap(i * 2 + s), 1)]).then_inc(cur_set, 1)
                wait_apart(pool, cur_set, i * 2 + (s + 1), source_done, 1)
                nc.gpsimd.indirect_dma_start(xg[:, s], None, x_in, bass.IndirectOffsetOnAxis(ap=cur[:, s:s + 1], axis=0))\
                    .then_inc(gathered[s], 16)
            paired(pool, NS, body)

        def over(ap, *shape):
            return ap.broadcast_to([P, *shape])

        @block.vector
        def _(dve):
            dve.sem_inc(hT_out, 2)
            dve.sem_inc(y_out, 1)
            done = 0

            def link(op):
                nonlocal done
                done += 1
                op.then_inc(route, 1)
                dve.wait_ge(route, done)
            dve.wait_ge(iotas, 1)
            dve.wait_ge(sc_done, 1)
            link(nc.vector.tensor_copy(scores[:].rearrange("p t e -> p (t e)"), sc_ps[:, 0]))
            for t in range(NT):
                op = nc.vector.max(out=top[:, t], in_=scores[:, t])
            link(op)
            nc.vector.tensor_tensor(gap[:], top[:, :, 1], top[:, :, 0], ALU.subtract).then_inc(gap_done, 1)
            for t in range(NT):
                op = nc.vector.max_index(out=top_i[:, t], in_max=top[:, t], in_values=scores[:, t])
            link(op)
            link(nc.vector.tensor_copy(best[:], top_i[:]))
            for r in range(2):
                op = nc.vector.tensor_tensor(chosen[:, r], over(iota_e[:].unsqueeze(1), NT, NE),
                                             over(best[:, :, r:r + 1], NT, NE), ALU.is_equal)
            link(op)
            nc.vector.tensor_tensor(either[:], chosen[:, 0], chosen[:, 1], ALU.add).then_inc(either_done, 1)
            dve.wait_ge(odds_done, 1)
            link(nc.vector.tensor_scalar(one_more[:], odds[:], 1.0, None, ALU.add))
            link(nc.vector.reciprocal(share[:, 0], one_more[:]))
            link(nc.vector.tensor_tensor(share[:, 1], share[:, 0], odds[:], ALU.mult))
            dve.wait_ge(rank_done, 1)
            link(nc.vector.tensor_copy(scan[:, 0], rank_ps[:, 1]))
            a = 0
            d = 1
            while d < NT:
                nc.vector.tensor_copy(scan[:, 1 - a, 0:d], scan[:, a, 0:d])
                link(nc.vector.tensor_tensor(scan[:, 1 - a, d:NT], scan[:, a, d:NT], scan[:, a, 0:NT - d], ALU.add))
                a, d = 1 - a, 2 * d
            link(nc.vector.tensor_tensor(counts_gt[:], over(scan[:, a, NT - 1].unsqueeze(2), NE, NT),
                                         over(iota_t[:].unsqueeze(1), NE, NT), ALU.is_gt))
            link(nc.vector.tensor_reduce(tiles[:], counts_gt[:], axis=AX.X, op=ALU.add))
            b = 0
            link(nc.vector.tensor_copy(ends[:, 0], tiles[:]))
            for d in (1, 2, 4):
                nc.vector.tensor_copy(ends[:, 1 - b, 0:d], ends[:, b, 0:d])
                link(nc.vector.tensor_tensor(ends[:, 1 - b, d:NE], ends[:, b, d:NE], ends[:, b, 0:NE - d], ALU.add))
                b = 1 - b
            link(nc.vector.tensor_tensor(past[:], over(iota_s[:].unsqueeze(2), NS, NE),
                                         over(ends[:, b].unsqueeze(1), NS, NE), ALU.is_ge))
            link(nc.vector.tensor_reduce(owner[:], past[:], axis=AX.X, op=ALU.add))
            link(nc.vector.tensor_scalar(owner[:], owner[:], float(NE - 1), None, ALU.min))
            nc.vector.tensor_copy(owner_i[:], owner[:]).then_inc(owner_done, 1)
            link(nc.vector.tensor_tensor(starts[:], ends[:, b], tiles[:], ALU.subtract))
            link(nc.vector.tensor_scalar(starts[:], starts[:], float(P), None, ALU.mult))
            link(nc.vector.tensor_tensor(pos_e[:], scan[:, a], rank_ps[:, 1], ALU.subtract))
            link(nc.vector.tensor_tensor(pos_e[:], pos_e[:], rank_ps[:, 0], ALU.add))
            link(nc.vector.tensor_tensor(pos_e[:], pos_e[:], over(starts[:].unsqueeze(1), NT, NE), ALU.add))
            for r in range(2):
                op = nc.vector.tensor_tensor(chosen[:, r], chosen[:, r], pos_e[:], ALU.mult)
            link(op)
            link(nc.vector.tensor_reduce(pos[:], chosen[:], axis=AX.X, op=ALU.add))
            link(nc.vector.tensor_copy(pos_i[:], pos[:]))
            nc.vector.tensor_scalar(low_i[:], pos_i[:], P - 1, None, ALU.bitwise_and)
            link(nc.vector.tensor_scalar(high_i[:], pos_i[:], P.bit_length() - 1, None, ALU.logical_shift_right))
            nc.vector.tensor_copy(high[:], high_i[:].rearrange("p r t -> p (r t)"))
            link(nc.vector.tensor_copy(low[:], low_i[:].rearrange("p r t -> p (r t)")))
            assert done == ROUTE_STEPS, done
            for b in range(NB):
                if b >= 2:
                    dve.wait_ge(batch_used, b - 1)
                nc.vector.tensor_tensor(hot_low[:, b % 2], over(iota_p[:].unsqueeze(1), BATCH, P),
                                        over(low[:, b * BATCH:(b + 1) * BATCH].unsqueeze(2), BATCH, P),
                                        ALU.is_equal).then_inc(low_hot, 1)
                nc.vector.tensor_tensor(hot_high[:, b % 2], over(iota_s[:].unsqueeze(1), BATCH, NS),
                                        over(high[:, b * BATCH:(b + 1) * BATCH].unsqueeze(2), BATCH, NS),
                                        ALU.is_equal).then_inc(high_eq, 1)
            dve.wait_ge(batch_used, NB)
            nc.vector.tensor_copy(source[:], sc_ps[:, 1, 0:NS]).then_inc(source_done, 1)

            def body(i, s, last):
                for c in range(2):
                    dve.wait_ge(hT_done, i * 4 + (s * 2 + c + 1))
                    nc.vector.tensor_copy(hT[:, s, 4 * c:4 * c + 4], hT_ps[:, 4 * c:4 * c + 4]).then_inc(hT_out, 1)
                dve.wait_ge(y_done, i * 2 + (s + 1))
                dve.wait_ge(stored[s], i * 16 + 16)
                nc.vector.tensor_copy(y[:, s], y_ps[:, 0:D]).then_inc(y_out, 1)
            paired(dve, NS, body)


def phase_experts(nc, x_in, xT, gate_w, gate_b, expert_w, expert_b, ident, x_out):
    with Phase(nc, "ffn") as ph:
        EP = NE // 2
        w = ph.sb("w", [P, KD, EP, 2, D])
        eb = ph.sb("eb", [NE, D])
        gw = ph.sb("gw", [P, KD, NE])
        gb = ph.sb("gb", [P, NE])
        idt = ph.sb("idt", [P, P])
        xt = ph.sb("xt", [P, 2, KD, BLK])
        x = ph.sb("x", [P, 2, TPB, D])
        lg = ph.sb("lg", [P, TPB, NE])
        mx = ph.sb("mx", [P, TPB])
        ex = ph.sb("ex", [P, TPB, NE])
        sm = ph.sb("sm", [P, TPB])
        rs = ph.sb("rs", [P, TPB])
        gate = ph.sb("gate", [P, TPB, NE])
        sel = ph.sb("sel", [P, TPB, NE])
        nil = ph.sb("nil", [P, TPB])
        we = ph.sb("we", [P, 2, TPB, NE])
        weT = ph.sb("weT", [NE, TPB, P])
        acc = ph.sb("acc", [P, 2, TPB, D])
        power = ph.sb("power", [P, TPB])
        stats = ph.sb("stats", [P, TPB, 6])
        mv = ph.sb("mv", [P, TPB, 2])
        vare = ph.sb("vare", [P, TPB])
        rstd = ph.sb("rstd", [P, TPB])
        xo = ph.sb("xo", [P, 2, TPB, D])
        y_ps = ph.ps("y_ps", [P, 4, 2, D])
        b_ps = ph.ps("b_ps", [P, TPB, D])
        lg_ps = ph.ps("lg_ps", [P, TPB, P])
        wT_ps = ph.ps("wT_ps", [P, TPB, P])
        consts = ph.sem("consts")
        NCONST = 16 * (4 + NE)
        loaded = [ph.sem(f"loaded{s}") for s in range(2)]
        in_free = ph.sem("in_free")
        lg_done = ph.sem("lg_done")
        step = ph.sem("step")
        shift_done = ph.sem("shift_done")
        exp_done = ph.sem("exp_done")
        we_done = ph.sem("we_done")
        wT_done = ph.sem("wT_done")
        wT_out = ph.sem("wT_out")
        b_done = ph.sem("b_done")
        b_out = ph.sem("b_out")
        y_done = ph.sem("y_done")
        half_done = ph.sem("half_done")
        y_out = ph.sem("y_out")
        power_set = ph.sem("power_set")
        stats_done = ph.sem("stats_done")
        mv_done = ph.sem("mv_done")
        vare_done = ph.sem("vare_done")
        rstd_done = ph.sem("rstd_done")
        normed = ph.sem("normed")
        stored = [ph.sem(f"stored{s}") for s in range(2)]
        block = ph.block()
        NY = TPB * EP

        @block.sync
        def _(sp):
            for s in range(2):
                sp.sem_inc(stored[s], 16)
            def load(i, s):
                tok = at(sp, i * (2 * BLK) + s * BLK, BLK)
                wait_apart(sp, in_free, i * 2 + (s + 1), consts, NCONST)
                sp.dma_start(xt[:, s], xT[:, tok].rearrange("(k p) n -> p k n", p=P)).then_inc(loaded[s], 16)
                sp.dma_start(x[:, s], x_in[tok, :].rearrange("(t p) c -> p t c", p=P)).then_inc(loaded[s], 16)
            load(0, 0)
            sp.dma_start(eb[:], expert_b).then_inc(consts, 16)
            sp.dma_start(gw[:], gate_w.rearrange("(k p) e -> p k e", p=P)).then_inc(consts, 16)
            sp.dma_start(gb[:], gate_b.partition_broadcast(P)).then_inc(consts, 16)
            sp.dma_start(idt[:], ident).then_inc(consts, 16)
            for e in range(NE):
                sp.dma_start(w[:, :, e // 2, e % 2], expert_w[e].rearrange("(k p) c -> p k c", p=P))\
                    .then_inc(consts, 16)

            def body(i, s, last):
                if not last:
                    load(i + s, 1 - s)
                tok = at(sp, i * (2 * BLK) + s * BLK, BLK)
                wait_apart(sp, normed, i * 2 + (s + 1), consts, NCONST)
                sp.dma_start(x_out[tok, :].rearrange("(t p) c -> p t c", p=P), xo[:, s]).then_inc(stored[s], 16)
            paired(sp, NBLK, body)
            for s in range(2):
                sp.wait_ge(stored[s], NBLK // 2 * 16 + 16)

        @block.tensor
        def _(pe):
            pe.wait_ge(consts, NCONST)

            def logits(i, s):
                pe.wait_ge(loaded[s], i * 32 + 32)
                for t in range(TPB):
                    for k in range(KD):
                        mm = nc.tensor.matmul(lg_ps[:, t, 0:NE], xt[:, s, k, t * P:(t + 1) * P], gw[:, k],
                                              start=(k == 0), stop=(k == KD - 1))
                mm.then_inc(lg_done, 1)

            def turn_weights(i, s):
                pe.wait_ge(we_done, i * 2 + (s + 1))
                for t in range(TPB):
                    mm = nc.tensor.transpose(wT_ps[0:NE, t], we[:, s, t], idt[:])
                mm.then_inc(wT_done, 1)

            def product(i, s, m):
                pe.wait_ge(y_out, i * (2 * NY) + (s * NY + m + 1))
                g, t = divmod(m, TPB)
                for k in range(KD):
                    mm = nc.tensor.matmul(y_ps[:, m % 4], xt[:, s, k, t * P:(t + 1) * P], w[:, k, g],
                                          start=(k == 0), stop=(k == KD - 1))
                mm.then_inc(y_done, 1)

            def body(i, s, last):
                for m in range(NY):
                    product(i, s, m)
                    if m == NY - 2 and not last:
                        turn_weights(i + s, 1 - s)
                    if m == 0:
                        pe.wait_ge(wT_out, i * 2 + (s + 1))
                        pe.wait_ge(b_out, i * 2 + (s + 1))
                        for t in range(TPB):
                            mm = nc.tensor.matmul(b_ps[:, t], weT[:, t], eb[:], start=True, stop=True)
                        mm.then_inc(b_done, 1)
                    if m == NY // 2 and not last:
                        logits(i + s, 1 - s)
                pe.drain().then_inc(in_free, 1)
            logits(0, 0)
            turn_weights(0, 0)
            paired(pe, NBLK, body)

        @block.scalar
        def _(act):
            def body(i, s, last):
                act.wait_ge(shift_done, i * 2 + (s + 1))
                nc.scalar.activation(ex[:], lg[:], ACT.Exp).then_inc(exp_done, 1)
                act.wait_ge(wT_done, i * 2 + (s + 1))
                act.wait_ge(b_done, i * 2 + (s + 1))
                nc.scalar.activation(weT[:], wT_ps[0:NE], ACT.Copy).then_inc(wT_out, 1)
            paired(act, NBLK, body)

        def each(ap):
            return ap.unsqueeze(2).broadcast_to([P, TPB, NE])

        @block.vector
        def _(dve):
            dve.sem_inc(in_free, 2)
            dve.sem_inc(y_out, 4)
            dve.sem_inc(b_out, 1)
            dve.sem_inc(b_done, 1)
            dve.wait_ge(consts, NCONST)
            STEPS = 11

            def gates(i, s):
                n = i * 2 + s
                done = 0

                def link(op):
                    nonlocal done
                    done += 1
                    op.then_inc(step, 1)
                    dve.wait_ge(step, n * STEPS + done)
                dve.wait_ge(lg_done, n + 1)
                link(nc.vector.tensor_tensor(lg[:], lg_ps[:, :, 0:NE],
                                             gb[:].unsqueeze(1).broadcast_to([P, TPB, NE]), ALU.add))
                link(nc.vector.tensor_reduce(mx[:], lg[:], axis=AX.X, op=ALU.max))
                nc.vector.tensor_tensor(lg[:], lg[:], each(mx[:]), ALU.subtract).then_inc(shift_done, 1)
                dve.wait_ge(exp_done, n + 1)
                link(nc.vector.tensor_reduce(sm[:], ex[:], axis=AX.X, op=ALU.add))
                link(nc.vector.reciprocal(rs[:], sm[:]))
                link(nc.vector.tensor_tensor(gate[:], ex[:], each(rs[:]), ALU.mult))
                link(nc.vector.tensor_scalar(sel[:], gate[:], 0.1, None, ALU.is_ge))
                link(nc.vector.tensor_tensor(gate[:], gate[:], sel[:], ALU.mult))
                link(nc.vector.tensor_reduce(sm[:], gate[:], axis=AX.X, op=ALU.add))
                link(nc.vector.tensor_scalar(nil[:], sm[:], 0.0, None, ALU.is_equal))
                link(nc.vector.tensor_tensor(sm[:], sm[:], nil[:], ALU.add))
                link(nc.vector.reciprocal(rs[:], sm[:]))
                nc.vector.tensor_tensor(we[:, s], gate[:], each(rs[:]), ALU.mult).then_inc(we_done, 1)

            def statistics(n, s):
                dve.wait_ge(y_out, n * NY + (NY + 4))
                for t in range(TPB):
                    op = nc.vector.bn_stats(stats[:, t], acc[:, s, t])
                op.then_inc(stats_done, 1)
                wait_apart(dve, stats_done, n + 1, consts, NCONST)
                for t in range(TPB):
                    op = nc.vector.bn_aggr(mv[:, t], stats[:, t])
                op.then_inc(mv_done, 1)

            def normalise(n, i, s):
                dve.wait_ge(stored[s], i * 16 + 16)
                dve.wait_ge(mv_done, n + 1)
                dve.wait_ge(rstd_done, n + 1)
                for t in range(TPB):
                    op = nc.vector.tensor_scalar(xo[:, s, t], acc[:, s, t], mv[:, t, 0:1], rstd[:, t:t + 1],
                                                 ALU.subtract, ALU.mult)
                op.then_inc(normed, 1)

            def body(i, s, first, last):
                n = i * 2 + s
                dve.wait_ge(loaded[s], i * 32 + 32)
                dve.wait_ge(b_done, n + 2)
                nc.vector.tensor_tensor(acc[:, s], b_ps[:], x[:, s], ALU.add).then_inc(b_out, 1)
                dve.wait_ge(b_out, n + 2)
                for m in range(0, NY, 2):
                    g, t = divmod(m, TPB)
                    if g:
                        dve.wait_ge(y_out, i * (2 * NY) + (s * NY + m + 2))
                    for e in range(2):
                        for d in range(2):
                            if e == 0:
                                dve.wait_ge(y_done, i * (2 * NY) + (s * NY + m + d + 1))
                            else:
                                dve.wait_ge(half_done, i * (2 * NY) + (s * NY + m + d + 1))
                            nc.vector.scalar_tensor_tensor(acc[:, s, t + d], y_ps[:, (m + d) % 4, e],
                                                           we[:, s, t + d, 2 * g + e:2 * g + e + 1],
                                                           acc[:, s, t + d], ALU.mult, ALU.add)\
                                .then_inc(y_out if e else half_done, 1)
                    if m == 2 and not first:
                        normalise(n - 1, i + s - 1, 1 - s)
                    if m == NY * 5 // 8 and not last:
                        gates(i + s, 1 - s)
                statistics(n, s)
            gates(0, 0)
            paired_first(dve, NBLK, body)
            normalise(NBLK - 1, NBLK // 2 - 1, 1)

        @block.gpsimd
        def _(pool):
            nc.gpsimd.memset(power[:], -0.5).then_inc(power_set, 1)

            def body(i, s, last):
                wait_apart(pool, mv_done, i * 2 + (s + 1), power_set, 1)
                nc.gpsimd.tensor_scalar(vare[:], mv[:, :, 1], LN_EPS, None, ALU.add).then_inc(vare_done, 1)
                pool.wait_ge(vare_done, i * 2 + (s + 1))
                nc.gpsimd.tensor_tensor(rstd[:], vare[:], power[:], ALU.pow).then_inc(rstd_done, 1)
            paired(pool, NBLK, body)


def window_masks():
    p, n = np.arange(P)[:, None], np.arange(P)[None, :]
    masked = np.stack([n > p, n < p, n > p, n < p])
    return np.where(masked, -1e30, 0.0).astype(np.float32)


def bass_decoder_layers(nc, a):
    def scratch(name, *shape):
        return nc.dram_tensor(f"scratch_{name}", list(shape), F32, kind="Internal").ap()

    qk_parts = scratch("qk_parts", 2, 3, D, T // 2)
    v_pad = scratch("v_pad", T, H * 32)
    o_T = scratch("o_T", QUADS, P, T)
    x1, x1T = scratch("x1", T, D), scratch("x1T", D, T)
    x2, x2T = scratch("x2", T, D), scratch("x2T", D, T)
    x3, x3T = scratch("x3", T, D), scratch("x3T", D, T)
    x4, x4T = scratch("x4", T, D), scratch("x4T", D, T)
    x5, x5T = scratch("x5", T, D), scratch("x5T", D, T)
    cross_T = scratch("cross_T", DM // P, P, T)
    routes = (scratch("y_sorted", MOE_TILES * P, D),
              nc.dram_tensor("scratch_positions", [P, 2 * T // P], I32, kind="Internal").ap(),
              scratch("shares", P, 2 * T // P))
    gate, z_T = scratch("gate", T, D), scratch("z_T", KD, P, T)

    phase_qkv(nc, a["xT"], a["w_qkv"], a["b_qkv"], qk_parts, v_pad)
    phase_core(nc, "self", qk_parts, v_pad, a["ident"], o_T, DH ** -0.5)
    phase_post(nc, "post0", o_T, QUADS, a["w_proj"], True, a["b_proj"], a["x"], a["ident"], x1, x1T)
    phase_cross(nc, x1T, a["ctxT"], a["Wq"], a["bq"], a["Wk"], a["bk"], a["Wv"], a["bv"], a["ident"], cross_T)
    phase_post(nc, "post1", cross_T, DM // P, a["Wu"], False, a["bu"], x1, a["ident"], x2, x2T)
    phase_moe(nc, x2, x2T, a["router_T"], a["w1_T"], a["w2_T"], a["before"], a["ident"], *routes)
    phase_post(nc, "post2", None, 0, None, False, None, x2, a["ident"], x3, x3T, routes)
    phase_rwkv_in(nc, x3T, [a["maa_r"], a["maa_k"], a["maa_v"], a["maa_g"]],
                  [a["WrT"], a["WkT"], a["WvT"], a["WgT"]], qk_parts, v_pad, gate)
    phase_rwkv_core(nc, qk_parts, v_pad, a["decay"], a["faaaa"], a["diag"], o_T)
    phase_group_norm(nc, o_T, a["identity"], a["ln_w"], a["ln_b"], gate, a["ident"], z_T)
    phase_post(nc, "post3", z_T, KD, a["WoT"], False, None, x3, a["ident"], x4, x4T)
    phase_split(nc, x4T, a["ctxT"], a["ctx"], qk_parts, v_pad)
    phase_core(nc, "window", qk_parts, v_pad, a["ident"], o_T, 1.0, a["masks"])
    phase_post(nc, "post4", o_T, QUADS, a["identity"], True, None, x4, a["ident"], x5, x5T)
    phase_experts(nc, x5, x5T, a["gate_w"], a["gate_b"], a["expert_w"], a["expert_b"], a["ident"],
                  a["out"])


def kernel(**inputs):
    import concourse.bacc as _bacc
    from concourse.bass_utils import run_bass_kernel_spmd as _run

    i = {name: np.asarray(value) for name, value in inputs.items()}
    x, ctx = i["x"].reshape(T, D), i["ctx_1024"].reshape(T, D)
    layout = dict(
        x=x, xT=x.T, ctx=ctx, ctxT=ctx.T,
        w_qkv=i["L0_attn_w_qkv"], b_qkv=i["L0_attn_b_qkv"], w_proj=i["L0_attn_w_proj"], b_proj=i["L0_attn_b_proj"],
        Wq=i["L0_xattn_Wq"], bq=i["L0_xattn_bq"], Wk=i["L0_xattn_Wk"], bk=i["L0_xattn_bk"],
        Wv=i["L0_xattn_Wv"], bv=i["L0_xattn_bv"], Wu=i["L0_xattn_Wu"], bu=i["L0_xattn_bu"],
        router_T=i["L0_ffn_router_w"].T, w1_T=i["L0_ffn_expert_w1"].transpose(0, 2, 1),
        w2_T=i["L0_ffn_expert_w2"].transpose(0, 2, 1),
        maa_r=i["L1_attn_time_maa_r"], maa_k=i["L1_attn_time_maa_k"],
        maa_v=i["L1_attn_time_maa_v"], maa_g=i["L1_attn_time_maa_g"],
        decay=i["L1_attn_time_decay"], faaaa=i["L1_attn_time_faaaa"],
        WrT=i["L1_attn_Wr"].T, WkT=i["L1_attn_Wk"].T, WvT=i["L1_attn_Wv"].T, WgT=i["L1_attn_Wg"].T,
        WoT=i["L1_attn_Wo"].T, ln_w=i["L1_attn_ln_w"], ln_b=i["L1_attn_ln_b"],
        gate_w=i["L1_ffn_gate_w"], gate_b=i["L1_ffn_gate_b"],
        expert_w=i["L1_ffn_expert_w"], expert_b=i["L1_ffn_expert_b"],
        ident=np.eye(P, dtype=np.float32),
        before=np.triu(np.ones((P, P), np.float32), 1),
        identity=np.eye(D, dtype=np.float32), diag=np.eye(P, S, dtype=np.float32), masks=window_masks(),
    )
    nc = _bacc.Bacc("TRN2", target_bir_lowering=False, num_devices=1)
    arrays, args = {}, {}
    for name, value in layout.items():
        value = np.ascontiguousarray(value)
        arrays[f"in_{name}"] = value
        args[name] = nc.dram_tensor(f"in_{name}", value.shape, mybir.dt.from_np(value.dtype),
                                    kind="ExternalInput").ap()
    args["out"] = nc.dram_tensor("out", (T, D), F32, kind="ExternalOutput").ap()
    bass_decoder_layers(nc, args)
    r = _run(nc, [arrays], core_ids=[0])
    return r.results[0]["out"].reshape(B, S, D)
```

```python
import numpy as np
import concourse.bass as bass
from concourse import mybir
from contextlib import ExitStack

F32 = mybir.dt.float32
BF16 = mybir.dt.bfloat16
U32 = mybir.dt.uint32
I32 = mybir.dt.int32
ALU = mybir.AluOpType
ACT = mybir.ActivationFunctionType
AX = mybir.AxisListType
ds = bass.ds

P = 128
D = 256
KD = D // P
B = 16
S = 256
T = B * S
H = 16
DH = D // H
QUADS = H // 4
BLK = 512
NBLK = T // BLK
TPB = BLK // P
DX = 64
DM = H * DX
NE = 8
FFN = 1024
MOE_TILES = 2 * T // P + NE
ROUTE_STEPS = 33
LN_EPS = 1e-5
GN_EPS = 1e-5 * 64

Q_PARTS = (0, 0, 0, 1, 1, 2)
K_PARTS = (0, 1, 2, 0, 1, 0)
ROWS = len(Q_PARTS) * DH
MAX_ROWS = 2


class Phase:

    def __init__(self, nc, name):
        self.nc, self.name, self.stack, self.sems = nc, name, ExitStack(), []

    def __enter__(self):
        self.stack.__enter__()
        return self

    def __exit__(self, *a):
        done = self.stack.__exit__(*a)
        self.nc.clear_and_free_semaphores(self.sems)
        self.nc.all_engine_barrier()
        return done

    def sb(self, name, shape, dt=F32):
        return self.stack.enter_context(self.nc.sbuf_tensor(f"{self.name}_{name}", shape, dt))

    def ps(self, name, shape, dt=F32):
        return self.stack.enter_context(self.nc.psum_tensor(f"{self.name}_{name}", shape, dt))

    def sem(self, name):
        self.sems.append(self.nc.alloc_semaphore(name=f"{self.name}_{name}"))
        return self.sems[-1]

    def block(self):
        return self.stack.enter_context(self.nc.Block())


def paired(eng, count, body):
    with eng.Fori(0, count // 2 - 1) as i:
        body(i, 0, False)
        body(i, 1, False)
    body(count // 2 - 1, 0, False)
    body(count // 2 - 1, 1, True)


def paired_first(eng, count, body):
    body(0, 0, True, False)
    body(0, 1, False, False)
    with eng.Fori(1, count // 2 - 1) as i:
        body(i, 0, False, False)
        body(i, 1, False, False)
    body(count // 2 - 1, 0, False, False)
    body(count // 2 - 1, 1, False, True)


def load_all(sp, load):
    load(0, 1)
    with sp.Fori(1, NBLK // 2) as i:
        load(i, 0)
        load(i, 1)


def at(eng, start, size):
    return slice(start, start + size) if isinstance(start, int) else ds(eng.snap(start), size)


def wait_apart(eng, sem, value, met, met_value):
    if not isinstance(value, int):
        value = eng.to_reg(value)
        eng.wait_ge(met, met_value)
    eng.wait_ge(sem, value)


def phase_qkv(nc, xT, w_qkv, b_qkv, qk_parts, v_pad):
    with Phase(nc, "qkv") as ph:
        w = ph.sb("w", [P, KD, 3 * D])
        bqk = ph.sb("bqk", [P, 4])
        bv = ph.sb("bv", [P, 2, D])
        x = ph.sb("x", [P, 2, KD, BLK])
        parts = ph.sb("parts", [P, 2, 4, 3, BLK], BF16)
        rest = ph.sb("rest", [P, 2, BLK])
        vp = ph.sb("vp", [P, 2, TPB, H, 32])
        qk_ps = ph.ps("qk_ps", [P, 4, BLK])
        v_ps = ph.ps("v_ps", [P, TPB, D])
        consts = ph.sem("consts")
        x_loaded = [ph.sem(f"x_loaded{s}") for s in range(2)]
        x_free = ph.sem("x_free")
        qk_done = ph.sem("qk_done")
        hi_done = ph.sem("hi_done")
        rest_done = ph.sem("rest_done")
        mid_done = ph.sem("mid_done")
        parts_done = ph.sem("parts_done")
        v_filled = ph.sem("v_filled")
        v_done = ph.sem("v_done")
        v_out = ph.sem("v_out")
        stored = [ph.sem(f"stored{s}") for s in range(2)]
        block = ph.block()

        @block.sync
        def _(sp):
            for s in range(2):
                sp.sem_inc(stored[s], 16)
            def load(i, s):
                tok = at(sp, i * (2 * BLK) + s * BLK, BLK)
                wait_apart(sp, x_free, i * 2 + (s + 1), consts, 64)
                sp.dma_start(x[:, s], xT[:, tok]
                             .rearrange("(k p) n -> p k n", p=P)).then_inc(x_loaded[s], 16)
            load(0, 0)
            sp.dma_start(w[:], w_qkv.rearrange("(k p) n -> p k n", p=P)).then_inc(consts, 16)
            sp.dma_start(bqk[:], b_qkv[0:2 * D].rearrange("(m p) -> p m", p=P),
                         allow_slow_non_contiguous=True).then_inc(consts, 16)
            for t in range(2):
                sp.dma_start(bv[:, t], b_qkv[2 * D:3 * D].partition_broadcast(P)).then_inc(consts, 16)

            def body(i, s, last):
                if not last:
                    load(i + s, 1 - s)
                tok = at(sp, i * (2 * BLK) + s * BLK, BLK)
                half = at(sp, i * BLK + s * (BLK // 2), BLK // 2)
                for m in range(4):
                    wait_apart(sp, parts_done, i * 8 + (s * 4 + m + 3), consts, 64)
                    sp.dma_start(qk_parts[m // 2, :, (m % 2) * P:(m % 2 + 1) * P, half]
                                 .rearrange("a p n -> p a n"), parts[:, s, m].bitcast(F32)).then_inc(stored[s], 16)
                wait_apart(sp, v_out, i * 4 + (s * 2 + 4), consts, 64)
                sp.dma_start(v_pad[tok, :].rearrange("(t p) c -> p t c", p=P),
                             vp[:, s].rearrange("p t h c -> p t (h c)")).then_inc(stored[s], 16)

            paired(sp, NBLK, body)
            for s in range(2):
                sp.wait_ge(stored[s], NBLK // 2 * 5 * 16 + 16)

        @block.tensor
        def _(pe):
            pe.sem_inc(x_free, 2)
            pe.wait_ge(consts, 64)

            def body(i, s, last):
                pe.wait_ge(x_loaded[s], i * 16 + 16)
                for m in range(4):
                    pe.wait_ge(rest_done, i * 8 + (s * 4 + m + 1))
                    for k in range(KD):
                        mm = nc.tensor.matmul(qk_ps[:, m], w[:, k, m * P:(m + 1) * P], x[:, s, k],
                                              start=(k == 0), stop=(k == KD - 1))
                    mm.then_inc(qk_done, 1)
                for t in range(TPB):
                    if t % 2 == 0:
                        pe.wait_ge(v_out, i * 4 + (s * 2 + t // 2 + 1))
                    for k in range(KD):
                        mm = nc.tensor.matmul(v_ps[:, t], x[:, s, k, t * P:(t + 1) * P],
                                              w[:, k, 2 * D:3 * D], start=(k == 0), stop=(k == KD - 1))
                    if t % 2:
                        mm.then_inc(v_done, 1)
                pe.drain().then_inc(x_free, 1)
            paired(pe, NBLK, body)

        @block.scalar
        def _(act):
            act.wait_ge(consts, 64)

            def body(i, s, last):
                act.wait_ge(stored[s], i * (5 * 16) + 16)
                for m in range(4):
                    act.wait_ge(qk_done, i * 8 + (s * 4 + m + 1))
                    nc.scalar.activation(parts[:, s, m, 0], qk_ps[:, m], ACT.Identity,
                                         bias=bqk[:, m:m + 1]).then_inc(hi_done, 1)
            paired(act, NBLK, body)

        @block.vector
        def _(dve):
            dve.sem_inc(rest_done, 4)
            dve.sem_inc(v_out, 2)
            dve.wait_ge(v_filled, 1)

            def body(i, s, last):
                for m in range(4):
                    dve.wait_ge(hi_done, i * 8 + (s * 4 + m + 1))
                    dve.wait_ge(parts_done, i * 8 + (s * 4 + m + 1))
                    nc.vector.scalar_tensor_tensor(rest[:, m % 2], qk_ps[:, m], bqk[:, m:m + 1],
                                                   parts[:, s, m, 0], ALU.add, ALU.subtract)\
                        .then_inc(rest_done, 1)
                dve.wait_ge(stored[s], i * (5 * 16) + 16)
                for t in (0, 2):
                    dve.wait_ge(v_done, i * 4 + (s * 2 + t // 2 + 1))
                    nc.vector.tensor_tensor(vp[:, s, t:t + 2, :, 0:DH],
                                            v_ps[:, t:t + 2].rearrange("p t (h c) -> p t h c", c=DH),
                                            bv[:].rearrange("p t (h c) -> p t h c", c=DH),
                                            ALU.add).then_inc(v_out, 1)
            paired(dve, NBLK, body)

        @block.gpsimd
        def _(pool):
            nc.gpsimd.memset(vp[:], 1.0).then_inc(v_filled, 1)
            pool.sem_inc(parts_done, 2)

            def body(i, s, last):
                for m in range(4):
                    wait_apart(pool, rest_done, i * 8 + (s * 4 + m + 5), v_filled, 1)
                    nc.gpsimd.tensor_copy(parts[:, s, m, 1], rest[:, m % 2]).then_inc(mid_done, 1)
                    pool.wait_ge(mid_done, i * 8 + (s * 4 + m + 1))
                    nc.gpsimd.tensor_tensor(parts[:, s, m, 2], rest[:, m % 2], parts[:, s, m, 1],
                                            ALU.subtract).then_inc(parts_done, 1)
            paired(pool, NBLK, body)


def phase_core(nc, name, qk_parts, v_pad, ident_in, out_T, scale, window_masks=None):
    with Phase(nc, name) as ph:
        q6 = ph.sb("q6", [P, 2, H, S], BF16)
        k6 = ph.sb("k6", [P, 2, H, S], BF16)
        v = ph.sb("v", [P, 2, 2, H * 32])
        consts_f32 = ph.sb("consts_f32", [P, 5, P])
        ident = ph.sb("ident", [P, P], BF16)
        masks = ph.sb("masks", [P, 4, P], BF16)
        nmax = ph.sb("nmax", [P, 2, 4])
        mparts = ph.sb("mparts", [P, 2, 4, MAX_ROWS], BF16)
        probs = ph.sb("probs", [P, 2, 4, 2, S])
        o_sb = ph.sb("o_sb", [P, 2, S])
        o_turned = ph.sb("o_turned", [P, 2, S])
        rsum = ph.sb("rsum", [P, 2, S // 32])
        o_scaled = ph.sb("o_scaled", [P, 2, S])
        o_norm = ph.sb("o_norm", [P, 2, S])
        s_ps = ph.ps("s_ps", [P, 2, 2, 2, S])
        t_ps = ph.ps("t_ps", [P, 2, 2, S])
        m_ps = ph.ps("m_ps", [P, 4, P])
        o_ps = ph.ps("o_ps", [P, S])
        consts = ph.sem("consts")
        filled = ph.sem("filled")
        ones_set = ph.sem("ones_set")
        loaded = [ph.sem(f"loaded{s}") for s in range(2)]
        batch_done = ph.sem("batch_done")
        s_done = ph.sem("s_done")
        max_done = ph.sem("max_done")
        hi_done = ph.sem("hi_done")
        mparts_done = ph.sem("mparts_done")
        mrow_done = ph.sem("mrow_done")
        mcopied = ph.sem("mcopied")
        t_done = ph.sem("t_done")
        t_free = ph.sem("t_free")
        pv_done = ph.sem("pv_done")
        o_copied = ph.sem("o_copied")
        turned = ph.sem("turned")
        rsum_done = ph.sem("rsum_done")
        scaled = ph.sem("scaled")
        o_ready = ph.sem("o_ready")
        stored = [ph.sem(f"stored{s}") for s in range(2)]
        block = ph.block()
        nload = 13
        n_masks = 0 if window_masks is None else 1
        NCONST = 16 * (1 + n_masks)
        PAIRS = H // 2

        def blocks(ap):
            return ap.rearrange("p (b r) -> p b r", r=32)

        @block.sync
        def _(sp):
            for s in range(2):
                sp.sem_inc(stored[s], 16)
            def load(tok, half, s):
                for r in range(len(Q_PARTS)):
                    for tile, qk, part in ((q6, 0, Q_PARTS[r]), (k6, 1, K_PARTS[r])):
                        sp.dma_start(tile[r * DH:(r + 1) * DH, s].bitcast(F32),
                                     qk_parts[qk, part, :, half].rearrange("(h d) n -> d h n", d=DH))\
                            .then_inc(loaded[s], 16)
                sp.dma_start(v[:, s], v_pad[tok, :].rearrange("(k p) c -> p k c", p=P))\
                    .then_inc(loaded[s], 16)
            load(slice(0, S), slice(0, S // 2), 0)
            sp.dma_start(consts_f32[:, 4], ident_in).then_inc(consts, 16)
            if n_masks:
                sp.dma_start(consts_f32[:, 0:4], window_masks.rearrange("a p n -> p a n")).then_inc(consts, 16)

            def body(i, s, last):
                if not last:
                    tok = at(sp, i * (2 * S) + (s + 1) * S, S)
                    half = at(sp, i * S + (s + 1) * (S // 2), S // 2)
                    wait_apart(sp, batch_done, i * 2 + (s + 1), consts, NCONST)
                    load(tok, half, 1 - s)
                tok = at(sp, i * (2 * S) + s * S, S)
                for j in range(QUADS):
                    wait_apart(sp, o_ready, i * (2 * QUADS) + (s * QUADS + j + 3), consts, NCONST)
                    sp.dma_start(out_T[j, :, tok], o_norm[:, j % 2])\
                        .then_inc(stored[j % 2], 16)

            paired(sp, B, body)
            for s in range(2):
                sp.wait_ge(stored[s], B * QUADS // 2 * 16 + 16)

        @block.tensor
        def _(pe):
            pe.sem_inc(pv_done, 2)
            pe.sem_inc(batch_done, 1)
            pe.wait_ge(consts, NCONST)
            pe.wait_ge(filled, 1)
            pe.wait_ge(ones_set, 1)

            def maximum_rows(n, buf):
                pe.wait_ge(mparts_done, n + 1)
                for c in range(4):
                    mm = nc.tensor.matmul(m_ps[ROWS:ROWS + MAX_ROWS, c], mparts[:, buf, c, :],
                                          ident[:], start=True, stop=True, tile_position=(0, ROWS))
                mm.then_inc(mrow_done, 1)

            def scores(s, p):
                buf = p % 2
                for h2 in range(2):
                    h = 2 * p + h2
                    for qt in range(2):
                        mm = nc.tensor.matmul(s_ps[:, buf, h2, qt], q6[0:ROWS, s, h, qt * P:(qt + 1) * P],
                                              k6[0:ROWS, s, h, :], start=True, stop=not n_masks)
                        if n_masks:
                            kt = 1 - qt
                            mm = nc.tensor.matmul(s_ps[:, buf, h2, qt, kt * P:(kt + 1) * P], ident[:],
                                                  masks[:, qt], start=False, stop=True)
                mm.then_inc(s_done, 1)

            def values(s, j):
                if j < 0:
                    s, j = 1 - s, QUADS - 1
                for kt in range(2):
                    for c in range(4):
                        h = 4 * j + c
                        mm = nc.tensor.matmul(o_ps[32 * c:32 * c + 32], v[:, s, kt, h * 32:(h + 1) * 32],
                                              probs[:, j % 2, c, kt], start=(kt == 0), stop=(kt == 1),
                                              tile_position=(0, 32 * c))
                mm.then_inc(pv_done, 1)

            def wait_values(i, s, j):
                pe.wait_ge(t_free, i * (2 * H) + (s * H + 4 * j + 6))
                pe.wait_ge(o_copied, i * (2 * QUADS) + (s * QUADS + j + 1))

            def body(i, s, first, last):
                for p in range(PAIRS):
                    n = i * (2 * PAIRS) + (s * PAIRS + p)
                    if p + 2 < PAIRS or not last:
                        pe.wait_ge(max_done, n + 1)
                        if p + 2 == PAIRS:
                            pe.wait_ge(loaded[1 - s], i * (16 * nload) + 16 * nload * (s + 1))
                        scores((s + (p + 2) // PAIRS) % 2, (p + 2) % PAIRS)
                    if p + 1 < PAIRS or not last:
                        pe.wait_ge(mcopied, n + 1)
                        maximum_rows(n + 1, (p + 1) % 2)
                    if p % 2 == 0 and (p or not first):
                        wait_values(i, s, p // 2 - 1)
                        values(s, p // 2 - 1)
                        if p == 0:
                            pe.drain().then_inc(batch_done, 1)
                    if last and p == PAIRS - 1:
                        pe.wait_ge(mcopied, n + 1)
                    for h2 in range(2):
                        h = 2 * p + h2
                        pe.wait_ge(t_free, i * (2 * H) + (s * H + h + 1))
                        for kt in range(2):
                            mm = nc.tensor.matmul(t_ps[:, h2, kt],
                                                  k6[0:ROWS + MAX_ROWS, s, h, kt * P:(kt + 1) * P],
                                                  q6[0:ROWS + MAX_ROWS, s, h, :],
                                                  start=True, stop=not n_masks)
                            if n_masks:
                                qt = 1 - kt
                                mm = nc.tensor.matmul(t_ps[:, h2, kt, qt * P:(qt + 1) * P], ident[:],
                                                      masks[:, 2 + kt], start=False, stop=True)
                        mm.then_inc(t_done, 1)
                if last:
                    wait_values(i, s, QUADS - 1)
                    values(s, QUADS - 1)

            pe.wait_ge(loaded[0], 16 * nload)
            scores(0, 0)
            scores(0, 1)
            maximum_rows(0, 0)
            paired_first(pe, B, body)

        @block.vector
        def _(dve):
            dve.wait_ge(consts, NCONST)
            filling = nc.vector.tensor_copy(ident[:], consts_f32[:, 4])
            if n_masks:
                filling = nc.vector.tensor_copy(masks[:], consts_f32[:, 0:4])
            filling.then_inc(filled, 1)
            dve.sem_inc(o_copied, 1)

            def maximum(n, p):
                dve.wait_ge(s_done, n)
                nc.vector.tensor_reduce(nmax[:, p % 2], s_ps[:, p % 2].rearrange("p a b n -> p (a b) n"),
                                        axis=AX.X, op=ALU.max, negate=True).then_inc(max_done, 1)

            def turn_out(i, s, j):
                n = i * (2 * QUADS) + (s * QUADS + j)
                dve.wait_ge(o_copied, n + 2)
                nc.vector.transpose(o_turned[:, j % 2], o_sb[:, j % 2]).then_inc(turned, 1)
                dve.wait_ge(turned, n + 1)
                nc.vector.reciprocal(rsum[:, j % 2], blocks(o_turned[:, j % 2])[:, :, DH]).then_inc(rsum_done, 1)

            def turn_back(i, s, j):
                n = i * (2 * QUADS) + (s * QUADS + j)
                dve.wait_ge(stored[j % 2], i * (QUADS * 16) + (s * QUADS // 2 + j // 2) * 16 + 16)
                dve.wait_ge(scaled, n + 1)
                nc.vector.transpose(o_norm[:, j % 2], o_scaled[:, j % 2]).then_inc(o_ready, 1)

            def body(i, s, first, last):
                for p in range(PAIRS):
                    if not (last and p >= PAIRS - 2):
                        maximum(i * (2 * PAIRS) + (s * PAIRS + p + 3), p)
                    if p >= 2 or not first:
                        (turn_back if p % 2 else turn_out)(i, s, p // 2 - 1)
                if last:
                    turn_out(i, s, QUADS - 1)
                    turn_back(i, s, QUADS - 1)

            maximum(1, 0)
            maximum(2, 1)
            paired_first(dve, B, body)

        @block.gpsimd
        def _(pool):
            nc.gpsimd.memset(k6[ROWS:ROWS + MAX_ROWS], 1.0).then_inc(ones_set, 1)
            pool.sem_inc(o_ready, 2)

            def split_maximum(n, buf):
                wait_apart(pool, max_done, n, ones_set, 1)
                nc.gpsimd.tensor_copy(mparts[:, buf, :, 0], nmax[:, buf]).then_inc(hi_done, 1)
                pool.wait_ge(hi_done, n)
                nc.gpsimd.tensor_tensor(mparts[:, buf, :, 1], nmax[:, buf], mparts[:, buf, :, 0],
                                        ALU.subtract).then_inc(mparts_done, 1)

            def body(i, s, first, last):
                def norm(j):
                    n = i * (2 * QUADS) + (s * QUADS + j)
                    pool.wait_ge(rsum_done, n + 1)
                    pool.wait_ge(o_ready, n + 1)
                    nc.gpsimd.tensor_tensor(blocks(o_scaled[:, j % 2]), blocks(o_turned[:, j % 2]),
                                            rsum[:, j % 2].unsqueeze(2).broadcast_to([P, S // 32, 32]), ALU.mult)\
                        .then_inc(scaled, 1)
                for p in range(PAIRS):
                    if not (last and p >= PAIRS - 2):
                        split_maximum(i * (2 * PAIRS) + (s * PAIRS + p + 3), p % 2)
                    if p % 2 == 0 and (p or not first):
                        norm(p // 2 - 1)
                if last:
                    norm(QUADS - 1)

            split_maximum(1, 0)
            split_maximum(2, 1)
            paired_first(pool, B, body)

        @block.scalar
        def _(act):
            act.sem_inc(t_free, 2)

            def copy_rows(n, s, p):
                act.wait_ge(mrow_done, n)
                nc.scalar.activation(q6[ROWS:ROWS + MAX_ROWS, s, 2 * p:2 * p + 2, :],
                                     m_ps[ROWS:ROWS + MAX_ROWS].rearrange("p (a b) n -> p a (b n)", a=2),
                                     ACT.Copy).then_inc(mcopied, 1)

            def body(i, s, first, last):
                def copy_out(j):
                    n = i * (2 * QUADS) + (s * QUADS + j)
                    act.wait_ge(pv_done, n + 3)
                    act.wait_ge(o_ready, n + 1)
                    nc.scalar.activation(o_sb[:, j % 2], o_ps[:], ACT.Copy).then_inc(o_copied, 1)
                for p in range(PAIRS):
                    if p + 1 < PAIRS or not last:
                        copy_rows(i * (2 * PAIRS) + (s * PAIRS + p + 2), (s + (p + 1) // PAIRS) % 2, (p + 1) % PAIRS)
                    if p % 2 == 0 and (p or not first):
                        copy_out(p // 2 - 1)
                    for h2 in range(2):
                        h = 2 * p + h2
                        act.wait_ge(t_done, i * (2 * H) + (s * H + h + 1))
                        act.wait_ge(pv_done, i * (2 * QUADS) + (s * QUADS + h // 4 + 1))
                        nc.scalar.activation(probs[:, (h // 4) % 2, h % 4], t_ps[:, h2],
                                             ACT.Exp, scale=scale).then_inc(t_free, 1)
                if last:
                    copy_out(QUADS - 1)

            copy_rows(1, 0, 0)
            paired_first(act, B, body)


def phase_post(nc, name, o_T, groups, w_out, padded, bias, x_in, ident, x_out, x_outT, routes=None):
    with Phase(nc, name) as ph:
        w = ph.sb("w", [P, max(groups, 1), D])
        bias_sb = ph.sb("bias", [P, TPB, D])
        idt = ph.sb("idt", [P, P])
        power = ph.sb("power", [P, TPB])
        o = ph.sb("o", [P, 2, max(groups, 1), BLK])
        x = ph.sb("x", [P, 2, TPB, D])
        xb = ph.sb("xb", [P, 2, TPB, D])
        r = ph.sb("r", [P, 2, TPB, D])
        stats = ph.sb("stats", [P, 2, TPB, 6])
        mv = ph.sb("mv", [P, 2, TPB, 2])
        vare = ph.sb("vare", [P, 2, TPB])
        rstd = ph.sb("rstd", [P, 2, TPB])
        xo = ph.sb("xo", [P, 2, TPB, D])
        xoT = ph.sb("xoT", [P, 2, KD, BLK])
        NT = T // P
        if routes:
            y_sorted, positions, shares = routes
            pos = ph.sb("pos", [P, 2, NT], I32)
            share = ph.sb("share", [P, 2, NT])
            pos_c = ph.sb("pos_c", [P, 2, 2, TPB], I32)
            share_c = ph.sb("share_c", [P, 2, 2, TPB])
            yg = ph.sb("yg", [P, 2, 2, TPB, D])
            picked = ph.sem("picked")
            gathered = [ph.sem(f"gathered{s}") for s in range(2)]
            half_sum = ph.sem("half_sum")
        turned = groups and w_out is None
        y_ps = ph.ps("y_ps", [P, 1, TPB, QUADS * P] if turned else [P, 2, TPB, D])
        xT_ps = ph.ps("xT_ps", [P, KD, BLK])
        consts = ph.sem("consts")
        zeroed = ph.sem("zeroed")
        power_set = ph.sem("power_set")
        loaded = [ph.sem(f"loaded{s}") for s in range(2)]
        in_free = ph.sem("in_free")
        y_done = ph.sem("y_done")
        biased = ph.sem("biased")
        summed = ph.sem("summed")
        stats_done = ph.sem("stats_done")
        mv_done = ph.sem("mv_done")
        vare_done = ph.sem("vare_done")
        rstd_done = ph.sem("rstd_done")
        normed = ph.sem("normed")
        xT_done = ph.sem("xT_done")
        xT_out = ph.sem("xT_out")
        stored = [ph.sem(f"stored{s}") for s in range(2)]
        block = ph.block()
        n_in = 2 if groups else 1
        n_out = 2 if x_outT is not None else 1
        NCONST = 16 * (1 + (0 if not groups or turned else 4 if padded else 1) + (TPB if bias is not None else 0)
                       + (2 if routes else 0))

        @block.sync
        def _(sp):
            for s in range(2):
                sp.sem_inc(stored[s], 16)
            def load(i, s):
                tok = at(sp, i * (2 * BLK) + s * BLK, BLK)
                wait_apart(sp, in_free, i * 2 + (s + 1), consts, NCONST)
                if groups:
                    sp.dma_start(o[:, s], o_T[:, :, tok].rearrange("g p n -> p g n")).then_inc(loaded[s], 16)
                sp.dma_start(x[:, s], x_in[tok, :].rearrange("(t p) c -> p t c", p=P)).then_inc(loaded[s], 16)
            load(0, 0)
            sp.dma_start(idt[:], ident).then_inc(consts, 16)
            if groups and padded and not turned:
                sp.wait_ge(zeroed, 1)
                rows = w_out.rearrange("(g c d) n -> c d g n", c=4, d=DH)
                for c in range(4):
                    sp.dma_start(w[32 * c:32 * c + DH], rows[c]).then_inc(consts, 16)
            elif groups and not turned:
                sp.wait_ge(zeroed, 1)
                sp.dma_start(w[:], w_out.rearrange("(g p) n -> p g n", p=P)).then_inc(consts, 16)
            if bias is not None:
                for t in range(TPB):
                    sp.dma_start(bias_sb[:, t], bias.partition_broadcast(P)).then_inc(consts, 16)
            if routes:
                sp.dma_start(pos[:].rearrange("p r t -> p (r t)"), positions).then_inc(consts, 16)
                sp.dma_start(share[:].rearrange("p r t -> p (r t)"), shares).then_inc(consts, 16)

            load_all(sp, load)
            for s in range(2):
                sp.wait_ge(stored[s], NBLK // 2 * 16 * n_out + 16)

        @block.tensor
        def _(pe):
            pe.wait_ge(consts, NCONST)
            if groups:
                pe.wait_ge(zeroed, 1)

            def project(i, s):
                pe.wait_ge(loaded[s], i * (16 * n_in) + 16 * n_in)
                if turned:
                    pe.wait_ge(in_free, i * 2 + (s + 2))
                for t in range(TPB):
                    for g in range(groups):
                        if turned:
                            mm = nc.tensor.transpose(y_ps[:, 0, t, g * P:(g + 1) * P],
                                                     o[:, s, g, t * P:(t + 1) * P], idt[:])
                        else:
                            mm = nc.tensor.matmul(y_ps[:, s, t], o[:, s, g, t * P:(t + 1) * P], w[:, g],
                                                  start=(g == 0), stop=(g == groups - 1))
                mm.then_inc(y_done, 1)

            def body(i, s, last):
                if groups and not last:
                    project(i + s, 1 - s)
                if x_outT is not None:
                    pe.wait_ge(normed, i * 2 + (s + 1))
                    pe.wait_ge(xT_out, i * 2 + (s + 1))
                    for t in range(TPB):
                        for k in range(KD):
                            mm = nc.tensor.transpose(xT_ps[:, k, t * P:(t + 1) * P],
                                                     xo[:, s, t, k * P:(k + 1) * P], idt[:])
                    mm.then_inc(xT_done, 1)
            if groups:
                project(0, 0)
            paired(pe, NBLK, body)

        @block.gpsimd
        def _(pool):
            nc.gpsimd.memset(w[:], 0.0).then_inc(zeroed, 1)
            nc.gpsimd.memset(power[:], -0.5).then_inc(power_set, 1)
            if bias is not None or routes:
                pool.wait_ge(consts, NCONST)

            def gather(i, s):
                tiles = at(pool, i * (2 * TPB) + s * TPB, TPB)
                wait_apart(pool, in_free, i * 2 + (s + 1), consts, NCONST)
                nc.gpsimd.tensor_copy(pos_c[:, s], pos[:, :, tiles])
                nc.gpsimd.tensor_copy(share_c[:, s], share[:, :, tiles]).then_inc(picked, 1)
                wait_apart(pool, picked, i * 2 + (s + 1), consts, NCONST)
                for r in range(2):
                    for t in range(TPB):
                        nc.gpsimd.indirect_dma_start(
                            yg[:, s, r, t], None, y_sorted,
                            bass.IndirectOffsetOnAxis(ap=pos_c[:, s, r, t:t + 1], axis=0)).then_inc(gathered[s], 16)
            if routes:
                gather(0, 0)

            def body(i, s, last):
                if routes and not last:
                    gather(i + s, 1 - s)
                if bias is not None:
                    pool.wait_ge(loaded[s], i * (16 * n_in) + 16 * n_in)
                    nc.gpsimd.tensor_tensor(xb[:, s], x[:, s], bias_sb[:], ALU.add).then_inc(biased, 1)
                wait_apart(pool, mv_done, i * 2 + (s + 1), power_set, 1)
                nc.gpsimd.tensor_scalar(vare[:, s], mv[:, s, :, 1], LN_EPS, None, ALU.add).then_inc(vare_done, 1)
                pool.wait_ge(vare_done, i * 2 + (s + 1))
                nc.gpsimd.tensor_tensor(rstd[:, s], vare[:, s], power[:], ALU.pow).then_inc(rstd_done, 1)
            paired(pool, NBLK, body)

        @block.vector
        def _(dve):
            dve.sem_inc(in_free, 2)

            def body(i, s, last):
                n = i * 2 + (s + 1)
                res = xb if bias is not None else x
                if groups:
                    dve.wait_ge(y_done, n)
                    if bias is not None:
                        dve.wait_ge(biased, n)
                    dve.wait_ge(loaded[s], i * (16 * n_in) + 16 * n_in)
                    if turned:
                        nc.vector.tensor_tensor(
                            r[:, s].rearrange("p t (h c) -> p (t h) c", c=DH),
                            y_ps[:, 0].rearrange("p t (h c) -> p (t h) c", c=32)[:, :, 0:DH],
                            res[:, s].rearrange("p t (h c) -> p (t h) c", c=DH), ALU.add).then_inc(summed, 1)
                    else:
                        nc.vector.tensor_tensor(r[:, s], y_ps[:, s], res[:, s], ALU.add).then_inc(summed, 1)
                elif routes:
                    dve.wait_ge(loaded[s], i * (16 * n_in) + 16 * n_in)
                    dve.wait_ge(gathered[s], i * (32 * TPB) + 32 * TPB)
                    dve.wait_ge(picked, n)
                    for t in range(TPB):
                        op = nc.vector.scalar_tensor_tensor(r[:, s, t], yg[:, s, 0, t], share_c[:, s, 0, t:t + 1],
                                                            x[:, s, t], ALU.mult, ALU.add)
                    op.then_inc(half_sum, 1)
                    dve.wait_ge(half_sum, n)
                    for t in range(TPB):
                        op = nc.vector.scalar_tensor_tensor(r[:, s, t], yg[:, s, 1, t], share_c[:, s, 1, t:t + 1],
                                                            r[:, s, t], ALU.mult, ALU.add)
                    op.then_inc(summed, 1)
                else:
                    dve.wait_ge(loaded[s], i * (16 * n_in) + 16 * n_in)
                    nc.vector.tensor_copy(r[:, s], x[:, s]).then_inc(summed, 1)
                dve.wait_ge(summed, n)
                dve.sem_inc(in_free, 1)
                for t in range(TPB):
                    last_op = nc.vector.bn_stats(stats[:, s, t], r[:, s, t])
                last_op.then_inc(stats_done, 1)
                wait_apart(dve, stats_done, n, consts, NCONST)
                for t in range(TPB):
                    last_op = nc.vector.bn_aggr(mv[:, s, t], stats[:, s, t])
                last_op.then_inc(mv_done, 1)
                dve.wait_ge(stored[s], i * (16 * n_out) + 16)
                dve.wait_ge(mv_done, n)
                dve.wait_ge(rstd_done, n)
                for t in range(TPB):
                    last_op = nc.vector.tensor_scalar(xo[:, s, t], r[:, s, t], mv[:, s, t, 0:1],
                                                      rstd[:, s, t:t + 1], ALU.subtract, ALU.mult)
                last_op.then_inc(normed, 1)
            paired(dve, NBLK, body)

        @block.scalar
        def _(act):
            act.sem_inc(xT_out, 1)

            def body(i, s, last):
                tok = at(act, i * (2 * BLK) + s * BLK, BLK)
                wait_apart(act, normed, i * 2 + (s + 1), consts, NCONST)
                act.dma_start(x_out[tok, :].rearrange("(t p) c -> p t c", p=P), xo[:, s]).then_inc(stored[s], 16)
                if x_outT is not None:
                    act.wait_ge(xT_done, i * 2 + (s + 1))
                    for k in range(KD):
                        op = nc.scalar.activation(xoT[:, s, k], xT_ps[:, k], ACT.Copy)
                    op.then_inc(xT_out, 1)
                    wait_apart(act, xT_out, i * 2 + (s + 2), consts, NCONST)
                    act.dma_start(x_outT[:, tok].rearrange("(k p) n -> p k n", p=P), xoT[:, s])\
                        .then_inc(stored[s], 16)
            paired(act, NBLK, body)


def phase_cross(nc, xT, ctxT, Wq, bq, Wk, bk, Wv, bv, ident, o_T):
    with Phase(nc, "cross") as ph:
        PAIRS = H // 2
        LAST = B * PAIRS - 1
        wq = ph.sb("wq", [P, KD, DM])
        wk = ph.sb("wk", [P, KD, DM])
        wv = ph.sb("wv", [P, KD, DM])
        bqs = ph.sb("bqs", [P, PAIRS])
        bq_scaled = ph.sb("bq_scaled", [P, PAIRS])
        bks = ph.sb("bks", [P, PAIRS])
        bvs = ph.sb("bvs", [P, 2, DM])
        idt = ph.sb("idt", [P, P])
        x = ph.sb("x", [P, 2, KD, S])
        c = ph.sb("c", [P, 2, KD, S])
        q = ph.sb("q", [P, 2, 2, S])
        k = ph.sb("k", [P, 2, S])
        v = ph.sb("v", [P, 2, 2, P])
        nmax = ph.sb("nmax", [P, 4])
        probs = ph.sb("probs", [P, 2, 4, S])
        sums = ph.sb("sums", [P, 2, 4])
        rsum = ph.sb("rsum", [P, 2, 4])
        probs_T = ph.sb("probs_T", [P, 2, 2, S])
        o_sb = ph.sb("o_sb", [P, 2, S])
        qk_ps = ph.ps("qk_ps", [P, 2, S])
        v_ps = ph.ps("v_ps", [P, 2, 2 * P])
        s_ps = ph.ps("s_ps", [P, 4, S])
        pT_ps = ph.ps("pT_ps", [P, 2, 2, S])
        o_ps = ph.ps("o_ps", [P, 2 * S])
        consts = ph.sem("consts")
        NCONST = 16 * 8
        bias_scaled = ph.sem("bias_scaled")
        q_filled = ph.sem("q_filled")
        loaded = [ph.sem(f"loaded{s}") for s in range(2)]
        in_free = ph.sem("in_free")
        qk_done = ph.sem("qk_done")
        qk_out = ph.sem("qk_out")
        vp_done = ph.sem("vp_done")
        v_out = ph.sem("v_out")
        s_done = ph.sem("s_done")
        max_done = ph.sem("max_done")
        exp_done = ph.sem("exp_done")
        rsum_done = ph.sem("rsum_done")
        scaled = ph.sem("scaled")
        pT_done = ph.sem("pT_done")
        pT_out = ph.sem("pT_out")
        pv_done = ph.sem("pv_done")
        o_out = ph.sem("o_out")
        stored = [ph.sem(f"stored{s}") for s in range(2)]
        block = ph.block()

        @block.sync
        def _(sp):
            for s in range(2):
                sp.sem_inc(stored[s], 16)
            def load(i, s):
                tok = at(sp, i * (2 * S) + s * S, S)
                wait_apart(sp, in_free, i * 2 + (s + 1), consts, NCONST)
                for dst, src in ((x, xT), (c, ctxT)):
                    sp.dma_start(dst[:, s], src[:, tok].rearrange("(k p) n -> p k n", p=P))\
                        .then_inc(loaded[s], 16)
            load(0, 0)
            for dst, src in ((wq, Wq), (wk, Wk), (wv, Wv)):
                sp.dma_start(dst[:], src.rearrange("(k p) n -> p k n", p=P)).then_inc(consts, 16)
            for dst, src in ((bqs, bq), (bks, bk)):
                sp.dma_start(dst[:], src.rearrange("(m p) -> p m", p=P),
                             allow_slow_non_contiguous=True).then_inc(consts, 16)
            for t in range(2):
                sp.dma_start(bvs[:, t], bv.partition_broadcast(P)).then_inc(consts, 16)
            sp.dma_start(idt[:], ident).then_inc(consts, 16)

            def body(i, s, last):
                if not last:
                    load(i + s, 1 - s)
                tok = at(sp, i * (2 * S) + s * S, S)
                for p in range(PAIRS):
                    wait_apart(sp, o_out, i * (2 * PAIRS) + (s * PAIRS + p + 2), consts, NCONST)
                    sp.dma_start(o_T[p, :, tok], o_sb[:, p % 2]).then_inc(stored[p % 2], 16)

            paired(sp, B, body)
            for s in range(2):
                sp.wait_ge(stored[s], B * PAIRS // 2 * 16 + 16)

        @block.tensor
        def _(pe):
            pe.sem_inc(in_free, 2)
            pe.wait_ge(consts, NCONST)
            pe.wait_ge(q_filled, 1)

            def project_qk(m, s, p):
                pe.wait_ge(qk_out, m + 1)
                for j, (wt, src) in enumerate(((wq, x), (wk, c))):
                    for kd in range(KD):
                        mm = nc.tensor.matmul(qk_ps[:, j], wt[:, kd, p * P:(p + 1) * P], src[:, s, kd],
                                              start=(kd == 0), stop=(kd == KD - 1))
                mm.then_inc(qk_done, 1)

            def project_v(m, s, p):
                pe.wait_ge(v_out, m + 1)
                for t in range(2):
                    for kd in range(KD):
                        mm = nc.tensor.matmul(v_ps[:, t, 0:P], c[:, s, kd, t * P:(t + 1) * P],
                                              wv[:, kd, p * P:(p + 1) * P],
                                              start=(kd == 0), stop=(kd == KD - 1))
                mm.then_inc(vp_done, 1)

            def scores(m, buf):
                pe.wait_ge(qk_out, m + 2)
                pe.wait_ge(exp_done, m + 1)
                for h2 in range(2):
                    for qt in range(2):
                        mm = nc.tensor.matmul(s_ps[:, 2 * h2 + qt], q[:, buf, h2, qt * P:(qt + 1) * P],
                                              k[:, buf], start=True, stop=True)
                    mm.then_inc(s_done, 1)

            def turn(m, buf):
                pe.wait_ge(scaled, m + 1)
                for h2 in range(2):
                    for kt in range(2):
                        for qt in range(2):
                            mm = nc.tensor.transpose(pT_ps[:, h2, kt, qt * P:(qt + 1) * P],
                                                     probs[:, buf, 2 * h2 + qt, kt * P:(kt + 1) * P], idt[:])
                mm.then_inc(pT_done, 1)

            def values(m, buf):
                pe.wait_ge(pT_out, m + 1)
                pe.wait_ge(v_out, m + 2)
                pe.wait_ge(o_out, m + 1)
                for kt in range(2):
                    for h2 in range(2):
                        mm = nc.tensor.matmul(o_ps[DX * h2:DX * h2 + DX, 0:S],
                                              v[:, buf, kt, h2 * DX:(h2 + 1) * DX],
                                              probs_T[:, h2, kt], start=(kt == 0), stop=(kt == 1),
                                              tile_position=(0, DX * h2))
                mm.then_inc(pv_done, 1)

            def body(i, s, first, last):
                for p in range(PAIRS):
                    m = i * (2 * PAIRS) + (s * PAIRS + p)
                    if not (last and p >= PAIRS - 2):
                        if p == PAIRS - 2:
                            pe.wait_ge(loaded[1 - s], i * 32 + 32 * (s + 1))
                        project_qk(m + 2, (s + (p + 2) // PAIRS) % 2, (p + 2) % PAIRS)
                    if not (first and p == 0):
                        turn(m - 1, (p + 1) % 2)
                    project_v(m, s, p)
                    if p == PAIRS - 1:
                        pe.drain().then_inc(in_free, 1)
                    if not (last and p == PAIRS - 1):
                        scores(m + 1, (p + 1) % 2)
                    if not (first and p == 0):
                        values(m - 1, (p + 1) % 2)

            pe.wait_ge(loaded[0], 32)
            project_qk(0, 0, 0)
            project_qk(1, 0, 1)
            scores(0, 0)
            paired_first(pe, B, body)
            turn(LAST, 1)
            values(LAST, 1)

        @block.scalar
        def _(act):
            act.sem_inc(qk_out, 1)
            act.sem_inc(exp_done, 1)
            act.wait_ge(consts, NCONST)
            act.wait_ge(q_filled, 1)
            act.wait_ge(bias_scaled, 1)

            def copy_qk(m, p):
                act.wait_ge(qk_done, m + 1)
                for h2 in range(2):
                    rows = slice(DX * h2, DX * h2 + DX)
                    nc.scalar.activation(q[rows, p % 2, h2], qk_ps[rows, 0], ACT.Identity,
                                         bias=bq_scaled[rows, p:p + 1], scale=DX ** -0.5)
                nc.scalar.activation(k[:, p % 2], qk_ps[:, 1], ACT.Identity, bias=bks[:, p:p + 1])\
                    .then_inc(qk_out, 1)

            def exps(m, buf):
                act.wait_ge(max_done, m + 1)
                act.wait_ge(pT_done, m + 1)
                for r in range(4):
                    op = nc.scalar.activation(probs[:, buf, r], s_ps[:, r], ACT.Exp, bias=nmax[:, r:r + 1],
                                              accum_out=sums[:, buf, r:r + 1])
                op.then_inc(exp_done, 1)

            def copy_out(i, s, p):
                act.wait_ge(pv_done, i * (2 * PAIRS) + (s * PAIRS + p + 1))
                act.wait_ge(stored[p % 2], i * (PAIRS * 16) + (s * PAIRS // 2 + p // 2) * 16 + 16)
                nc.scalar.activation(o_sb[:, p % 2], o_ps[:, 0:S], ACT.Copy).then_inc(o_out, 1)

            def body(i, s, first, last):
                for p in range(PAIRS):
                    m = i * (2 * PAIRS) + (s * PAIRS + p)
                    if not (last and p >= PAIRS - 2):
                        copy_qk(m + 2, (p + 2) % PAIRS)
                    if not (first and p == 0):
                        copy_out(i, s, p - 1)
                    if not (last and p == PAIRS - 1):
                        exps(m + 1, (p + 1) % 2)
            copy_qk(0, 0)
            copy_qk(1, 1)
            exps(0, 0)
            paired_first(act, B, body)
            copy_out(B // 2 - 1, 1, PAIRS - 1)

        @block.vector
        def _(dve):
            dve.sem_inc(v_out, 1)
            dve.sem_inc(o_out, 1)
            dve.sem_inc(pT_done, 2)
            dve.wait_ge(consts, NCONST)
            nc.vector.tensor_scalar(bq_scaled[:], bqs[:], DX ** -0.5, None, ALU.mult).then_inc(bias_scaled, 1)

            def copy_turned(m):
                dve.wait_ge(pT_done, m + 3)
                for h2 in range(2):
                    op = nc.vector.tensor_copy(probs_T[:, h2], pT_ps[:, h2])
                op.then_inc(pT_out, 1)

            def copy_v(m, p):
                dve.wait_ge(vp_done, m + 1)
                nc.vector.tensor_tensor(v[:, p % 2], v_ps[:, :, 0:P], bvs[:, :, p * P:(p + 1) * P], ALU.add)\
                    .then_inc(v_out, 1)

            def maxima(m, buf):
                dve.wait_ge(exp_done, m + 1)
                for h2 in range(2):
                    dve.wait_ge(s_done, m * 2 + (h2 + 1))
                    op = nc.vector.tensor_reduce(nmax[:, 2 * h2:2 * h2 + 2], s_ps[:, 2 * h2:2 * h2 + 2],
                                                 axis=AX.X, op=ALU.max, negate=True)
                op.then_inc(max_done, 1)

            def reciprocals(m, buf):
                dve.wait_ge(exp_done, m + 2)
                nc.vector.reciprocal(rsum[:, buf], sums[:, buf]).then_inc(rsum_done, 1)

            def body(i, s, first, last):
                for p in range(PAIRS):
                    m = i * (2 * PAIRS) + (s * PAIRS + p)
                    if not (first and p == 0):
                        copy_turned(m - 1)
                    copy_v(m, p)
                    if not (last and p == PAIRS - 1):
                        maxima(m + 1, (p + 1) % 2)
                        reciprocals(m + 1, (p + 1) % 2)
            maxima(0, 0)
            reciprocals(0, 0)
            paired_first(dve, B, body)
            copy_turned(LAST)

        @block.gpsimd
        def _(pool):
            nc.gpsimd.memset(q[:], 0.0).then_inc(q_filled, 1)

            def body(i, s, last):
                pool.wait_ge(rsum_done, i * 2 + (s + 1))
                nc.gpsimd.tensor_tensor(probs[:, s], probs[:, s],
                                        rsum[:, s].unsqueeze(2).broadcast_to([P, 4, S]), ALU.mult)\
                    .then_inc(scaled, 1)
            paired(pool, LAST + 1, body)


def phase_rwkv_in(nc, xT, maas, WT, qk_parts, v_pad, gate):
    with Phase(nc, "rin") as ph:
        w = ph.sb("w", [P, 4, KD, D])
        maa = ph.sb("maa", [P, 4, KD])
        x = ph.sb("x", [P, 2, KD, 2, S + 1])
        dx = ph.sb("dx", [P, KD, 2, S])
        mix = ph.sb("mix", [P, 4, KD, BLK])
        parts = ph.sb("parts", [P, 2, 4, 3, BLK], BF16)
        rest = ph.sb("rest", [P, 2, BLK])
        vp = ph.sb("vp", [P, 2, TPB, H, 32])
        g = ph.sb("g", [P, 2, TPB, D])
        qk_ps = ph.ps("qk_ps", [P, 4, BLK])
        v_ps = ph.ps("v_ps", [P, TPB, D])
        g_ps = ph.ps("g_ps", [P, TPB, D])
        consts = ph.sem("consts")
        NCONST = 16 * 8
        x_loaded = [ph.sem(f"x_loaded{s}") for s in range(2)]
        x_free = ph.sem("x_free")
        x_zeroed = ph.sem("x_zeroed")
        dx_done = ph.sem("dx_done")
        mixed = ph.sem("mixed")
        mix_free = ph.sem("mix_free")
        qk_done = ph.sem("qk_done")
        hi_done = ph.sem("hi_done")
        rest_done = ph.sem("rest_done")
        mid_done = ph.sem("mid_done")
        parts_done = ph.sem("parts_done")
        v_zeroed = ph.sem("v_zeroed")
        v_done = ph.sem("v_done")
        v_out = ph.sem("v_out")
        g_done = ph.sem("g_done")
        g_out = ph.sem("g_out")
        stored = [ph.sem(f"stored{s}") for s in range(2)]
        block = ph.block()

        @block.sync
        def _(sp):
            for s in range(2):
                sp.sem_inc(stored[s], 16)
            def load(i, s):
                tok = at(sp, i * (2 * BLK) + s * BLK, BLK)
                wait_apart(sp, x_free, i * 2 + (s + 1), consts, NCONST)
                for k in range(KD):
                    sp.dma_start(x[:, s, k, :, 1:S + 1], xT[k * P:(k + 1) * P, tok]
                                 .rearrange("p (b n) -> p b n", b=2)).then_inc(x_loaded[s], 16)
            load(0, 0)
            for j in range(4):
                sp.dma_start(w[:, j], WT[j].rearrange("(k p) n -> p k n", p=P)).then_inc(consts, 16)
                sp.dma_start(maa[:, j], maas[j].rearrange("a b (k p) -> p (a b k)", p=P),
                             allow_slow_non_contiguous=True).then_inc(consts, 16)
            sp.wait_ge(x_zeroed, 1)

            def body(i, s, last):
                if not last:
                    load(i + s, 1 - s)
                tok = at(sp, i * (2 * BLK) + s * BLK, BLK)
                half = at(sp, i * BLK + s * (BLK // 2), BLK // 2)
                for m in range(4):
                    wait_apart(sp, parts_done, i * 8 + (s * 4 + m + 3), consts, NCONST)
                    sp.dma_start(qk_parts[m // 2, :, (m % 2) * P:(m % 2 + 1) * P, half]
                                 .rearrange("a p n -> p a n"), parts[:, s, m].bitcast(F32)).then_inc(stored[s], 16)
                wait_apart(sp, v_out, i * 4 + (s * 2 + 4), consts, NCONST)
                sp.dma_start(v_pad[tok, :].rearrange("(t p) c -> p t c", p=P),
                             vp[:, s].rearrange("p t h c -> p t (h c)")).then_inc(stored[s], 16)
                wait_apart(sp, g_out, i * 4 + (s * 2 + 4), consts, NCONST)
                sp.dma_start(gate[tok, :].rearrange("(t p) c -> p t c", p=P), g[:, s]).then_inc(stored[s], 16)

            paired(sp, NBLK, body)
            for s in range(2):
                sp.wait_ge(stored[s], NBLK // 2 * 6 * 16 + 16)

        @block.vector
        def _(dve):
            dve.sem_inc(x_free, 2)
            dve.sem_inc(rest_done, 4)
            dve.sem_inc(v_out, 2)
            nc.vector.memset(x[:, :, :, :, 0:1], 0.0).then_inc(x_zeroed, 1)
            dve.wait_ge(consts, NCONST)
            dve.wait_ge(x_zeroed, 1)
            dve.wait_ge(v_zeroed, 1)

            def shift(i, s):
                n = i * 2 + (s + 1)
                dve.wait_ge(x_loaded[s], i * 32 + 32)
                nc.vector.tensor_tensor(dx[:].rearrange("p k b n -> p (k b) n"),
                                        x[:, s, :, :, 0:S].rearrange("p k b n -> p (k b) n"),
                                        x[:, s, :, :, 1:S + 1].rearrange("p k b n -> p (k b) n"),
                                        ALU.subtract).then_inc(dx_done, 1)
                dve.wait_ge(mix_free, n)
                dve.wait_ge(dx_done, n)
                for j in range(4):
                    for k in range(KD):
                        op = nc.vector.scalar_tensor_tensor(
                            mix[:, j, k].rearrange("p (b n) -> p b n", b=2), dx[:, k], maa[:, j, k:k + 1],
                            x[:, s, k, :, 1:S + 1], ALU.mult, ALU.add)
                    op.then_inc(mixed, 1)
                dve.wait_ge(mixed, n * 4)
                dve.sem_inc(x_free, 1)

            def body(i, s, last):
                shift(i, s)
                for m in range(4):
                    dve.wait_ge(hi_done, i * 8 + (s * 4 + m + 1))
                    dve.wait_ge(parts_done, i * 8 + (s * 4 + m + 1))
                    nc.vector.tensor_tensor(rest[:, m % 2], qk_ps[:, m], parts[:, s, m, 0], ALU.subtract)\
                        .then_inc(rest_done, 1)
                dve.wait_ge(stored[s], i * (6 * 16) + 16)
                for t in (0, 2):
                    dve.wait_ge(v_done, i * 4 + (s * 2 + t // 2 + 1))
                    nc.vector.tensor_copy(vp[:, s, t:t + 2, :, 0:DH],
                                          v_ps[:, t:t + 2].rearrange("p t (h c) -> p t h c", c=DH))\
                        .then_inc(v_out, 1)
            paired(dve, NBLK, body)

        @block.tensor
        def _(pe):
            pe.sem_inc(mix_free, 1)
            pe.wait_ge(consts, NCONST)

            def body(i, s, last):
                for m in range(4):
                    pe.wait_ge(mixed, i * 8 + (s * 4 + m // 2 + 1))
                    pe.wait_ge(rest_done, i * 8 + (s * 4 + m + 1))
                    for k in range(KD):
                        mm = nc.tensor.matmul(qk_ps[:, m], w[:, m // 2, k, (m % 2) * P:(m % 2 + 1) * P],
                                              mix[:, m // 2, k], start=(k == 0), stop=(k == KD - 1))
                    mm.then_inc(qk_done, 1)
                for j, out, free, done in ((2, v_ps, v_out, v_done), (3, g_ps, g_out, g_done)):
                    pe.wait_ge(mixed, i * 8 + (s * 4 + j + 1))
                    for t in range(TPB):
                        if t % 2 == 0:
                            pe.wait_ge(free, i * 4 + (s * 2 + t // 2 + 1))
                        for k in range(KD):
                            mm = nc.tensor.matmul(out[:, t], mix[:, j, k, t * P:(t + 1) * P], w[:, j, k],
                                                  start=(k == 0), stop=(k == KD - 1))
                        if t % 2:
                            mm.then_inc(done, 1)
                pe.drain().then_inc(mix_free, 1)
            paired(pe, NBLK, body)

        @block.scalar
        def _(act):
            act.sem_inc(g_out, 2)

            def body(i, s, last):
                act.wait_ge(stored[s], i * (6 * 16) + 16)
                for m in range(4):
                    act.wait_ge(qk_done, i * 8 + (s * 4 + m + 1))
                    nc.scalar.activation(parts[:, s, m, 0], qk_ps[:, m], ACT.Copy).then_inc(hi_done, 1)
                for t in (0, 2):
                    act.wait_ge(g_done, i * 4 + (s * 2 + t // 2 + 1))
                    nc.scalar.activation(g[:, s, t:t + 2].rearrange("p t c -> p (t c)"),
                                         g_ps[:, t:t + 2].rearrange("p t c -> p (t c)"), ACT.Gelu)\
                        .then_inc(g_out, 1)
            paired(act, NBLK, body)

        @block.gpsimd
        def _(pool):
            nc.gpsimd.memset(vp[:], 0.0).then_inc(v_zeroed, 1)
            pool.sem_inc(parts_done, 2)

            def body(i, s, last):
                for m in range(4):
                    wait_apart(pool, rest_done, i * 8 + (s * 4 + m + 5), v_zeroed, 1)
                    nc.gpsimd.tensor_copy(parts[:, s, m, 1], rest[:, m % 2]).then_inc(mid_done, 1)
                    pool.wait_ge(mid_done, i * 8 + (s * 4 + m + 1))
                    nc.gpsimd.tensor_tensor(parts[:, s, m, 2], rest[:, m % 2], parts[:, s, m, 1],
                                            ALU.subtract).then_inc(parts_done, 1)
            paired(pool, NBLK, body)


def phase_rwkv_core(nc, qk_parts, v_pad, decay, faaaa, diag, out_T, ctxT, ctx, next_k_parts, next_v_pad):
    with Phase(nc, "rwkv") as ph:
        WIDE = S + P
        q6 = ph.sb("q6", [P, 2, H, S], BF16)
        k6 = ph.sb("k6", [P, 2, H, S], BF16)
        v = ph.sb("v", [P, 2, 2, H * 32])
        dg = ph.sb("dg", [P, S])
        dec = ph.sb("dec", [P, H])
        u = ph.sb("u", [P, H])
        neg = ph.sb("neg", [P, H])
        dist = ph.sb("dist", [P, S])
        weight = ph.sb("weight", [P, H, S])
        att = ph.sb("att", [P, 2, 4, WIDE])
        o_sb = ph.sb("o_sb", [P, 2, S])
        kx = ph.sb("kx", [P, 2, KD, S])
        k_parts = ph.sb("k_parts", [P, 2, 3, KD, S], BF16)
        k_rest = ph.sb("k_rest", [P, KD, S])
        vx = ph.sb("vx", [P, 2, 2, D])
        vp = ph.sb("vp", [P, 2, 2, H, 32])
        t_ps = ph.ps("t_ps", [P, 4, 2 * S])
        o_ps = ph.ps("o_ps", [P, 2, 2 * S])
        consts = ph.sem("consts")
        dist_done = ph.sem("dist_done")
        expdec_done = ph.sem("expdec_done")
        neg_done = ph.sem("neg_done")
        powers_done = ph.sem("powers_done")
        masked = ph.sem("masked")
        weight_done = ph.sem("weight_done")
        loaded = [ph.sem(f"loaded{s}") for s in range(2)]
        batch_done = ph.sem("batch_done")
        t_done = ph.sem("t_done")
        att_done = ph.sem("att_done")
        pv_done = ph.sem("pv_done")
        o_out = ph.sem("o_out")
        stored = [ph.sem(f"stored{s}") for s in range(2)]
        vp_filled = ph.sem("vp_filled")
        ctx_loaded = [ph.sem(f"ctx_loaded{s}") for s in range(2)]
        k_hi = ph.sem("k_hi")
        k_rested = ph.sem("k_rested")
        k_mid = ph.sem("k_mid")
        k_lo = ph.sem("k_lo")
        v_spread = ph.sem("v_spread")
        ctx_stored = [ph.sem(f"ctx_stored{s}") for s in range(2)]
        block = ph.block()
        nload = 13
        NCONST = 48

        @block.sync
        def _(sp):
            for s in range(2):
                sp.sem_inc(stored[s], 16)
                sp.sem_inc(ctx_stored[s], 16)
            def load(tok, half, s):
                for r in range(len(Q_PARTS)):
                    for tile, qk, part in ((q6, 0, Q_PARTS[r]), (k6, 1, K_PARTS[r])):
                        sp.dma_start(tile[r * DH:(r + 1) * DH, s].bitcast(F32),
                                     qk_parts[qk, part, :, half].rearrange("(h d) n -> d h n", d=DH))\
                            .then_inc(loaded[s], 16)
                sp.dma_start(v[:, s], v_pad[tok, :].rearrange("(k p) c -> p k c", p=P))\
                    .then_inc(loaded[s], 16)
            sp.dma_start(dec[:], decay.rearrange("h a -> (h a)").partition_broadcast(P)).then_inc(consts, 16)
            sp.dma_start(u[:], faaaa.rearrange("h a -> (h a)").partition_broadcast(P)).then_inc(consts, 16)
            sp.dma_start(dg[:], diag).then_inc(consts, 16)
            load(slice(0, S), slice(0, S // 2), 0)

            def body(i, s, last):
                if not last:
                    tok = at(sp, i * (2 * S) + (s + 1) * S, S)
                    half = at(sp, i * S + (s + 1) * (S // 2), S // 2)
                    wait_apart(sp, batch_done, i * 2 + (s + 1), consts, NCONST)
                    load(tok, half, 1 - s)
                tok = at(sp, i * (2 * S) + s * S, S)
                for j in range(QUADS):
                    wait_apart(sp, o_out, i * (2 * QUADS) + (s * QUADS + j + 3), consts, NCONST)
                    sp.dma_start(out_T[j, :, tok], o_sb[:, j % 2]).then_inc(stored[j % 2], 16)

            paired(sp, B, body)
            for s in range(2):
                sp.wait_ge(stored[s], B * QUADS // 2 * 16 + 16)
                sp.wait_ge(ctx_stored[s], B // 2 * 64 + 16)

        @block.gpsimd
        def _(pool):
            nc.gpsimd.memset(vp[:], 1.0).then_inc(vp_filled, 1)
            nc.gpsimd.iota(dist[:], pattern=[[1, S]], base=-1, channel_multiplier=-1,
                           allow_small_or_imprecise_dtypes=True).then_inc(dist_done, 1)
            pool.wait_ge(dist_done, 1)
            nc.gpsimd.tensor_scalar(dist[:], dist[:], 0.0, None, ALU.max).then_inc(dist_done, 1)
            pool.wait_ge(powers_done, 1)
            nc.gpsimd.affine_select(out=weight[:], in_=weight[:], pattern=[[0, H], [1, S]],
                                    compare_op=ALU.is_ge, fill=0.0, base=-1, channel_multiplier=-1)\
                .then_inc(masked, 1)

            def body(i, s, last):
                n = i * 2 + s
                pool.wait_ge(k_hi, n + 1)
                pool.wait_ge(ctx_loaded[s], i * 32 + 32)
                nc.gpsimd.tensor_tensor(k_rest[:], kx[:, s], k_parts[:, s, 0], ALU.subtract).then_inc(k_rested, 1)
                pool.wait_ge(k_rested, n + 1)
                pool.wait_ge(k_mid, n + 1)
                nc.gpsimd.tensor_tensor(k_parts[:, s, 2], k_rest[:], k_parts[:, s, 1], ALU.subtract)\
                    .then_inc(k_lo, 1)
            paired(pool, B, body)

        @block.tensor
        def _(pe):
            pe.sem_inc(pv_done, 2)
            pe.sem_inc(batch_done, 1)

            def scores(s, h):
                for kt in range(2):
                    mm = nc.tensor.matmul(t_ps[:, h % 4, (0, S)[kt]:(S, WIDE)[kt]],
                                          k6[0:ROWS, s, h, kt * P:(kt + 1) * P], q6[0:ROWS, s, h, kt * P:S],
                                          start=True, stop=True)
                mm.then_inc(t_done, 1)

            def values(s, j):
                for kt in range(2):
                    for c in range(4):
                        h = 4 * j + c
                        mm = nc.tensor.matmul(o_ps[32 * c:32 * c + 32, j % 2, kt * P:S],
                                              v[:, s, kt, h * 32:(h + 1) * 32],
                                              att[:, j % 2, c, (0, S)[kt]:(S, WIDE)[kt]],
                                              start=(kt == 0), stop=(kt == 1), tile_position=(0, 32 * c))
                mm.then_inc(pv_done, 1)

            def body(i, s, last):
                pe.wait_ge(loaded[s], i * (16 * nload) + 16 * nload)
                for j in range(QUADS + 1):
                    n = i * (2 * QUADS) + (s * QUADS + j)
                    if j < QUADS:
                        for c in range(4):
                            pe.wait_ge(att_done, n * 4 + (c + 1))
                            scores(s, 4 * j + c)
                    if j:
                        pe.wait_ge(att_done, n * 4 + 4)
                        pe.wait_ge(o_out, n)
                        values(s, j - 1)
                pe.drain().then_inc(batch_done, 1)
            paired(pe, B, body)

        @block.vector
        def _(dve):
            dve.sem_inc(att_done, 4)
            dve.wait_ge(expdec_done, 1)
            nc.vector.tensor_scalar(neg[:], neg[:], -1.0, None, ALU.mult).then_inc(neg_done, 1)
            dve.wait_ge(masked, 1)
            for h in range(H):
                op = nc.vector.scalar_tensor_tensor(weight[:, h], dg[:], u[:, h:h + 1], weight[:, h],
                                                    ALU.mult, ALU.add)
            op.then_inc(weight_done, 1)
            dve.wait_ge(weight_done, 1)

            def body(i, s, last):
                for h in range(H):
                    dve.wait_ge(t_done, i * (2 * H) + (s * H + h + 1))
                    dve.wait_ge(pv_done, i * (2 * QUADS) + (s * QUADS + h // 4 + 1))
                    nc.vector.tensor_tensor(att[:, (h // 4) % 2, h % 4, 0:S], t_ps[:, h % 4, 0:S],
                                            weight[:, h], ALU.mult)
                    nc.vector.tensor_tensor(att[:, (h // 4) % 2, h % 4, S:WIDE], t_ps[:, h % 4, S:WIDE],
                                            weight[:, h, 0:P], ALU.mult).then_inc(att_done, 1)
            paired(dve, B, body)

        @block.scalar
        def _(act):
            act.sem_inc(o_out, 2)
            act.wait_ge(consts, NCONST)
            nc.scalar.activation(neg[:], dec[:], ACT.Exp).then_inc(expdec_done, 1)
            act.wait_ge(neg_done, 1)
            act.wait_ge(dist_done, 2)
            for h in range(H):
                op = nc.scalar.activation(weight[:, h], dist[:], ACT.Exp, scale=neg[:, h:h + 1])
            op.then_inc(powers_done, 1)

            def load_context(i, s):
                tok = at(act, i * (2 * S) + s * S, S)
                act.dma_start(kx[:, s], ctxT[:, tok].rearrange("(k p) n -> p k n", p=P)).then_inc(ctx_loaded[s], 16)
                act.dma_start(vx[:, s], ctx[tok, :].rearrange("(t p) c -> p t c", p=P)).then_inc(ctx_loaded[s], 16)

            def store_context(i, s):
                n = i * 2 + s
                tok = at(act, i * (2 * S) + s * S, S)
                half = at(act, i * S + s * (S // 2), S // 2)
                wait_apart(act, k_lo, n + 1, consts, NCONST)
                wait_apart(act, k_mid, n + 1, consts, NCONST)
                wait_apart(act, v_spread, n + 1, consts, NCONST)
                for a in range(3):
                    act.dma_start(next_k_parts[a, :, half].rearrange("(k p) n -> p k n", p=P),
                                  k_parts[:, s, a].bitcast(F32)).then_inc(ctx_stored[s], 16)
                act.dma_start(next_v_pad[tok, :].rearrange("(t p) c -> p t c", p=P),
                              vp[:, s].rearrange("p t h c -> p t (h c)")).then_inc(ctx_stored[s], 16)

            def body(i, s, last):
                n = i * 2 + s
                for j in range(QUADS):
                    if j == 0 and not last:
                        load_context(i + s, 1 - s)
                    if j == 1:
                        act.wait_ge(ctx_loaded[s], i * 32 + 32)
                        act.wait_ge(ctx_stored[s], i * 64 + 16)
                        nc.scalar.activation(k_parts[:, s, 0], kx[:, s], ACT.Copy).then_inc(k_hi, 1)
                        nc.scalar.activation(vp[:, s, :, :, 0:DH],
                                             vx[:, s].rearrange("p t (h c) -> p t h c", c=DH), ACT.Copy)\
                            .then_inc(v_spread, 1)
                    if j == 2:
                        act.wait_ge(k_rested, n + 1)
                        nc.scalar.activation(k_parts[:, s, 1], k_rest[:], ACT.Copy).then_inc(k_mid, 1)
                    if j == 3:
                        store_context(i, s)
                    act.wait_ge(stored[j % 2], i * (QUADS * 16) + (s * QUADS // 2 + j // 2) * 16 + 16)
                    act.wait_ge(pv_done, i * (2 * QUADS) + (s * QUADS + j + 3))
                    nc.scalar.activation(o_sb[:, j % 2], o_ps[:, j % 2, 0:S], ACT.Copy).then_inc(o_out, 1)
            act.wait_ge(vp_filled, 1)
            load_context(0, 0)
            paired(act, B, body)


def phase_rwkv_out(nc, y_T, ln_w, ln_b, gate, w_out, x_in, ident, x_out, q_parts):
    with Phase(nc, "rout") as ph:
        w = ph.sb("w", [P, KD, D])
        idt = ph.sb("idt", [P, P])
        lw = ph.sb("lw", [P, D])
        lb = ph.sb("lb", [P, D])
        power = ph.sb("power", [P, TPB])
        yT = ph.sb("yT", [P, 2, QUADS, BLK])
        g = ph.sb("g", [P, 2, TPB, D])
        gb = ph.sb("gb", [P, 2, TPB, D])
        x = ph.sb("x", [P, 2, TPB, D])
        yc = ph.sb("yc", [P, TPB, D])
        sq = ph.sb("sq", [P, TPB, D])
        sums = ph.sb("sums", [P, TPB * H])
        mean = ph.sb("mean", [P, TPB * H])
        sqs = ph.sb("sqs", [P, TPB * H])
        var = ph.sb("var", [P, TPB * H])
        std = ph.sb("std", [P, TPB * H])
        newton = ph.sb("newton", [P, TPB * H])
        rstd = ph.sb("rstd", [P, TPB * H])
        z = ph.sb("z", [P, TPB, D])
        zT = ph.sb("zT", [P, KD, BLK])
        r = ph.sb("r", [P, TPB, D])
        stats = ph.sb("stats", [P, TPB, 6])
        mv = ph.sb("mv", [P, TPB, 2])
        vare = ph.sb("vare", [P, TPB])
        ln_rstd = ph.sb("ln_rstd", [P, TPB])
        xo = ph.sb("xo", [P, 2, TPB, D])
        parts = ph.sb("parts", [P, 2, 3, KD, BLK], BF16)
        rest = ph.sb("rest", [P, KD, BLK])
        y_ps = ph.ps("y_ps", [P, TPB, QUADS, P])
        turn_ps = ph.ps("turn_ps", [P, KD, BLK])
        o_ps = ph.ps("o_ps", [P, TPB, D])
        consts = ph.sem("consts")
        NCONST = 16 * 4
        power_set = ph.sem("power_set")
        y_loaded = [ph.sem(f"y_loaded{s}") for s in range(2)]
        loaded = [ph.sem(f"loaded{s}") for s in range(2)]
        y_done = ph.sem("y_done")
        step = ph.sem("step")
        centred = ph.sem("centred")
        squared = ph.sem("squared")
        sqs_done = ph.sem("sqs_done")
        var_done = ph.sem("var_done")
        std_done = ph.sem("std_done")
        yn_done = ph.sem("yn_done")
        gated = ph.sem("gated")
        gates_done = ph.sem("gates_done")
        z_done = ph.sem("z_done")
        zT_done = ph.sem("zT_done")
        zT_out = ph.sem("zT_out")
        o_done = ph.sem("o_done")
        summed = ph.sem("summed")
        stats_done = ph.sem("stats_done")
        mv_done = ph.sem("mv_done")
        vare_done = ph.sem("vare_done")
        ln_rstd_done = ph.sem("ln_rstd_done")
        normed = ph.sem("normed")
        xT_done = ph.sem("xT_done")
        hi_done = ph.sem("hi_done")
        rest_done = ph.sem("rest_done")
        mid_done = ph.sem("mid_done")
        lo_done = ph.sem("lo_done")
        stored = [ph.sem(f"stored{s}") for s in range(2)]
        block = ph.block()
        NSTORE = 4

        @block.sync
        def _(sp):
            for s in range(2):
                sp.sem_inc(stored[s], 16)

            def load_y(i, s):
                tok = at(sp, i * (2 * BLK) + s * BLK, BLK)
                if not (isinstance(i, int) and i == 0):
                    wait_apart(sp, y_done, i * 2 + (s - 1), consts, NCONST)
                sp.dma_start(yT[:, s], y_T[:, :, tok].rearrange("g p n -> p g n")).then_inc(y_loaded[s], 16)

            def load(i, s):
                tok = at(sp, i * (2 * BLK) + s * BLK, BLK)
                wait_apart(sp, summed, i * 2 + (s + 1), consts, NCONST)
                sp.dma_start(g[:, s], gate[tok, :].rearrange("(t p) c -> p t c", p=P)).then_inc(loaded[s], 16)
                sp.dma_start(x[:, s], x_in[tok, :].rearrange("(t p) c -> p t c", p=P)).then_inc(loaded[s], 16)
            load_y(0, 0)
            sp.dma_start(idt[:], ident).then_inc(consts, 16)
            sp.dma_start(lw[:], ln_w.partition_broadcast(P)).then_inc(consts, 16)
            sp.dma_start(lb[:], ln_b.partition_broadcast(P)).then_inc(consts, 16)
            sp.dma_start(w[:], w_out.rearrange("(k p) n -> p k n", p=P)).then_inc(consts, 16)
            load(0, 0)
            load_y(0, 1)
            load(0, 1)

            def store_parts(i, s):
                half = at(sp, i * BLK + s * (BLK // 2), BLK // 2)
                wait_apart(sp, lo_done, i * 2 + (s + 2), consts, NCONST)
                for a in range(3):
                    sp.dma_start(q_parts[a, :, half].rearrange("(k p) n -> p k n", p=P),
                                 parts[:, s, a].bitcast(F32)).then_inc(stored[s], 16)

            def body(i, s, first, last):
                more = not isinstance(i, int) or i == 0
                if more:
                    load_y(i + 1, s)
                if not first:
                    store_parts(i + s - 1, 1 - s)
                if more:
                    load(i + 1, s)
                tok = at(sp, i * (2 * BLK) + s * BLK, BLK)
                wait_apart(sp, normed, i * 2 + (s + 1), consts, NCONST)
                sp.dma_start(x_out[tok, :].rearrange("(t p) c -> p t c", p=P), xo[:, s]).then_inc(stored[s], 16)
            paired_first(sp, NBLK, body)
            store_parts(NBLK // 2 - 1, 1)
            for s in range(2):
                sp.wait_ge(stored[s], NBLK // 2 * 16 * NSTORE + 16)

        @block.tensor
        def _(pe):
            pe.wait_ge(consts, NCONST)

            def turn_y(i, s):
                pe.wait_ge(y_loaded[s], i * 16 + 16)
                pe.wait_ge(centred, i * 2 + (s + 1))
                for t in range(TPB):
                    for q in range(QUADS):
                        mm = nc.tensor.transpose(y_ps[:, t, q], yT[:, s, q, t * P:(t + 1) * P], idt[:])
                mm.then_inc(y_done, 1)

            def turn_z(i, s):
                pe.wait_ge(z_done, i * 2 + (s + 1))
                pe.wait_ge(rest_done, i * 2 + (s + 1))
                for t in range(TPB):
                    for k in range(KD):
                        mm = nc.tensor.transpose(turn_ps[:, k, t * P:(t + 1) * P], z[:, t, k * P:(k + 1) * P],
                                                 idt[:])
                mm.then_inc(zT_done, 1)

            def body(i, s, last):
                n = i * 2 + s
                pe.wait_ge(zT_out, n + 1)
                pe.wait_ge(summed, n + 2)
                for t in range(TPB):
                    for k in range(KD):
                        mm = nc.tensor.matmul(o_ps[:, t], zT[:, k, t * P:(t + 1) * P], w[:, k],
                                              start=(k == 0), stop=(k == KD - 1))
                mm.then_inc(o_done, 1)
                if not isinstance(i, int):
                    turn_y(i + 1, s)
                if not last:
                    turn_z(i + s, 1 - s)
                    pe.wait_ge(zT_out, n + 2)
                else:
                    pe.wait_ge(rest_done, n + 2)
                pe.wait_ge(normed, n + 1)
                for t in range(TPB):
                    for k in range(KD):
                        mm = nc.tensor.transpose(turn_ps[:, k, t * P:(t + 1) * P],
                                                 xo[:, s, t, k * P:(k + 1) * P], idt[:])
                mm.then_inc(xT_done, 1)
            turn_y(0, 0)
            turn_y(0, 1)
            turn_z(0, 0)
            paired(pe, NBLK, body)

        def heads(ap):
            return ap.rearrange("p t (h c) -> p (t h) c", c=DH)

        def spread(ap):
            return ap.unsqueeze(2).broadcast_to([P, TPB * H, DH])

        @block.vector
        def _(dve):
            dve.sem_inc(centred, 1)
            dve.sem_inc(zT_done, 1)
            dve.sem_inc(summed, 2)
            dve.sem_inc(rest_done, 2)
            dve.sem_inc(lo_done, 1)
            dve.wait_ge(consts, NCONST)
            STEPS = 7
            y_heads = y_ps[:].rearrange("p t q (c r) -> p (t q c) r", r=32)[:, :, 0:DH]

            def chain(n, at_step):
                def link(op):
                    nonlocal at_step
                    at_step += 1
                    op.then_inc(step, 1)
                    dve.wait_ge(step, n * STEPS + at_step)
                return link

            def centre(i, s):
                n = i * 2 + s
                link = chain(n, 0)
                dve.wait_ge(y_done, n + 1)
                link(nc.vector.tensor_reduce(sums[:], y_heads, axis=AX.X, op=ALU.add))
                link(nc.vector.tensor_scalar(mean[:], sums[:], 1.0 / DH, None, ALU.mult))
                nc.vector.tensor_tensor(heads(yc[:]), y_heads, spread(mean[:]), ALU.subtract).then_inc(centred, 1)

            def variance(i, s):
                n = i * 2 + s
                dve.wait_ge(squared, n + 1)
                nc.vector.tensor_reduce(sqs[:], heads(sq[:]), axis=AX.X, op=ALU.add).then_inc(sqs_done, 1)
                dve.wait_ge(sqs_done, n + 1)
                nc.vector.tensor_scalar(var[:], sqs[:], 1.0 / DH, GN_EPS, ALU.mult, ALU.add).then_inc(var_done, 1)

            def scale(i, s):
                n = i * 2 + s
                link = chain(n, 2)
                dve.wait_ge(var_done, n + 1)
                dve.wait_ge(std_done, n + 1)
                link(nc.vector.reciprocal(rstd[:], std[:]))
                link(nc.vector.tensor_tensor(newton[:], rstd[:], rstd[:], ALU.mult))
                link(nc.vector.tensor_tensor(newton[:], newton[:], var[:], ALU.mult))
                link(nc.vector.tensor_scalar(newton[:], newton[:], -0.5, 1.5, ALU.mult, ALU.add))
                link(nc.vector.tensor_tensor(rstd[:], rstd[:], newton[:], ALU.mult))
                dve.wait_ge(centred, n + 2)
                nc.vector.tensor_tensor(heads(yc[:]), heads(yc[:]), spread(rstd[:]), ALU.mult).then_inc(yn_done, 1)

            def apply_gate(i, s):
                n = i * 2 + s
                dve.wait_ge(yn_done, n + 1)
                dve.wait_ge(gates_done, n + 1)
                nc.vector.tensor_tensor(yc[:], yc[:], g[:, s], ALU.mult).then_inc(gated, 1)
                dve.wait_ge(gated, n + 1)
                dve.wait_ge(zT_done, n + 1)
                nc.vector.tensor_tensor(z[:], yc[:], gb[:, s], ALU.add).then_inc(z_done, 1)

            def add_up(i, s):
                n = i * 2 + s
                dve.wait_ge(o_done, n + 1)
                dve.wait_ge(loaded[s], i * 32 + 32)
                nc.vector.tensor_tensor(r[:], o_ps[:], x[:, s], ALU.add).then_inc(summed, 1)
                dve.wait_ge(summed, n + 3)
                for t in range(TPB):
                    op = nc.vector.bn_stats(stats[:, t], r[:, t])
                op.then_inc(stats_done, 1)
                wait_apart(dve, stats_done, n + 1, consts, NCONST)
                for t in range(TPB):
                    op = nc.vector.bn_aggr(mv[:, t], stats[:, t])
                op.then_inc(mv_done, 1)

            def normalise(i, s):
                n = i * 2 + s
                dve.wait_ge(stored[s], i * (16 * NSTORE) + 16)
                dve.wait_ge(mv_done, n + 1)
                dve.wait_ge(ln_rstd_done, n + 1)
                for t in range(TPB):
                    op = nc.vector.tensor_scalar(xo[:, s, t], r[:, t], mv[:, t, 0:1], ln_rstd[:, t:t + 1],
                                                 ALU.subtract, ALU.mult)
                op.then_inc(normed, 1)

            def split_rest(i, s):
                n = i * 2 + s
                dve.wait_ge(hi_done, n + 1)
                dve.wait_ge(lo_done, n + 1)
                nc.vector.tensor_tensor(rest[:], turn_ps[:], parts[:, s, 0], ALU.subtract).then_inc(rest_done, 1)

            def body(i, s, first, last):
                nxt, before = (i + s, 1 - s), (i + s - 1, 1 - s)
                if not last:
                    centre(*nxt)
                if not first:
                    split_rest(*before)
                if not last:
                    variance(*nxt)
                add_up(i, s)
                if not last:
                    scale(*nxt)
                    apply_gate(*nxt)
                normalise(i, s)
            for stage in (centre, variance, scale, apply_gate):
                stage(0, 0)
            paired_first(dve, NBLK, body)
            split_rest(NBLK // 2 - 1, 1)

        @block.scalar
        def _(act):
            def square_root(i, s):
                n = i * 2 + s
                act.wait_ge(centred, n + 2)
                nc.scalar.activation(sq[:], yc[:], ACT.Square).then_inc(squared, 1)
                act.wait_ge(var_done, n + 1)
                nc.scalar.activation(std[:], var[:], ACT.Sqrt).then_inc(std_done, 1)

            def copy_z(i, s):
                act.wait_ge(zT_done, i * 2 + (s + 2))
                for k in range(KD):
                    op = nc.scalar.activation(zT[:, k], turn_ps[:, k], ACT.Copy)
                op.then_inc(zT_out, 1)

            def body(i, s, last):
                if not last:
                    square_root(i + s, 1 - s)
                    copy_z(i + s, 1 - s)
                act.wait_ge(stored[s], i * (16 * NSTORE) + 16)
                act.wait_ge(xT_done, i * 2 + (s + 1))
                for k in range(KD):
                    op = nc.scalar.activation(parts[:, s, 0, k], turn_ps[:, k], ACT.Copy)
                op.then_inc(hi_done, 1)
            square_root(0, 0)
            copy_z(0, 0)
            paired(act, NBLK, body)

        @block.gpsimd
        def _(pool):
            nc.gpsimd.memset(power[:], -0.5).then_inc(power_set, 1)
            pool.wait_ge(consts, NCONST)
            pool.wait_ge(power_set, 1)

            def wide(ap):
                return ap.unsqueeze(1).broadcast_to([P, TPB, D])

            def weigh_gate(i, s):
                wait_apart(pool, loaded[s], i * 32 + 32, power_set, 1)
                nc.gpsimd.tensor_tensor(gb[:, s], g[:, s], wide(lb[:]), ALU.mult)
                nc.gpsimd.tensor_tensor(g[:, s], g[:, s], wide(lw[:]), ALU.mult).then_inc(gates_done, 1)

            def split(i, s):
                n = i * 2 + s
                wait_apart(pool, rest_done, n + 3, power_set, 1)
                nc.gpsimd.tensor_copy(parts[:, s, 1], rest[:]).then_inc(mid_done, 1)
                pool.wait_ge(mid_done, n + 1)
                nc.gpsimd.tensor_tensor(parts[:, s, 2], rest[:], parts[:, s, 1], ALU.subtract).then_inc(lo_done, 1)

            def body(i, s, first, last):
                n = i * 2 + s
                if not first:
                    split(i + s - 1, 1 - s)
                wait_apart(pool, mv_done, n + 1, power_set, 1)
                nc.gpsimd.tensor_scalar(vare[:], mv[:, :, 1], LN_EPS, None, ALU.add).then_inc(vare_done, 1)
                pool.wait_ge(vare_done, n + 1)
                nc.gpsimd.tensor_tensor(ln_rstd[:], vare[:], power[:], ALU.pow).then_inc(ln_rstd_done, 1)
                if not isinstance(i, int) or i == 0:
                    weigh_gate(i + 1, s)
            weigh_gate(0, 0)
            weigh_gate(0, 1)
            paired_first(pool, NBLK, body)
            split(NBLK // 2 - 1, 1)


def phase_moe(nc, x_in, xT, router_T, w1_T, w2_T, before, ident, y_sorted, positions, shares):
    with Phase(nc, "moe") as ph:
        NF = FFN // P
        NT = T // P
        NS = MOE_TILES
        BATCH = 8
        NB = 2 * NT // BATCH
        w1 = ph.sb("w1", [P, NE, KD, FFN])
        w2 = ph.sb("w2", [P, NE, NF, D])
        rw = ph.sb("rw", [P, KD, NE])
        idt = ph.sb("idt", [P, P])
        bef = ph.sb("bef", [P, P])
        ones = ph.sb("ones", [P, P])
        iota_e = ph.sb("iota_e", [P, NE])
        iota_t = ph.sb("iota_t", [P, NT])
        iota_s = ph.sb("iota_s", [P, NS])
        iota_p = ph.sb("iota_p", [P, P])
        token = ph.sb("token", [P, NT])
        E_LATE = NE - KD * T // (KD * FFN)
        xt = w1[:, E_LATE:NE].rearrange("p e k f -> p (e k f)").rearrange("p (k n) -> p k n", k=KD)
        scores = ph.sb("scores", [P, NT, NE])
        top = ph.sb("top", [P, NT, NE])
        top_i = ph.sb("top_i", [P, NT, NE], U32)
        best = ph.sb("best", [P, NT, NE])
        gap = ph.sb("gap", [P, NT])
        odds = ph.sb("odds", [P, NT])
        one_more = ph.sb("one_more", [P, NT])
        share = ph.sb("share", [P, 2, NT])
        chosen = ph.sb("chosen", [P, 2, NT, NE])
        either = ph.sb("either", [P, NT, NE])
        scan = ph.sb("scan", [P, 2, NT, NE])
        counts_gt = ph.sb("counts_gt", [P, NE, NT])
        tiles = ph.sb("tiles", [P, NE])
        ends = ph.sb("ends", [P, 2, NE])
        starts = ph.sb("starts", [P, NE])
        past = ph.sb("past", [P, NS, NE])
        owner = ph.sb("owner", [P, NS])
        owner_i = ph.sb("owner_i", [P, NS], I32)
        pos_e = ph.sb("pos_e", [P, NT, NE])
        pos = ph.sb("pos", [P, 2, NT])
        pos_i = ph.sb("pos_i", [P, 2, NT], I32)
        low_i = ph.sb("low_i", [P, 2, NT], I32)
        high_i = ph.sb("high_i", [P, 2, NT], I32)
        low = ph.sb("low", [P, 2 * NT])
        high = ph.sb("high", [P, 2 * NT])
        hot_low = ph.sb("hot_low", [P, 2, BATCH, P])
        hot_high = ph.sb("hot_high", [P, 2, BATCH, NS])
        source = ph.sb("source", [P, NS], I32)
        cur = ph.sb("cur", [P, 2], I32)
        xg = ph.sb("xg", [P, 2, D])
        xgT = ph.sb("xgT", [P, 2, KD, P])
        h = ph.sb("h", [P, 2, FFN])
        hT = ph.sb("hT", [P, 2, NF, P])
        y = ph.sb("y", [P, 2, D])
        sc_ps = ph.ps("sc_ps", [P, 2, 256])
        rank_ps = ph.ps("rank_ps", [P, 2, NT, NE])
        xT_ps = ph.ps("xT_ps", [P, KD, 256])
        h_ps = ph.ps("h_ps", [P, 2, BLK])
        hT_ps = ph.ps("hT_ps", [P, NF, P])
        y_ps = ph.ps("y_ps", [P, BLK])
        consts = ph.sem("consts")
        NCONST = 16 * 3
        weights = ph.sem("weights")
        x_columns = [ph.sem(f"x_columns{b}") for b in range(NBLK)]
        iotas = ph.sem("iotas")
        ones_set = ph.sem("ones_set")
        sc_done = ph.sem("sc_done")
        route = ph.sem("route")
        gap_done = ph.sem("gap_done")
        odds_done = ph.sem("odds_done")
        either_done = ph.sem("either_done")
        rank_done = ph.sem("rank_done")
        owner_done = ph.sem("owner_done")
        low_hot = ph.sem("low_hot")
        high_eq = ph.sem("high_eq")
        high_hot = ph.sem("high_hot")
        batch_used = ph.sem("batch_used")
        source_done = ph.sem("source_done")
        cur_set = ph.sem("cur_set")
        gathered = [ph.sem(f"gathered{s}") for s in range(2)]
        turned = ph.sem("turned")
        xT_out = ph.sem("xT_out")
        h_done = ph.sem("h_done")
        gelu_done = ph.sem("gelu_done")
        hT_done = ph.sem("hT_done")
        hT_out = ph.sem("hT_out")
        y_done = ph.sem("y_done")
        y_out = ph.sem("y_out")
        routes_stored = ph.sem("routes_stored")
        stored = [ph.sem(f"stored{s}") for s in range(2)]
        block = ph.block()

        @block.sync
        def _(sp):
            for s in range(2):
                sp.sem_inc(stored[s], 16)
            sp.dma_start(rw[:], router_T.rearrange("(k p) e -> p k e", p=P)).then_inc(consts, 16)
            sp.dma_start(bef[:], before).then_inc(consts, 16)
            sp.dma_start(idt[:], ident).then_inc(consts, 16)

            for b in range(NBLK):
                sp.dma_start(xt[:, :, b * BLK:(b + 1) * BLK],
                             xT[:, b * BLK:(b + 1) * BLK].rearrange("(k p) n -> p k n", p=P))\
                    .then_inc(x_columns[b], 16)
            for e in range(NE):
                sp.dma_start(w2[:, e], w2_T[e].rearrange("(f p) c -> p f c", p=P)).then_inc(weights, 16)
            for e in range(NE):
                if e == E_LATE:
                    sp.wait_ge(sc_done, 1)
                sp.dma_start(w1[:, e], w1_T[e].rearrange("(k p) f -> p k f", p=P)).then_inc(weights, 16)
            sp.wait_ge(route, ROUTE_STEPS)
            sp.dma_start(positions, pos_i[:].rearrange("p r t -> p (r t)")).then_inc(routes_stored, 16)
            sp.dma_start(shares, share[:].rearrange("p r t -> p (r t)")).then_inc(routes_stored, 16)

            def body(i, s, last):
                rows = at(sp, i * (2 * P) + s * P, P)
                wait_apart(sp, y_out, i * 2 + (s + 2), consts, NCONST)
                sp.dma_start(y_sorted[rows, :], y[:, s]).then_inc(stored[s], 16)
            paired(sp, NS, body)
            sp.wait_ge(routes_stored, 32)
            for s in range(2):
                sp.wait_ge(stored[s], NS // 2 * 16 + 16)

        @block.tensor
        def _(pe):
            pe.wait_ge(consts, NCONST)
            for b in range(NBLK):
                pe.wait_ge(x_columns[b], 16)
                for t in range(TPB):
                    for k in range(KD):
                        tile = b * TPB + t
                        nc.tensor.matmul(sc_ps[:, 0, tile * NE:(tile + 1) * NE], xt[:, k, tile * P:(tile + 1) * P],
                                         rw[:, k], start=(k == 0), stop=(k == KD - 1))
            pe.drain().then_inc(sc_done, 1)
            pe.wait_ge(either_done, 1)
            pe.wait_ge(ones_set, 1)
            nc.tensor.matmul(rank_ps[:, 0], bef[:], either[:].rearrange("p t e -> p (t e)"), start=True, stop=True)
            nc.tensor.matmul(rank_ps[:, 1], ones[:], either[:].rearrange("p t e -> p (t e)"), start=True, stop=True)\
                .then_inc(rank_done, 1)
            for b in range(NB):
                pe.wait_ge(low_hot, b + 1)
                pe.wait_ge(high_hot, b + 1)
                for t in range(BATCH):
                    mm = nc.tensor.matmul(sc_ps[:, 1, 0:NS], hot_low[:, b % 2, t], hot_high[:, b % 2, t],
                                          start=(b == 0 and t == 0), stop=(b == NB - 1 and t == BATCH - 1))
                mm.then_inc(batch_used, 1)
            pe.wait_ge(weights, 16 * 2 * NE)
            pe.wait_ge(owner_done, 1)

            def expert(j):
                return pe.value_load(owner_i[0:1, j:j + 1] if isinstance(j, int) else owner_i[0:1, ds(pe.snap(j), 1)],
                                     min_val=0, max_val=NE - 1)

            def turn_x(i, s):
                pe.wait_ge(gathered[s], i * 16 + 16)
                pe.wait_ge(xT_out, i * 2 + (s + 1))
                for k in range(KD):
                    mm = nc.tensor.transpose(xT_ps[:, k, 0:P], xg[:, s, k * P:(k + 1) * P], idt[:])
                mm.then_inc(turned, 1)

            def first(i, s):
                e = expert(i * 2 + s)
                pe.wait_ge(xT_out, i * 2 + (s + 2))
                for c in range(2):
                    pe.wait_ge(gelu_done, i * 4 + (s * 2 + c + 1))
                    for k in range(KD):
                        mm = nc.tensor.matmul(h_ps[:, c], xgT[:, s, k],
                                              w1[:, ds(e, 1), k, c * BLK:(c + 1) * BLK].rearrange("p a n -> p (a n)"),
                                              start=(k == 0), stop=(k == KD - 1))
                    mm.then_inc(h_done, 1)

            def turn_h(i, s):
                pe.wait_ge(gelu_done, i * 4 + (s * 2 + 4))
                for c in range(2):
                    pe.wait_ge(hT_out, i * 4 + (s * 2 + c + 1))
                    for f in range(4 * c, 4 * c + 4):
                        mm = nc.tensor.transpose(hT_ps[:, f], h[:, s, f * P:(f + 1) * P], idt[:])
                    mm.then_inc(hT_done, 1)

            def second(i, s):
                e = expert(i * 2 + s)
                pe.wait_ge(hT_out, i * 4 + (s * 2 + 4))
                pe.wait_ge(y_out, i * 2 + (s + 1))
                for f in range(NF):
                    mm = nc.tensor.matmul(y_ps[:, 0:D], hT[:, s, f],
                                          w2[:, ds(e, 1), f].rearrange("p a n -> p (a n)"),
                                          start=(f == 0), stop=(f == NF - 1))
                mm.then_inc(y_done, 1)

            def step(i, s, left):
                if left >= 1:
                    first(i + s, 1 - s)
                if left >= 2:
                    turn_x(i + 1, s)
                second(i, s)
                if left >= 1:
                    turn_h(i + s, 1 - s)
            turn_x(0, 0)
            first(0, 0)
            turn_x(0, 1)
            turn_h(0, 0)
            with pe.Fori(0, NS // 2 - 1) as i:
                step(i, 0, 2)
                step(i, 1, 2)
            step(NS // 2 - 1, 0, 1)
            step(NS // 2 - 1, 1, 0)

        @block.scalar
        def _(act):
            act.sem_inc(xT_out, 1)
            act.sem_inc(gelu_done, 2)
            act.wait_ge(gap_done, 1)
            nc.scalar.activation(odds[:], gap[:], ACT.Exp).then_inc(odds_done, 1)

            def copy_x(i, s):
                act.wait_ge(turned, i * 2 + (s + 3))
                nc.scalar.activation(xgT[:, s], xT_ps[:, :, 0:P], ACT.Copy).then_inc(xT_out, 1)

            def body(i, s, last):
                for c in range(2):
                    act.wait_ge(h_done, i * 4 + (s * 2 + c + 1))
                    nc.scalar.activation(h[:, s, c * BLK:(c + 1) * BLK], h_ps[:, c], ACT.Gelu).then_inc(gelu_done, 1)
                if not last:
                    copy_x(i + s, 1 - s)
            copy_x(0, 0)
            paired(act, NS, body)

        @block.gpsimd
        def _(pool):
            pool.sem_inc(turned, 2)
            nc.gpsimd.memset(ones[:], 1.0).then_inc(ones_set, 1)
            for tile, n, base, step, lanes in ((iota_e, NE, 0, 1, 0), (iota_t, NT, 0, P, 0), (iota_s, NS, 0, 1, 0),
                                               (iota_p, P, 0, 1, 0), (token, NT, 0, P, 1)):
                op = nc.gpsimd.iota(tile[:], pattern=[[step, n]], base=base, channel_multiplier=lanes,
                                    allow_small_or_imprecise_dtypes=True)
            op.then_inc(iotas, 1)
            pool.wait_ge(iotas, 1)
            for b in range(NB):
                pool.wait_ge(high_eq, b + 1)
                t = b * BATCH % NT
                nc.gpsimd.tensor_tensor(hot_high[:, b % 2], hot_high[:, b % 2],
                                        token[:, t:t + BATCH].unsqueeze(2).broadcast_to([P, BATCH, NS]),
                                        ALU.mult).then_inc(high_hot, 1)
            pool.wait_ge(source_done, 1)

            def body(i, s, last):
                wait_apart(pool, turned, i * 2 + (s + 1), source_done, 1)
                nc.gpsimd.tensor_copy(cur[:, s:s + 1], source[:, i * 2 + s:i * 2 + s + 1] if isinstance(i, int)
                                      else source[:, ds(pool.snap(i * 2 + s), 1)]).then_inc(cur_set, 1)
                wait_apart(pool, cur_set, i * 2 + (s + 1), source_done, 1)
                nc.gpsimd.indirect_dma_start(xg[:, s], None, x_in, bass.IndirectOffsetOnAxis(ap=cur[:, s:s + 1], axis=0))\
                    .then_inc(gathered[s], 16)
            paired(pool, NS, body)

        def over(ap, *shape):
            return ap.broadcast_to([P, *shape])

        @block.vector
        def _(dve):
            dve.sem_inc(hT_out, 2)
            dve.sem_inc(y_out, 1)
            done = 0

            def link(op):
                nonlocal done
                done += 1
                op.then_inc(route, 1)
                dve.wait_ge(route, done)
            dve.wait_ge(iotas, 1)
            dve.wait_ge(sc_done, 1)
            link(nc.vector.tensor_copy(scores[:].rearrange("p t e -> p (t e)"), sc_ps[:, 0]))
            for t in range(NT):
                op = nc.vector.max(out=top[:, t], in_=scores[:, t])
            link(op)
            nc.vector.tensor_tensor(gap[:], top[:, :, 1], top[:, :, 0], ALU.subtract).then_inc(gap_done, 1)
            for t in range(NT):
                op = nc.vector.max_index(out=top_i[:, t], in_max=top[:, t], in_values=scores[:, t])
            link(op)
            link(nc.vector.tensor_copy(best[:], top_i[:]))
            for r in range(2):
                op = nc.vector.tensor_tensor(chosen[:, r], over(iota_e[:].unsqueeze(1), NT, NE),
                                             over(best[:, :, r:r + 1], NT, NE), ALU.is_equal)
            link(op)
            nc.vector.tensor_tensor(either[:], chosen[:, 0], chosen[:, 1], ALU.add).then_inc(either_done, 1)
            dve.wait_ge(odds_done, 1)
            link(nc.vector.tensor_scalar(one_more[:], odds[:], 1.0, None, ALU.add))
            link(nc.vector.reciprocal(share[:, 0], one_more[:]))
            link(nc.vector.tensor_tensor(share[:, 1], share[:, 0], odds[:], ALU.mult))
            dve.wait_ge(rank_done, 1)
            link(nc.vector.tensor_copy(scan[:, 0], rank_ps[:, 1]))
            a = 0
            d = 1
            while d < NT:
                nc.vector.tensor_copy(scan[:, 1 - a, 0:d], scan[:, a, 0:d])
                link(nc.vector.tensor_tensor(scan[:, 1 - a, d:NT], scan[:, a, d:NT], scan[:, a, 0:NT - d], ALU.add))
                a, d = 1 - a, 2 * d
            link(nc.vector.tensor_tensor(counts_gt[:], over(scan[:, a, NT - 1].unsqueeze(2), NE, NT),
                                         over(iota_t[:].unsqueeze(1), NE, NT), ALU.is_gt))
            link(nc.vector.tensor_reduce(tiles[:], counts_gt[:], axis=AX.X, op=ALU.add))
            b = 0
            link(nc.vector.tensor_copy(ends[:, 0], tiles[:]))
            for d in (1, 2, 4):
                nc.vector.tensor_copy(ends[:, 1 - b, 0:d], ends[:, b, 0:d])
                link(nc.vector.tensor_tensor(ends[:, 1 - b, d:NE], ends[:, b, d:NE], ends[:, b, 0:NE - d], ALU.add))
                b = 1 - b
            link(nc.vector.tensor_tensor(past[:], over(iota_s[:].unsqueeze(2), NS, NE),
                                         over(ends[:, b].unsqueeze(1), NS, NE), ALU.is_ge))
            link(nc.vector.tensor_reduce(owner[:], past[:], axis=AX.X, op=ALU.add))
            link(nc.vector.tensor_scalar(owner[:], owner[:], float(NE - 1), None, ALU.min))
            nc.vector.tensor_copy(owner_i[:], owner[:]).then_inc(owner_done, 1)
            link(nc.vector.tensor_tensor(starts[:], ends[:, b], tiles[:], ALU.subtract))
            link(nc.vector.tensor_scalar(starts[:], starts[:], float(P), None, ALU.mult))
            link(nc.vector.tensor_tensor(pos_e[:], scan[:, a], rank_ps[:, 1], ALU.subtract))
            link(nc.vector.tensor_tensor(pos_e[:], pos_e[:], rank_ps[:, 0], ALU.add))
            link(nc.vector.tensor_tensor(pos_e[:], pos_e[:], over(starts[:].unsqueeze(1), NT, NE), ALU.add))
            for r in range(2):
                op = nc.vector.tensor_tensor(chosen[:, r], chosen[:, r], pos_e[:], ALU.mult)
            link(op)
            link(nc.vector.tensor_reduce(pos[:], chosen[:], axis=AX.X, op=ALU.add))
            link(nc.vector.tensor_copy(pos_i[:], pos[:]))
            nc.vector.tensor_scalar(low_i[:], pos_i[:], P - 1, None, ALU.bitwise_and)
            link(nc.vector.tensor_scalar(high_i[:], pos_i[:], P.bit_length() - 1, None, ALU.logical_shift_right))
            nc.vector.tensor_copy(high[:], high_i[:].rearrange("p r t -> p (r t)"))
            link(nc.vector.tensor_copy(low[:], low_i[:].rearrange("p r t -> p (r t)")))
            assert done == ROUTE_STEPS, done
            for b in range(NB):
                if b >= 2:
                    dve.wait_ge(batch_used, b - 1)
                nc.vector.tensor_tensor(hot_low[:, b % 2], over(iota_p[:].unsqueeze(1), BATCH, P),
                                        over(low[:, b * BATCH:(b + 1) * BATCH].unsqueeze(2), BATCH, P),
                                        ALU.is_equal).then_inc(low_hot, 1)
                nc.vector.tensor_tensor(hot_high[:, b % 2], over(iota_s[:].unsqueeze(1), BATCH, NS),
                                        over(high[:, b * BATCH:(b + 1) * BATCH].unsqueeze(2), BATCH, NS),
                                        ALU.is_equal).then_inc(high_eq, 1)
            dve.wait_ge(batch_used, NB)
            nc.vector.tensor_copy(source[:], sc_ps[:, 1, 0:NS]).then_inc(source_done, 1)

            def body(i, s, last):
                for c in range(2):
                    dve.wait_ge(hT_done, i * 4 + (s * 2 + c + 1))
                    nc.vector.tensor_copy(hT[:, s, 4 * c:4 * c + 4], hT_ps[:, 4 * c:4 * c + 4]).then_inc(hT_out, 1)
                dve.wait_ge(y_done, i * 2 + (s + 1))
                dve.wait_ge(stored[s], i * 16 + 16)
                nc.vector.tensor_copy(y[:, s], y_ps[:, 0:D]).then_inc(y_out, 1)
            paired(dve, NS, body)


def phase_experts(nc, x_in, xT, gate_w, gate_b, expert_w, expert_b, ident, x_out):
    with Phase(nc, "ffn") as ph:
        EP = NE // 2
        w = ph.sb("w", [P, KD, EP, 2, D])
        eb = ph.sb("eb", [NE, D])
        gw = ph.sb("gw", [P, KD, NE])
        gb = ph.sb("gb", [P, NE])
        idt = ph.sb("idt", [P, P])
        xt = ph.sb("xt", [P, 2, KD, BLK])
        x = ph.sb("x", [P, 2, TPB, D])
        lg = ph.sb("lg", [P, TPB, NE])
        mx = ph.sb("mx", [P, TPB])
        ex = ph.sb("ex", [P, TPB, NE])
        sm = ph.sb("sm", [P, TPB])
        rs = ph.sb("rs", [P, TPB])
        gate = ph.sb("gate", [P, TPB, NE])
        sel = ph.sb("sel", [P, TPB, NE])
        nil = ph.sb("nil", [P, TPB])
        we = ph.sb("we", [P, 2, TPB, NE])
        weT = ph.sb("weT", [NE, TPB, P])
        acc = ph.sb("acc", [P, 2, TPB, D])
        power = ph.sb("power", [P, TPB])
        stats = ph.sb("stats", [P, TPB, 6])
        mv = ph.sb("mv", [P, TPB, 2])
        vare = ph.sb("vare", [P, TPB])
        rstd = ph.sb("rstd", [P, TPB])
        xo = ph.sb("xo", [P, 2, TPB, D])
        y_ps = ph.ps("y_ps", [P, 4, 2, D])
        b_ps = ph.ps("b_ps", [P, TPB, D])
        lg_ps = ph.ps("lg_ps", [P, TPB, P])
        wT_ps = ph.ps("wT_ps", [P, TPB, P])
        consts = ph.sem("consts")
        NCONST = 16 * (4 + NE)
        loaded = [ph.sem(f"loaded{s}") for s in range(2)]
        in_free = ph.sem("in_free")
        lg_done = ph.sem("lg_done")
        step = ph.sem("step")
        shift_done = ph.sem("shift_done")
        exp_done = ph.sem("exp_done")
        we_done = ph.sem("we_done")
        wT_done = ph.sem("wT_done")
        wT_out = ph.sem("wT_out")
        b_done = ph.sem("b_done")
        b_out = ph.sem("b_out")
        y_done = ph.sem("y_done")
        half_done = ph.sem("half_done")
        y_out = ph.sem("y_out")
        power_set = ph.sem("power_set")
        stats_done = ph.sem("stats_done")
        mv_done = ph.sem("mv_done")
        vare_done = ph.sem("vare_done")
        rstd_done = ph.sem("rstd_done")
        normed = ph.sem("normed")
        stored = [ph.sem(f"stored{s}") for s in range(2)]
        block = ph.block()
        NY = TPB * EP

        @block.sync
        def _(sp):
            for s in range(2):
                sp.sem_inc(stored[s], 16)
            def load(i, s):
                tok = at(sp, i * (2 * BLK) + s * BLK, BLK)
                wait_apart(sp, in_free, i * 2 + (s + 1), consts, NCONST)
                sp.dma_start(xt[:, s], xT[:, tok].rearrange("(k p) n -> p k n", p=P)).then_inc(loaded[s], 16)
                sp.dma_start(x[:, s], x_in[tok, :].rearrange("(t p) c -> p t c", p=P)).then_inc(loaded[s], 16)
            load(0, 0)
            sp.dma_start(eb[:], expert_b).then_inc(consts, 16)
            sp.dma_start(gw[:], gate_w.rearrange("(k p) e -> p k e", p=P)).then_inc(consts, 16)
            sp.dma_start(gb[:], gate_b.partition_broadcast(P)).then_inc(consts, 16)
            sp.dma_start(idt[:], ident).then_inc(consts, 16)
            for e in range(NE):
                sp.dma_start(w[:, :, e // 2, e % 2], expert_w[e].rearrange("(k p) c -> p k c", p=P))\
                    .then_inc(consts, 16)

            def body(i, s, last):
                if not last:
                    load(i + s, 1 - s)
                tok = at(sp, i * (2 * BLK) + s * BLK, BLK)
                wait_apart(sp, normed, i * 2 + (s + 1), consts, NCONST)
                sp.dma_start(x_out[tok, :].rearrange("(t p) c -> p t c", p=P), xo[:, s]).then_inc(stored[s], 16)
            paired(sp, NBLK, body)
            for s in range(2):
                sp.wait_ge(stored[s], NBLK // 2 * 16 + 16)

        @block.tensor
        def _(pe):
            pe.wait_ge(consts, NCONST)

            def logits(i, s):
                pe.wait_ge(loaded[s], i * 32 + 32)
                for t in range(TPB):
                    for k in range(KD):
                        mm = nc.tensor.matmul(lg_ps[:, t, 0:NE], xt[:, s, k, t * P:(t + 1) * P], gw[:, k],
                                              start=(k == 0), stop=(k == KD - 1))
                mm.then_inc(lg_done, 1)

            def turn_weights(i, s):
                pe.wait_ge(we_done, i * 2 + (s + 1))
                for t in range(TPB):
                    mm = nc.tensor.transpose(wT_ps[0:NE, t], we[:, s, t], idt[:])
                mm.then_inc(wT_done, 1)

            def product(i, s, m):
                pe.wait_ge(y_out, i * (2 * NY) + (s * NY + m + 1))
                g, t = divmod(m, TPB)
                for k in range(KD):
                    mm = nc.tensor.matmul(y_ps[:, m % 4], xt[:, s, k, t * P:(t + 1) * P], w[:, k, g],
                                          start=(k == 0), stop=(k == KD - 1))
                mm.then_inc(y_done, 1)

            def body(i, s, last):
                for m in range(NY):
                    product(i, s, m)
                    if m == NY - 2 and not last:
                        turn_weights(i + s, 1 - s)
                    if m == 0:
                        pe.wait_ge(wT_out, i * 2 + (s + 1))
                        pe.wait_ge(b_out, i * 2 + (s + 1))
                        for t in range(TPB):
                            mm = nc.tensor.matmul(b_ps[:, t], weT[:, t], eb[:], start=True, stop=True)
                        mm.then_inc(b_done, 1)
                    if m == NY // 2 and not last:
                        logits(i + s, 1 - s)
                pe.drain().then_inc(in_free, 1)
            logits(0, 0)
            turn_weights(0, 0)
            paired(pe, NBLK, body)

        @block.scalar
        def _(act):
            def body(i, s, last):
                act.wait_ge(shift_done, i * 2 + (s + 1))
                nc.scalar.activation(ex[:], lg[:], ACT.Exp).then_inc(exp_done, 1)
                act.wait_ge(wT_done, i * 2 + (s + 1))
                act.wait_ge(b_done, i * 2 + (s + 1))
                nc.scalar.activation(weT[:], wT_ps[0:NE], ACT.Copy).then_inc(wT_out, 1)
            paired(act, NBLK, body)

        def each(ap):
            return ap.unsqueeze(2).broadcast_to([P, TPB, NE])

        @block.vector
        def _(dve):
            dve.sem_inc(in_free, 2)
            dve.sem_inc(y_out, 4)
            dve.sem_inc(b_out, 1)
            dve.sem_inc(b_done, 1)
            dve.wait_ge(consts, NCONST)
            STEPS = 11

            def gates(i, s):
                n = i * 2 + s
                done = 0

                def link(op):
                    nonlocal done
                    done += 1
                    op.then_inc(step, 1)
                    dve.wait_ge(step, n * STEPS + done)
                dve.wait_ge(lg_done, n + 1)
                link(nc.vector.tensor_tensor(lg[:], lg_ps[:, :, 0:NE],
                                             gb[:].unsqueeze(1).broadcast_to([P, TPB, NE]), ALU.add))
                link(nc.vector.tensor_reduce(mx[:], lg[:], axis=AX.X, op=ALU.max))
                nc.vector.tensor_tensor(lg[:], lg[:], each(mx[:]), ALU.subtract).then_inc(shift_done, 1)
                dve.wait_ge(exp_done, n + 1)
                link(nc.vector.tensor_reduce(sm[:], ex[:], axis=AX.X, op=ALU.add))
                link(nc.vector.reciprocal(rs[:], sm[:]))
                link(nc.vector.tensor_tensor(gate[:], ex[:], each(rs[:]), ALU.mult))
                link(nc.vector.tensor_scalar(sel[:], gate[:], 0.1, None, ALU.is_ge))
                link(nc.vector.tensor_tensor(gate[:], gate[:], sel[:], ALU.mult))
                link(nc.vector.tensor_reduce(sm[:], gate[:], axis=AX.X, op=ALU.add))
                link(nc.vector.tensor_scalar(nil[:], sm[:], 0.0, None, ALU.is_equal))
                link(nc.vector.tensor_tensor(sm[:], sm[:], nil[:], ALU.add))
                link(nc.vector.reciprocal(rs[:], sm[:]))
                nc.vector.tensor_tensor(we[:, s], gate[:], each(rs[:]), ALU.mult).then_inc(we_done, 1)

            def statistics(n, s):
                dve.wait_ge(y_out, n * NY + (NY + 4))
                for t in range(TPB):
                    op = nc.vector.bn_stats(stats[:, t], acc[:, s, t])
                op.then_inc(stats_done, 1)
                wait_apart(dve, stats_done, n + 1, consts, NCONST)
                for t in range(TPB):
                    op = nc.vector.bn_aggr(mv[:, t], stats[:, t])
                op.then_inc(mv_done, 1)

            def normalise(n, i, s):
                dve.wait_ge(stored[s], i * 16 + 16)
                dve.wait_ge(mv_done, n + 1)
                dve.wait_ge(rstd_done, n + 1)
                for t in range(TPB):
                    op = nc.vector.tensor_scalar(xo[:, s, t], acc[:, s, t], mv[:, t, 0:1], rstd[:, t:t + 1],
                                                 ALU.subtract, ALU.mult)
                op.then_inc(normed, 1)

            def body(i, s, first, last):
                n = i * 2 + s
                dve.wait_ge(loaded[s], i * 32 + 32)
                dve.wait_ge(b_done, n + 2)
                nc.vector.tensor_tensor(acc[:, s], b_ps[:], x[:, s], ALU.add).then_inc(b_out, 1)
                dve.wait_ge(b_out, n + 2)
                for m in range(0, NY, 2):
                    g, t = divmod(m, TPB)
                    if g:
                        dve.wait_ge(y_out, i * (2 * NY) + (s * NY + m + 2))
                    for e in range(2):
                        for d in range(2):
                            if e == 0:
                                dve.wait_ge(y_done, i * (2 * NY) + (s * NY + m + d + 1))
                            else:
                                dve.wait_ge(half_done, i * (2 * NY) + (s * NY + m + d + 1))
                            nc.vector.scalar_tensor_tensor(acc[:, s, t + d], y_ps[:, (m + d) % 4, e],
                                                           we[:, s, t + d, 2 * g + e:2 * g + e + 1],
                                                           acc[:, s, t + d], ALU.mult, ALU.add)\
                                .then_inc(y_out if e else half_done, 1)
                    if m == 2 and not first:
                        normalise(n - 1, i + s - 1, 1 - s)
                    if m == NY * 5 // 8 and not last:
                        gates(i + s, 1 - s)
                statistics(n, s)
            gates(0, 0)
            paired_first(dve, NBLK, body)
            normalise(NBLK - 1, NBLK // 2 - 1, 1)

        @block.gpsimd
        def _(pool):
            nc.gpsimd.memset(power[:], -0.5).then_inc(power_set, 1)

            def body(i, s, last):
                wait_apart(pool, mv_done, i * 2 + (s + 1), power_set, 1)
                nc.gpsimd.tensor_scalar(vare[:], mv[:, :, 1], LN_EPS, None, ALU.add).then_inc(vare_done, 1)
                pool.wait_ge(vare_done, i * 2 + (s + 1))
                nc.gpsimd.tensor_tensor(rstd[:], vare[:], power[:], ALU.pow).then_inc(rstd_done, 1)
            paired(pool, NBLK, body)


def window_masks():
    p, n = np.arange(P)[:, None], np.arange(P)[None, :]
    masked = np.stack([n > p, n < p, n > p, n < p])
    return np.where(masked, -1e30, 0.0).astype(np.float32)


def bass_decoder_layers(nc, a):
    def scratch(name, *shape):
        return nc.dram_tensor(f"scratch_{name}", list(shape), F32, kind="Internal").ap()

    qk_parts = scratch("qk_parts", 2, 3, D, T // 2)
    v_pad = scratch("v_pad", T, H * 32)
    win_parts = scratch("win_parts", 2, 3, D, T // 2)
    win_v_pad = scratch("win_v_pad", T, H * 32)
    o_T = scratch("o_T", QUADS, P, T)
    x1, x1T = scratch("x1", T, D), scratch("x1T", D, T)
    x2, x2T = scratch("x2", T, D), scratch("x2T", D, T)
    x3, x3T = scratch("x3", T, D), scratch("x3T", D, T)
    x4 = scratch("x4", T, D)
    x5, x5T = scratch("x5", T, D), scratch("x5T", D, T)
    cross_T = scratch("cross_T", DM // P, P, T)
    routes = (scratch("y_sorted", MOE_TILES * P, D),
              nc.dram_tensor("scratch_positions", [P, 2 * T // P], I32, kind="Internal").ap(),
              scratch("shares", P, 2 * T // P))
    gate = scratch("gate", T, D)

    phase_qkv(nc, a["xT"], a["w_qkv"], a["b_qkv"], qk_parts, v_pad)
    phase_core(nc, "self", qk_parts, v_pad, a["ident"], o_T, DH ** -0.5)
    phase_post(nc, "post0", o_T, QUADS, a["w_proj"], True, a["b_proj"], a["x"], a["ident"], x1, x1T)
    phase_cross(nc, x1T, a["ctxT"], a["Wq"], a["bq"], a["Wk"], a["bk"], a["Wv"], a["bv"], a["ident"], cross_T)
    phase_post(nc, "post1", cross_T, DM // P, a["Wu"], False, a["bu"], x1, a["ident"], x2, x2T)
    phase_moe(nc, x2, x2T, a["router_T"], a["w1_T"], a["w2_T"], a["before"], a["ident"], *routes)
    phase_post(nc, "post2", None, 0, None, False, None, x2, a["ident"], x3, x3T, routes)
    phase_rwkv_in(nc, x3T, [a["maa_r"], a["maa_k"], a["maa_v"], a["maa_g"]],
                  [a["WrT"], a["WkT"], a["WvT"], a["WgT"]], qk_parts, v_pad, gate)
    phase_rwkv_core(nc, qk_parts, v_pad, a["decay"], a["faaaa"], a["diag"], o_T,
                    a["ctxT"], a["ctx"], win_parts[1], win_v_pad)
    phase_rwkv_out(nc, o_T, a["ln_w"], a["ln_b"], gate, a["WoT"], x3, a["ident"], x4, win_parts[0])
    phase_core(nc, "window", win_parts, win_v_pad, a["ident"], o_T, 1.0, a["masks"])
    phase_post(nc, "post4", o_T, QUADS, None, True, None, x4, a["ident"], x5, x5T)
    phase_experts(nc, x5, x5T, a["gate_w"], a["gate_b"], a["expert_w"], a["expert_b"], a["ident"],
                  a["out"])


def kernel(**inputs):
    import concourse.bacc as _bacc
    from concourse.bass_utils import run_bass_kernel_spmd as _run

    i = {name: np.asarray(value) for name, value in inputs.items()}
    x, ctx = i["x"].reshape(T, D), i["ctx_1024"].reshape(T, D)
    layout = dict(
        x=x, xT=x.T, ctx=ctx, ctxT=ctx.T,
        w_qkv=i["L0_attn_w_qkv"], b_qkv=i["L0_attn_b_qkv"], w_proj=i["L0_attn_w_proj"], b_proj=i["L0_attn_b_proj"],
        Wq=i["L0_xattn_Wq"], bq=i["L0_xattn_bq"], Wk=i["L0_xattn_Wk"], bk=i["L0_xattn_bk"],
        Wv=i["L0_xattn_Wv"], bv=i["L0_xattn_bv"], Wu=i["L0_xattn_Wu"], bu=i["L0_xattn_bu"],
        router_T=i["L0_ffn_router_w"].T, w1_T=i["L0_ffn_expert_w1"].transpose(0, 2, 1),
        w2_T=i["L0_ffn_expert_w2"].transpose(0, 2, 1),
        maa_r=i["L1_attn_time_maa_r"], maa_k=i["L1_attn_time_maa_k"],
        maa_v=i["L1_attn_time_maa_v"], maa_g=i["L1_attn_time_maa_g"],
        decay=i["L1_attn_time_decay"], faaaa=i["L1_attn_time_faaaa"],
        WrT=i["L1_attn_Wr"].T, WkT=i["L1_attn_Wk"].T, WvT=i["L1_attn_Wv"].T, WgT=i["L1_attn_Wg"].T,
        WoT=i["L1_attn_Wo"].T, ln_w=i["L1_attn_ln_w"], ln_b=i["L1_attn_ln_b"],
        gate_w=i["L1_ffn_gate_w"], gate_b=i["L1_ffn_gate_b"],
        expert_w=i["L1_ffn_expert_w"], expert_b=i["L1_ffn_expert_b"],
        ident=np.eye(P, dtype=np.float32),
        before=np.triu(np.ones((P, P), np.float32), 1),
        diag=np.eye(P, S, dtype=np.float32), masks=window_masks(),
    )
    nc = _bacc.Bacc("TRN2", target_bir_lowering=False, num_devices=1)
    arrays, args = {}, {}
    for name, value in layout.items():
        value = np.ascontiguousarray(value)
        arrays[f"in_{name}"] = value
        args[name] = nc.dram_tensor(f"in_{name}", value.shape, mybir.dt.from_np(value.dtype),
                                    kind="ExternalInput").ap()
    args["out"] = nc.dram_tensor("out", (T, D), F32, kind="ExternalOutput").ap()
    bass_decoder_layers(nc, args)
    r = _run(nc, [arrays], core_ids=[0])
    return r.results[0]["out"].reshape(B, S, D)
```
